# Optimizing a Trainium2 kernel written in Bass

```python
import numpy as np
import jax
import jax.numpy as jnp

def _softmax(x, axis=-1):
    return jax.nn.softmax(x, axis=axis)

def _gelu(x):
    return jax.nn.gelu(x, approximate=True)

def _silu(x):
    return jax.nn.silu(x)

def _sigmoid(x):
    return jax.nn.sigmoid(x)

def _layernorm(x, axis=-1, eps=1e-05):
    m = jnp.mean(x, axis=axis, keepdims=True)
    v = jnp.var(x, axis=axis, keepdims=True)
    return (x - m) / jnp.sqrt(v + eps)

def _scatter_add(tgt, idx, src, axis=0):
    return tgt.at[idx].add(src)

def _segment_sum(src, seg, n):
    return jax.ops.segment_sum(src, seg, n)
kernel_name = 'mk_flamingo_gated_d4_seqx_r8_16d327'

def setup_inputs(seed: int=0):
    np.random.seed(seed)
    _w = jnp.asarray

    def _rec_inputs():
        import jax
        import jax.numpy as jnp
        _rk = jax.random.key(seed)
        x = -0.0002928 + 1 * jax.random.normal(jax.random.fold_in(_rk, 1), (4, 512, 128), jnp.float32)
        _lenS = 512 - jax.random.randint(jax.random.fold_in(_rk, 7), (4,), 0, max(1, 512 // 4) + 1, jnp.int32)
        _lenS2 = 77 - jax.random.randint(jax.random.fold_in(_rk, 8), (4,), 0, max(1, 77 // 4) + 1, jnp.int32)
        _ctx_1024P = jax.random.normal(jax.random.fold_in(_rk, 11), (4, 16, 128), jnp.float32)
        _ctx_1024c = jax.random.dirichlet(jax.random.fold_in(_rk, 511), 0.3 * jnp.ones((16,), jnp.float32), (4, 77))
        _ctx_1024t = jnp.einsum('bsk,bkd->bsd', _ctx_1024c, _ctx_1024P)
        _ctx_1024t = _ctx_1024t * jax.lax.rsqrt(jnp.mean(jnp.square(_ctx_1024t)) + 1e-12) * 0.953939
        ctx_1024 = -1.39393e-06 + 0.999914 * (_ctx_1024t + 0.3 * jax.random.normal(jax.random.fold_in(_rk, 611), (4, 77, 128), jnp.float32))
        _validS = jnp.arange(512)[None, :] < _lenS[:, None]
        _validS2 = jnp.arange(77)[None, :] < _lenS2[:, None]
        _causal = jnp.tril(jnp.ones((512, 512), dtype=bool))
        mask_SxS2_bk0 = jnp.logical_not(jnp.broadcast_to(_validS2[0:1, :], (512, 77)))
        mask_BxS2_ik0 = jnp.where(jnp.broadcast_to(_validS2[:, :], (4, 77)), 0, 1).astype(jnp.int32)
        mask_BxS2_if1 = jnp.where(jnp.ones((4, 77), dtype=bool), 1, 0).astype(jnp.int32)
        _g = jax.random.normal(jax.random.fold_in(_rk, 9001), (2, 4), jnp.float32)
        _g = jnp.sign(_g) * jnp.maximum(jnp.abs(_g), 1.0) + (_g == 0) * 1.0
        g_xattn = _g[0]
        g_ffn = _g[1]
        return (x, ctx_1024, mask_SxS2_bk0, mask_BxS2_ik0, mask_BxS2_if1, g_xattn, g_ffn)
    x, ctx_1024, mask_SxS2_bk0, mask_BxS2_ik0, mask_BxS2_if1, g_xattn, g_ffn = _rec_inputs()

    def _L0_xattn_setup():
        import jax, jax.numpy as jnp
        import numpy as np
        D_MODEL = 128
        N_HEADS = 16
        HEAD_DIM = D_MODEL // N_HEADS
        B, SQ, SK = (2, 256, 256)

        def _split_heads(x):
            b, s, _ = x.shape
            return x.reshape(b, s, N_HEADS, HEAD_DIM).transpose(0, 2, 1, 3)
        key = jax.random.key(seed)
        ks = jax.random.split(key, 12)
        init = 0.02
        inp = {'queries': jax.random.normal(ks[0], (B, SQ, D_MODEL), jnp.float32), 'keys': jax.random.normal(ks[1], (B, SK, D_MODEL), jnp.float32), 'values': jax.random.normal(ks[2], (B, SK, D_MODEL), jnp.float32), 'Wq': jax.random.normal(ks[3], (D_MODEL, D_MODEL), jnp.float32) * init, 'bq': jnp.zeros((D_MODEL,), jnp.float32), 'Wk': jax.random.normal(ks[4], (D_MODEL, D_MODEL), jnp.float32) * init, 'bk': jnp.zeros((D_MODEL,), jnp.float32), 'Wv': jax.random.normal(ks[5], (D_MODEL, D_MODEL), jnp.float32) * init, 'bv': jnp.zeros((D_MODEL,), jnp.float32), 'Wo': jax.random.normal(ks[6], (D_MODEL, D_MODEL), jnp.float32) * init, 'bo': jnp.zeros((D_MODEL,), jnp.float32), 'mask': jnp.tril(jnp.ones((SQ, SK), dtype=bool))}
        return inp
    _L0_xattn_all = _L0_xattn_setup()
    _L0_xattn_in = {k: v for k, v in _L0_xattn_all.items() if k in ('Wq', 'bq', 'Wk', 'bk', 'Wv', 'bv', 'Wo', 'bo')}
    del _L0_xattn_all

    def _L0_ffn_setup():
        import jax, jax.numpy as jnp
        import numpy as np
        D_MODEL = 128
        M = 64
        INNER = 16
        key = jax.random.key(seed)
        ks = jax.random.split(key, 9)

        def init(k, shape, fan_in):
            bound = 1.0 / np.sqrt(fan_in)
            return jax.random.uniform(k, shape, jnp.float32, -bound, bound)
        x = jax.random.normal(ks[0], (16, 512, D_MODEL), dtype=jnp.float32)
        Win = init(ks[1], (D_MODEL, M), D_MODEL)
        bin_ = init(ks[2], (M,), D_MODEL)
        W1 = init(ks[3], (M, INNER), 1)
        b1 = init(ks[4], (M, INNER), 1)
        W2 = init(ks[5], (M, INNER), INNER)
        b2 = init(ks[6], (M,), INNER)
        Wout = init(ks[7], (M, D_MODEL), M)
        bout = init(ks[8], (D_MODEL,), M)
        return {'x': x, 'Win': Win, 'bin_': bin_, 'W1': W1, 'b1': b1, 'W2': W2, 'b2': b2, 'Wout': Wout, 'bout': bout}
    _L0_ffn_all = _L0_ffn_setup()
    _L0_ffn_in = {k: v for k, v in _L0_ffn_all.items() if k in ('Win', 'bin_', 'W1', 'b1', 'W2', 'b2', 'Wout', 'bout')}
    del _L0_ffn_all

    def _L1_xattn_setup():
        import jax, jax.numpy as jnp
        import numpy as np
        import math
        B, S, D, H = (1, 256, 128, 16)
        DK = D // H
        DH = 64
        LOG_T_MIN = math.log(0.1)
        LOG_T_MAX = math.log(10.0)

        def _linear(x, W, b):
            return x @ W.T + b
        key = jax.random.key(seed)
        ks = jax.random.split(key, 20)
        p = 0.02
        return {'query': jax.random.normal(ks[0], (B, S, D), jnp.float32), 'key': jax.random.normal(ks[1], (B, S, D), jnp.float32), 'value': jax.random.normal(ks[2], (B, S, D), jnp.float32), 'Wq': jax.random.normal(ks[3], (D, D), jnp.float32) * p, 'bq': jax.random.normal(ks[4], (D,), jnp.float32) * p, 'Wk': jax.random.normal(ks[5], (D, D), jnp.float32) * p, 'bk': jax.random.normal(ks[6], (D,), jnp.float32) * p, 'Wv': jax.random.normal(ks[7], (D, D), jnp.float32) * p, 'bv': jax.random.normal(ks[8], (D,), jnp.float32) * p, 'Wo': jax.random.normal(ks[9], (D, D), jnp.float32) * p, 'bo': jax.random.normal(ks[10], (D,), jnp.float32) * p, 'w1': jax.random.normal(ks[11], (DH, 3), jnp.float32) * 0.3, 'b1': jax.random.normal(ks[12], (DH,), jnp.float32) * 0.1, 'w2': jax.random.normal(ks[13], (DH, DH), jnp.float32) * 0.1, 'b2': jax.random.normal(ks[14], (DH,), jnp.float32) * 0.1, 'w3': jax.random.normal(ks[15], (1, DH), jnp.float32) * 0.1, 'b3': jnp.full((1,), (LOG_T_MIN + LOG_T_MAX) / 2, jnp.float32)}
    _L1_xattn_all = _L1_xattn_setup()
    _L1_xattn_in = {k: v for k, v in _L1_xattn_all.items() if k in ('Wq', 'bq', 'Wk', 'bk', 'Wv', 'bv', 'Wo', 'bo', 'w1', 'b1', 'w2', 'b2', 'w3', 'b3')}
    del _L1_xattn_all

    def _L1_ffn_setup():
        import jax, jax.numpy as jnp
        import numpy as np
        B, S, D, F, E, K = (4, 256, 128, 512, 4, 2)
        key = jax.random.key(seed)
        k = jax.random.split(key, 6)
        x = jax.random.normal(k[0], (B, S, D), jnp.float32)
        router_w = jax.random.normal(k[1], (D, E), jnp.float32) * D ** (-0.5)
        router_b = jnp.zeros((E,), jnp.float32)
        w1 = jax.random.normal(k[2], (E, D, F), jnp.float32) * 0.02
        w3 = jax.random.normal(k[3], (E, D, F), jnp.float32) * 0.02
        w2 = jax.random.normal(k[4], (E, F, D), jnp.float32) * 0.02
        return {'x': x, 'router_w': router_w, 'router_b': router_b, 'w1': w1, 'w3': w3, 'w2': w2}
    _L1_ffn_all = _L1_ffn_setup()
    _L1_ffn_in = {k: v for k, v in _L1_ffn_all.items() if k in ('router_w', 'router_b', 'w1', 'w3', 'w2')}
    del _L1_ffn_all

    def _L2_xattn_setup():
        import jax, jax.numpy as jnp
        import numpy as np
        H = 128
        NH = 16
        HD = H // NH
        key = jax.random.key(seed)
        ks = jax.random.split(key, 12)
        inp = {'query': jax.random.normal(ks[0], (4, 128, H), dtype=jnp.float32), 'key': jax.random.normal(ks[1], (4, 256, H), dtype=jnp.float32), 'value': jax.random.normal(ks[2], (4, 256, H), dtype=jnp.float32), 'key_padding_mask': jax.random.randint(ks[3], (4, 256), 0, 2, dtype=jnp.int32), 'Wq': jax.random.normal(ks[4], (H, H), dtype=jnp.float32) * (1.0 / np.sqrt(H)), 'bq': jnp.zeros((H,), dtype=jnp.float32), 'Wk': jax.random.normal(ks[5], (H, H), dtype=jnp.float32) * (1.0 / np.sqrt(H)), 'bk': jnp.zeros((H,), dtype=jnp.float32), 'Wv': jax.random.normal(ks[6], (H, H), dtype=jnp.float32) * (1.0 / np.sqrt(H)), 'bv': jnp.zeros((H,), dtype=jnp.float32), 'Wo': jax.random.normal(ks[7], (H, H), dtype=jnp.float32) * (1.0 / np.sqrt(H)), 'bo': jnp.zeros((H,), dtype=jnp.float32)}
        return inp
    _L2_xattn_all = _L2_xattn_setup()
    _L2_xattn_in = {k: v for k, v in _L2_xattn_all.items() if k in ('Wq', 'bq', 'Wk', 'bk', 'Wv', 'bv', 'Wo', 'bo')}
    del _L2_xattn_all

    def _L2_ffn_setup():
        import jax, jax.numpy as jnp
        import numpy as np
        E, K = (8, 2)
        DM, DE = (128, 352)
        B, S = (1, 256)
        EPS = 1e-06

        def _rmsnorm(x, w):
            var = jnp.mean(jnp.square(x), axis=-1, keepdims=True)
            return x * jax.lax.rsqrt(var + EPS) * w
        key = jax.random.key(seed)
        kx, kg, k1, k2, k3 = jax.random.split(key, 5)

        def kaiming_uniform(k, shape, fan_in):
            bound = 1.0 / np.sqrt(fan_in)
            return jax.random.uniform(k, shape, jnp.float32, -bound, bound)
        return {'x': jax.random.normal(kx, (B, S, DM), jnp.float32), 'gate_w': kaiming_uniform(kg, (E, DM), DM), 'rms_w': jnp.ones((DM,), jnp.float32), 'W1': kaiming_uniform(k1, (E, DE, DM), DE * DM), 'W2': kaiming_uniform(k2, (E, DE, DM), DE * DM), 'W3': kaiming_uniform(k3, (E, DM, DE), DM * DE)}
    _L2_ffn_all = _L2_ffn_setup()
    _L2_ffn_in = {k: v for k, v in _L2_ffn_all.items() if k in ('gate_w', 'rms_w', 'W1', 'W2', 'W3')}
    del _L2_ffn_all

    def _L3_xattn_setup():
        import jax, jax.numpy as jnp
        import numpy as np
        NEG = -10000.0
        key = jax.random.key(seed)
        k1, k2, k3 = jax.random.split(key, 3)
        B, L, D, H = (16, 256, 128, 128)
        x1 = jax.random.normal(k1, (B, L, D), dtype=jnp.float32)
        x2 = jax.random.normal(k2, (B, L, D), dtype=jnp.float32)
        x2_mask = jnp.ones((B, L), dtype=jnp.int64)
        W = jax.random.normal(k3, (H, D), dtype=jnp.float32) * (1.0 / np.sqrt(D))
        diagonal = jnp.ones((H,), dtype=jnp.float32)
        return {'x1': x1, 'x2': x2, 'x2_mask': x2_mask, 'W': W, 'diagonal': diagonal}
    _L3_xattn_all = _L3_xattn_setup()
    _L3_xattn_in = {k: v for k, v in _L3_xattn_all.items() if k in ('W', 'diagonal')}
    del _L3_xattn_all

    def _L3_ffn_setup():
        import jax, jax.numpy as jnp
        import numpy as np
        IN_F = 128
        OUT_F = 128
        N_EXPERTS = 8
        TOP_K = 2
        key = jax.random.key(seed)
        ks = jax.random.split(key, 5)
        scale_in = 1.0 / np.sqrt(IN_F)
        x = jax.random.normal(ks[0], (4, 256, IN_F), dtype=jnp.float32)
        W_experts = jax.random.uniform(ks[1], (N_EXPERTS, OUT_F, IN_F), jnp.float32, -scale_in, scale_in)
        b_experts = jax.random.uniform(ks[2], (N_EXPERTS, OUT_F), jnp.float32, -scale_in, scale_in)
        W_router = jax.random.uniform(ks[3], (N_EXPERTS, IN_F), jnp.float32, -scale_in, scale_in)
        b_router = jax.random.uniform(ks[4], (N_EXPERTS,), jnp.float32, -scale_in, scale_in)
        return {'x': x, 'W_experts': W_experts, 'b_experts': b_experts, 'W_router': W_router, 'b_router': b_router}
    _L3_ffn_all = _L3_ffn_setup()
    _L3_ffn_in = {k: v for k, v in _L3_ffn_all.items() if k in ('W_experts', 'b_experts', 'W_router', 'b_router')}
    del _L3_ffn_all
    return {'x': x, 'ctx_1024': ctx_1024, 'mask_SxS2_bk0': mask_SxS2_bk0, 'mask_BxS2_ik0': mask_BxS2_ik0, 'mask_BxS2_if1': mask_BxS2_if1, 'g_xattn': g_xattn, 'g_ffn': g_ffn, 'L0_xattn_Wq': _L0_xattn_in['Wq'], 'L0_xattn_bq': _L0_xattn_in['bq'], 'L0_xattn_Wk': _L0_xattn_in['Wk'], 'L0_xattn_bk': _L0_xattn_in['bk'], 'L0_xattn_Wv': _L0_xattn_in['Wv'], 'L0_xattn_bv': _L0_xattn_in['bv'], 'L0_xattn_Wo': _L0_xattn_in['Wo'], 'L0_xattn_bo': _L0_xattn_in['bo'], 'L0_ffn_Win': _L0_ffn_in['Win'], 'L0_ffn_bin_': _L0_ffn_in['bin_'], 'L0_ffn_W1': _L0_ffn_in['W1'], 'L0_ffn_b1': _L0_ffn_in['b1'], 'L0_ffn_W2': _L0_ffn_in['W2'], 'L0_ffn_b2': _L0_ffn_in['b2'], 'L0_ffn_Wout': _L0_ffn_in['Wout'], 'L0_ffn_bout': _L0_ffn_in['bout'], 'L1_xattn_Wq': _L1_xattn_in['Wq'], 'L1_xattn_bq': _L1_xattn_in['bq'], 'L1_xattn_Wk': _L1_xattn_in['Wk'], 'L1_xattn_bk': _L1_xattn_in['bk'], 'L1_xattn_Wv': _L1_xattn_in['Wv'], 'L1_xattn_bv': _L1_xattn_in['bv'], 'L1_xattn_Wo': _L1_xattn_in['Wo'], 'L1_xattn_bo': _L1_xattn_in['bo'], 'L1_xattn_w1': _L1_xattn_in['w1'], 'L1_xattn_b1': _L1_xattn_in['b1'], 'L1_xattn_w2': _L1_xattn_in['w2'], 'L1_xattn_b2': _L1_xattn_in['b2'], 'L1_xattn_w3': _L1_xattn_in['w3'], 'L1_xattn_b3': _L1_xattn_in['b3'], 'L1_ffn_router_w': _L1_ffn_in['router_w'], 'L1_ffn_router_b': _L1_ffn_in['router_b'], 'L1_ffn_w1': _L1_ffn_in['w1'], 'L1_ffn_w3': _L1_ffn_in['w3'], 'L1_ffn_w2': _L1_ffn_in['w2'], 'L2_xattn_Wq': _L2_xattn_in['Wq'], 'L2_xattn_bq': _L2_xattn_in['bq'], 'L2_xattn_Wk': _L2_xattn_in['Wk'], 'L2_xattn_bk': _L2_xattn_in['bk'], 'L2_xattn_Wv': _L2_xattn_in['Wv'], 'L2_xattn_bv': _L2_xattn_in['bv'], 'L2_xattn_Wo': _L2_xattn_in['Wo'], 'L2_xattn_bo': _L2_xattn_in['bo'], 'L2_ffn_gate_w': _L2_ffn_in['gate_w'], 'L2_ffn_rms_w': _L2_ffn_in['rms_w'], 'L2_ffn_W1': _L2_ffn_in['W1'], 'L2_ffn_W2': _L2_ffn_in['W2'], 'L2_ffn_W3': _L2_ffn_in['W3'], 'L3_xattn_W': _L3_xattn_in['W'], 'L3_xattn_diagonal': _L3_xattn_in['diagonal'], 'L3_ffn_W_experts': _L3_ffn_in['W_experts'], 'L3_ffn_b_experts': _L3_ffn_in['b_experts'], 'L3_ffn_W_router': _L3_ffn_in['W_router'], 'L3_ffn_b_router': _L3_ffn_in['b_router']}

def reference(x, ctx_1024, mask_SxS2_bk0, mask_BxS2_ik0, mask_BxS2_if1, g_xattn, g_ffn, L0_xattn_Wq, L0_xattn_bq, L0_xattn_Wk, L0_xattn_bk, L0_xattn_Wv, L0_xattn_bv, L0_xattn_Wo, L0_xattn_bo, L0_ffn_Win, L0_ffn_bin_, L0_ffn_W1, L0_ffn_b1, L0_ffn_W2, L0_ffn_b2, L0_ffn_Wout, L0_ffn_bout, L1_xattn_Wq, L1_xattn_bq, L1_xattn_Wk, L1_xattn_bk, L1_xattn_Wv, L1_xattn_bv, L1_xattn_Wo, L1_xattn_bo, L1_xattn_w1, L1_xattn_b1, L1_xattn_w2, L1_xattn_b2, L1_xattn_w3, L1_xattn_b3, L1_ffn_router_w, L1_ffn_router_b, L1_ffn_w1, L1_ffn_w3, L1_ffn_w2, L2_xattn_Wq, L2_xattn_bq, L2_xattn_Wk, L2_xattn_bk, L2_xattn_Wv, L2_xattn_bv, L2_xattn_Wo, L2_xattn_bo, L2_ffn_gate_w, L2_ffn_rms_w, L2_ffn_W1, L2_ffn_W2, L2_ffn_W3, L3_xattn_W, L3_xattn_diagonal, L3_ffn_W_experts, L3_ffn_b_experts, L3_ffn_W_router, L3_ffn_b_router):
    import jax
    import jax.numpy as jnp

    def _L0_xattn_ref(queries, keys, values, Wq, bq, Wk, bk, Wv, bv, Wo, bo, mask):
        import jax, jax.numpy as jnp
        import numpy as np
        D_MODEL = 128
        N_HEADS = 16
        HEAD_DIM = D_MODEL // N_HEADS
        B, SQ, SK = (2, 256, 256)

        def _split_heads(x):
            b, s, _ = x.shape
            return x.reshape(b, s, N_HEADS, HEAD_DIM).transpose(0, 2, 1, 3)
        q = _split_heads(queries @ Wq + bq)
        k = _split_heads(keys @ Wk + bk)
        v = _split_heads(values @ Wv + bv)
        scale = 1.0 / np.sqrt(HEAD_DIM).astype(np.float32)
        scores = jnp.einsum('bhqd,bhkd->bhqk', q, k) * scale
        neg = jnp.finfo(scores.dtype).min
        scores = jnp.where(mask[None, None, :, :], scores, neg)
        probs = jax.nn.softmax(scores, axis=-1)
        out = jnp.einsum('bhqk,bhkd->bhqd', probs, v)
        b, h, sq, hd = out.shape
        out = out.transpose(0, 2, 1, 3).reshape(b, sq, h * hd)
        return out @ Wo + bo

    def _L0_ffn_ref(x, Win, bin_, W1, b1, W2, b2, Wout, bout):
        import jax, jax.numpy as jnp
        import numpy as np
        D_MODEL = 128
        M = 64
        INNER = 16
        s = jnp.einsum('btd,dm->btm', x, Win) + bin_
        h = jax.nn.relu(s[..., None] * W1 + b1)
        g = jnp.einsum('btmh,mh->btm', h, W2) + b2
        out = jnp.einsum('btm,md->btd', g, Wout) + bout
        return out

    def _L1_xattn_ref(query, key, value, Wq, bq, Wk, bk, Wv, bv, Wo, bo, w1, b1, w2, b2, w3, b3):
        import jax, jax.numpy as jnp
        import numpy as np
        import math
        B, S, D, H = (1, 256, 128, 16)
        DK = D // H
        DH = 64
        LOG_T_MIN = math.log(0.1)
        LOG_T_MAX = math.log(10.0)

        def _linear(x, W, b):
            return x @ W.T + b
        b, sq, d = query.shape
        sk = key.shape[1]
        h, dk = (H, DK)
        Q = _linear(query, Wq, bq).reshape(b, sq, h, dk).transpose(0, 2, 1, 3)
        K = _linear(key, Wk, bk).reshape(b, sk, h, dk).transpose(0, 2, 1, 3)
        V = _linear(value, Wv, bv).reshape(b, sk, h, dk).transpose(0, 2, 1, 3)
        qk = jnp.einsum('bhqd,bhkd->bhqk', Q, K)
        scores = qk / math.sqrt(dk)
        mean_sim = scores.mean(axis=(-2, -1))
        max_sim = scores.max(axis=-1).mean(axis=-1)
        probs = jax.nn.softmax(scores, axis=-1)
        entropy_proxy = jnp.var(probs, axis=-1, ddof=1).mean(axis=-1)
        feats = jnp.stack([mean_sim, max_sim, entropy_proxy], axis=-1)
        hidden = jax.nn.gelu(_linear(feats, w1, b1), approximate=False)
        hidden = jax.nn.gelu(_linear(hidden, w2, b2), approximate=False)
        log_t = jnp.clip(_linear(hidden, w3, b3), LOG_T_MIN, LOG_T_MAX)
        t = jnp.exp(log_t)[..., None]
        attn_scores = qk / (2.0 * t)
        attn = jax.nn.softmax(attn_scores, axis=-1)
        attn = jnp.nan_to_num(attn, nan=0.0)
        out = jnp.einsum('bhqk,bhkd->bhqd', attn, V)
        out = out.transpose(0, 2, 1, 3).reshape(b, sq, d)
        return _linear(out, Wo, bo)

    def _L1_ffn_ref(x, router_w, router_b, w1, w3, w2):
        import jax, jax.numpy as jnp
        import numpy as np
        B, S, D, F, E, K = (4, 256, 128, 512, 4, 2)
        b, s, d = x.shape
        T = b * s
        e = router_w.shape[1]
        xf = x.reshape(T, d)
        logits = xf @ router_w + router_b
        probs = jax.nn.softmax(logits, axis=-1)
        top_p, top_i = jax.lax.top_k(probs, K)
        top_p = top_p / jnp.sum(top_p, axis=-1, keepdims=True)
        gates = jnp.zeros((T, e), xf.dtype).at[jnp.arange(T)[:, None], top_i].add(top_p)
        h = jax.nn.silu(jnp.einsum('td,edf->etf', xf, w1)) * jnp.einsum('td,edf->etf', xf, w3)
        expert_out = jnp.einsum('etf,efd->etd', h, w2)
        out = jnp.einsum('te,etd->td', gates, expert_out)
        return out.reshape(b, s, d)

    def _L2_xattn_ref(query, key, value, key_padding_mask, Wq, bq, Wk, bk, Wv, bv, Wo, bo):
        import jax, jax.numpy as jnp
        import numpy as np
        H = 128
        NH = 16
        HD = H // NH
        B, Sq, _ = query.shape
        Sk = key.shape[1]
        scaling = HD ** (-0.5)
        q = (query @ Wq + bq).reshape(B, Sq, NH, HD).transpose(0, 2, 1, 3)
        k = (key @ Wk + bk).reshape(B, Sk, NH, HD).transpose(0, 2, 1, 3)
        v = (value @ Wv + bv).reshape(B, Sk, NH, HD).transpose(0, 2, 1, 3)
        scores = jnp.einsum('bhqd,bhkd->bhqk', q, k) * scaling
        scores = jnp.where((key_padding_mask == 0)[:, None, None, :], -jnp.inf, scores)
        attn = jax.nn.softmax(scores, axis=-1)
        out = jnp.einsum('bhqk,bhkd->bhqd', attn, v)
        out = out.transpose(0, 2, 1, 3).reshape(B, Sq, H)
        return out @ Wo + bo

    def _L2_ffn_ref(x, gate_w, rms_w, W1, W2, W3):
        import jax, jax.numpy as jnp
        import numpy as np
        E, K = (8, 2)
        DM, DE = (128, 352)
        B, S = (1, 256)
        EPS = 1e-06

        def _rmsnorm(x, w):
            var = jnp.mean(jnp.square(x), axis=-1, keepdims=True)
            return x * jax.lax.rsqrt(var + EPS) * w
        y = _rmsnorm(x, rms_w)
        logits = jnp.einsum('bsd,ed->bse', y, gate_w)
        vals, idx = jax.lax.top_k(logits, K)
        w = jax.nn.softmax(vals, axis=-1)
        w_full = jnp.einsum('bsk,bske->bse', w, jax.nn.one_hot(idx, E, dtype=x.dtype))
        up = jnp.einsum('bsd,end->bsen', y, W1)
        gate = jnp.einsum('bsd,end->bsen', y, W2)
        h = jax.nn.silu(up) * gate
        out = jnp.einsum('bsen,emn->bsem', h, W3)
        comb = jnp.einsum('bsem,bse->bsm', out, w_full)
        return x + comb

    def _L3_xattn_ref(x1, x2, x2_mask, W, diagonal):
        import jax, jax.numpy as jnp
        import numpy as np
        NEG = -10000.0
        x1_rep = jax.nn.relu(jnp.einsum('bld,hd->blh', x1, W))
        x2_rep = jax.nn.relu(jnp.einsum('bld,hd->blh', x2, W))
        scores = jnp.einsum('bih,bjh->bij', x1_rep * diagonal, x2_rep)
        m = (1.0 - x2_mask.astype(scores.dtype)) * NEG
        alpha = jax.nn.softmax(scores + m[:, None, :], axis=-1)
        return jnp.einsum('bij,bjd->bid', alpha, x2)

    def _L3_ffn_ref(x, W_experts, b_experts, W_router, b_router):
        import jax, jax.numpy as jnp
        import numpy as np
        IN_F = 128
        OUT_F = 128
        N_EXPERTS = 8
        TOP_K = 2
        router_logits = jnp.einsum('bsd,ed->bse', x, W_router) + b_router
        router_weights = jax.nn.softmax(router_logits, axis=-1)
        if TOP_K < N_EXPERTS:
            topk_w, topk_idx = jax.lax.top_k(router_weights, TOP_K)
            sparse = jnp.zeros_like(router_weights)
            router_weights = jnp.take_along_axis(sparse, topk_idx, axis=-1)
            router_weights = sparse.at[..., :].set(0.0)
            b_idx = jnp.arange(sparse.shape[0])[:, None, None]
            s_idx = jnp.arange(sparse.shape[1])[None, :, None]
            router_weights = sparse.at[b_idx, s_idx, topk_idx].set(topk_w)
        expert_out = jnp.einsum('bsd,eod->bseo', x, W_experts) + b_experts
        return jnp.einsum('bseo,bse->bso', expert_out, router_weights)
    x = x + jnp.tanh(g_xattn[0]) * _L0_xattn_ref(_layernorm(x, axis=-1), ctx_1024, ctx_1024, L0_xattn_Wq, L0_xattn_bq, L0_xattn_Wk, L0_xattn_bk, L0_xattn_Wv, L0_xattn_bv, L0_xattn_Wo, L0_xattn_bo, mask_SxS2_bk0)
    x = x + jnp.tanh(g_ffn[0]) * _L0_ffn_ref(_layernorm(x, axis=-1), L0_ffn_Win, L0_ffn_bin_, L0_ffn_W1, L0_ffn_b1, L0_ffn_W2, L0_ffn_b2, L0_ffn_Wout, L0_ffn_bout)
    x = x + jnp.tanh(g_xattn[1]) * _L1_xattn_ref(_layernorm(x, axis=-1), ctx_1024, ctx_1024, L1_xattn_Wq, L1_xattn_bq, L1_xattn_Wk, L1_xattn_bk, L1_xattn_Wv, L1_xattn_bv, L1_xattn_Wo, L1_xattn_bo, L1_xattn_w1, L1_xattn_b1, L1_xattn_w2, L1_xattn_b2, L1_xattn_w3, L1_xattn_b3)
    x = x + jnp.tanh(g_ffn[1]) * _L1_ffn_ref(_layernorm(x, axis=-1), L1_ffn_router_w, L1_ffn_router_b, L1_ffn_w1, L1_ffn_w3, L1_ffn_w2)
    x = x + jnp.tanh(g_xattn[2]) * _L2_xattn_ref(_layernorm(x, axis=-1), ctx_1024, ctx_1024, mask_BxS2_ik0, L2_xattn_Wq, L2_xattn_bq, L2_xattn_Wk, L2_xattn_bk, L2_xattn_Wv, L2_xattn_bv, L2_xattn_Wo, L2_xattn_bo)
    x = x + jnp.tanh(g_ffn[2]) * _L2_ffn_ref(_layernorm(x, axis=-1), L2_ffn_gate_w, L2_ffn_rms_w, L2_ffn_W1, L2_ffn_W2, L2_ffn_W3)
    x = x + jnp.tanh(g_xattn[3]) * _L3_xattn_ref(_layernorm(x, axis=-1), ctx_1024, mask_BxS2_if1, L3_xattn_W, L3_xattn_diagonal)
    x = x + jnp.tanh(g_ffn[3]) * _L3_ffn_ref(_layernorm(x, axis=-1), L3_ffn_W_experts, L3_ffn_b_experts, L3_ffn_W_router, L3_ffn_b_router)
    return x

_drawn_inputs = setup_inputs


def setup_inputs(seed=0):
    import zlib

    import numpy as np

    out = dict(_drawn_inputs(seed))
    spreads = {'L0_xattn_bq': (0.0, 0.8),
     'L0_xattn_bk': (0.0, 2.0),
     'L0_xattn_bv': (0.0, 0.331),
     'L0_xattn_bo': (0.0, 0.1),
     'L1_ffn_router_b': (0.0, 0.8),
     'L2_xattn_bq': (0.0, 0.1),
     'L2_xattn_bk': (0.0, 2.0),
     'L2_xattn_bv': (0.0, 0.1),
     'L2_xattn_bo': (0.0, 0.1),
     'L2_ffn_rms_w': (1.0, 0.6),
     'L3_xattn_diagonal': (1.0, 0.2)}
    factors = {'g_ffn': 8.0,
     'L0_xattn_Wq': 8.0,
     'L0_xattn_Wk': 8.0,
     'L0_ffn_bin_': 7.675,
     'L1_xattn_Wq': 8.0,
     'L1_xattn_bq': 8.0,
     'L1_xattn_Wk': 8.0,
     'L1_xattn_bk': 200.0,
     'L1_xattn_bv': 7.222,
     'L1_xattn_w1': 8.0,
     'L1_xattn_b1': 8.0,
     'L1_xattn_w2': 8.0,
     'L1_xattn_b2': 8.0,
     'L1_xattn_w3': 8.0,
     'L1_ffn_router_w': 5.193,
     'L1_ffn_w1': 4.026,
     'L1_ffn_w3': 3.794,
     'L1_ffn_w2': 3.942,
     'L2_ffn_gate_w': 8.0,
     'L2_ffn_W1': 8.0,
     'L2_ffn_W2': 8.0,
     'L2_ffn_W3': 8.0,
     'L3_ffn_b_experts': 4.259}
    for name, (base, spread) in spreads.items():
        noise = np.random.default_rng([zlib.crc32(name.encode()), seed]).standard_normal(out[name].shape)
        drawn = base * np.exp(spread * noise) if base else spread * noise
        out[name] = jnp.asarray(drawn.astype(out[name].dtype))
    for name, factor in factors.items():
        out[name] = (out[name] * factor).astype(out[name].dtype)
    return out
```

```python
import math
from contextlib import ExitStack

import concourse.bass as bass
from concourse import mybir

F32 = mybir.dt.float32
F32R = mybir.dt.float32r
BF16 = mybir.dt.bfloat16
ALU = mybir.AluOpType
ACT = mybir.ActivationFunctionType
AX = mybir.AxisListType

P = 128
T = 4
N = P * T
B = 4
STREAMS = 2
S2 = 77
H = 16
HD = 8
G = 4
J = H // G
ROOT = float(HD) ** -0.5
OFF = float(2.0 ** 100)
PAD = -3.0e38
LOG_T_MIN, LOG_T_MAX = math.log(0.1), math.log(10.0)
LN_EPS = 1e-5
RMS_EPS = 1e-6
LAYERS = 4
UNITS = 2 * LAYERS * STREAMS

MOE1 = 4
F1 = 512
MOE2 = 8
F2 = 352
MOE3 = 8
EMAX = 8
LG = 16
M0, I0 = 64, 16
C0 = M0 * I0 // P


def kind(u):
    return "AF"[(u // STREAMS) % 2] + str(u // STREAMS // 2)


def pieces(width):
    return [(o, min(P, width - o)) for o in range(0, width, P)]


class Signal:

    def __init__(self, sem, seen, counts, name):
        self.sem, self.counts = sem, counts.setdefault(name, {})
        self.seen, self.total = seen.get(name, {}), 0

    def up(self, *key, by=1):
        self.total += by
        self.counts[key] = self.total
        return (self.sem, by)

    def at(self, *key):
        return (self.sem, self.seen.get(key, 1))


def build(nc, a, out, seen, counts):
    with ExitStack() as ctx:
        sems = []

        def sb(name, shape, dt=F32):
            return ctx.enter_context(nc.sbuf_tensor(name, shape, dt))

        def sig(name):
            s = ctx.enter_context(nc.semaphore(name))
            sems.append(s)
            return Signal(s, seen, counts, name)

        bank = [ctx.enter_context(nc.psum_tensor(f"bank{i}", [P, 512], F32)) for i in range(8)]

        ident = sb("ident", [P, P])
        identb = sb("identb", [P, P], BF16)
        spread = sb("spread", [P, P])
        pick_r = sb("pick_r", [H, H, S2], F32R)
        pick8 = sb("pick8", [EMAX, EMAX, P])
        quad = sb("quad", [P, 4, J])
        hmask = sb("hmask", [P, J])
        ones = sb("ones", [P, N])
        onesb = sb("onesb", [1, P], BF16)
        minus_half = sb("minus_half", [P, T])
        gates_col = sb("gates_col", [P, 2, LAYERS])
        graw = sb("graw", [P, 2, LAYERS])

        WqR = [sb(f"WqR{l}", [P, G, 4 * 32]) for l in range(3)]
        WkR = [sb(f"WkR{l}", [P, G, 4 * 32]) for l in range(3)]
        Wv = [sb(f"Wv{l}", [P, P]) for l in range(3)]
        Wo = [sb(f"Wo{l}", [P, G, P]) for l in range(3)]
        brow = sb("brow", [1, 3, 3, P])
        bcol = sb("bcol", [P, 3, 2, G])
        W3x = sb("W3x", [P, P])
        diag = sb("diag", [P, 1])
        t_w1b = sb("t_w1b", [P, 3, 64])
        t_w1T = sb("t_w1T", [3, 64])
        t_b1 = sb("t_b1", [64, 1])
        t_b2 = sb("t_b2", [64, 1])
        t_w2T = sb("t_w2T", [64, 64])
        t_w3 = sb("t_w3", [64, 1])
        t_b3 = sb("t_b3", [S2, 1])
        f0_in = sb("f0_in", [P, M0 * I0])
        f0_out = sb("f0_out", [P, C0, P])
        f0_cols = sb("f0_cols", [P, 3, C0])
        f0_bias = sb("f0_bias", [P, 1])
        m1_router = sb("m1_router", [P, MOE1])
        m1_rb = sb("m1_rb", [1, MOE1])
        m1_w1 = sb("m1_w1", [P, MOE1, F1])
        m1_w3 = sb("m1_w3", [P, MOE1, F1])
        m1_w2 = sb("m1_w2", [P, MOE1, F1 // P, P])
        m2_router = sb("m2_router", [P, MOE2])
        m2_rms = sb("m2_rms", [P, 1])
        m2_w1 = sb("m2_w1", [P, MOE2 * F2])
        m2_w2 = sb("m2_w2", [P, MOE2 * F2])
        m2_w3 = sb("m2_w3", [P, MOE2, 3, P])
        m3_router = sb("m3_router", [P, MOE3])
        m3_rb = sb("m3_rb", [1, MOE3])
        m3_w = sb("m3_w", [P, MOE3, P])
        m3_b = sb("m3_b", [MOE3, P])
        mask_q = sb("mask_q", [P, T, S2], BF16)
        mask_k = sb("mask_k", [S2, N], BF16)

        with ExitStack() as pro:
            def tmp(name, shape, dt=F32):
                return pro.enter_context(nc.sbuf_tensor(name, shape, dt))

            nat1 = [tmp(f"nat1{i}", [P, P]) for i in range(3)]
            Wq = [tmp(f"Wq{l}", [P, P]) for l in range(3)]
            Wk = [tmp(f"Wk{l}", [P, P]) for l in range(3)]
            nat_in = tmp("nat_in", [P, M0])
            natwo = tmp("natwo", [P, P])
            natwo_g = tmp("natwo_g", [P, G, J, 32])
            nat3x = tmp("nat3x", [P, P])
            nat_t1 = tmp("nat_t1", [64, 3])
            nat_t2 = tmp("nat_t2", [64, 64])
            NCH = MOE2 * F2 // P
            nat_m1 = tmp("nat_m1", [P, NCH, P])
            nat_m2 = tmp("nat_m2", [P, NCH, P])
            nat_m3 = tmp("nat_m3", [P, MOE2, F2])
            nat_e = tmp("nat_e", [P, MOE3, P])
            nat_r = tmp("nat_r", [MOE2, 2, P])
            nat_f0 = tmp("nat_f0", [C0, 4, P])
            nat_bin = tmp("nat_bin", [C0, M0 // C0])
            f0_wout = tmp("f0_wout", [M0, P])
            f0_b2 = tmp("f0_b2", [M0, 1])
            f0_bout = tmp("f0_bout", [P, 1])
            m8 = tmp("m8", [P, T, S2], mybir.dt.uint8)
            mf = tmp("mf", [P, T, S2])
            pick_f = tmp("pick_f", [H, H, S2])
            quad_b = tmp("quad_b", [P, 4, J])

            landed = {n: sig("landed_" + n) for n in ("small", "gates", "wo", "turn", "m2", "rest", "mask")}
            zeroed = sig("zeroed")
            const = sig("const")
            turned = sig("turned")
            keptA, keptD = sig("kept_act"), sig("kept_dve")
            folded = sig("folded")

            groups = []

            def grouped(load, items):
                row, width = [], 0
                for src, dst in items:
                    k = src.shape[0]
                    if row and (width + k > 512):
                        groups.append((load, row))
                        row, width = [], 0
                    row.append((src, dst, width))
                    width += k
                groups.append((load, row))

            grouped("turn", [(nat1[0][:], Wq[1][:]), (nat1[1][:], Wk[1][:]), (nat1[2][:], Wv[1][:]), (nat3x[:], W3x[:])])
            grouped("turn", [(natwo_g[:, g, :, :].rearrange("p j c -> p (j c)"), Wo[1][:, g, :]) for g in range(G)])
            grouped("turn", [(nat_t1[:], t_w1T[:]), (nat_t2[:], t_w2T[:]), (nat_r[:, 0, :], m2_router[:]),
                             (nat_r[:, 1, :], m3_router[:]), (nat_f0[:, 0, :], f0_cols[:, 0, :]),
                             (nat_f0[:, 3, :], f0_cols[:, 1, :]), (nat_f0[:, 2, :], f0_cols[:, 2, :])])
            grouped("mask", [(mf[:, t, :], mask_k[:, t * P:(t + 1) * P]) for t in range(T)])
            grouped("m2", [(nat_e[:, e, :], m3_w[:, e, :]) for e in range(MOE3)])
            for nat, w in ((nat_m1, m2_w1), (nat_m2, m2_w2)):
                grouped("m2", [(nat[:, c, :], w[:, c * P:(c + 1) * P]) for c in range(NCH)])
            grouped("m2", [(nat_m3[:, e, o:o + w], m2_w3[0:w, e, i, :]) for e in range(MOE2)
                           for i, (o, w) in enumerate(pieces(F2))])

            block = pro.enter_context(nc.Block())

            @block.sync
            def _(sp):
                for l in (0, 2):
                    for n, w in (("Wq", Wq), ("Wk", Wk), ("Wv", Wv)):
                        sp.dma_start(w[l][:], a[f"L{l}_xattn_{n}"]).then_inc(*landed["small"].up(by=16))
                for l in range(3):
                    for i, n in enumerate(("bq", "bk", "bv")):
                        sp.dma_start(brow[0:1, l, i, :], a[f"L{l}_xattn_{n}"].rearrange("(o n) -> o n", o=1)) \
                            .then_inc(*landed["small"].up(by=16))
                for src, dst in ((a["L3_xattn_diagonal"], diag), (a["L1_xattn_b1"], t_b1), (a["L1_xattn_b2"], t_b2),
                                 (a["L0_ffn_b2"], f0_b2), (a["L0_ffn_bout"], f0_bout), (a["L2_ffn_rms_w"], m2_rms)):
                    sp.dma_start(dst[:], src.rearrange("(n o) -> n o", o=1)).then_inc(*landed["small"].up(by=16))
                sp.dma_start(t_w3[:], a["L1_xattn_w3"].rearrange("o n -> n o")).then_inc(*landed["small"].up(by=16))
                sp.dma_start(t_b3[:], a["L1_xattn_b3"].partition_broadcast(S2)).then_inc(*landed["small"].up(by=16))
                sp.dma_start(nat_in[:], a["L0_ffn_Win"]).then_inc(*landed["small"].up(by=16))
                sp.dma_start(f0_wout[:], a["L0_ffn_Wout"]).then_inc(*landed["small"].up(by=16))
                for c in range(C0):
                    sp.dma_start(f0_out[:, c, :],
                                 a["L0_ffn_Wout"][c * 8:c * 8 + 8, :].unsqueeze(1).to_broadcast([8, I0, P])) \
                        .then_inc(*landed["small"].up(by=16))
                sp.dma_start(m1_router[:], a["L1_ffn_router_w"]).then_inc(*landed["small"].up(by=16))
                sp.dma_start(m1_rb[:], a["L1_ffn_router_b"].rearrange("(o n) -> o n", o=1)).then_inc(*landed["small"].up(by=16))
                sp.dma_start(m3_rb[:], a["L3_ffn_b_router"].rearrange("(o n) -> o n", o=1)).then_inc(*landed["small"].up(by=16))
                sp.dma_start(m3_b[:], a["L3_ffn_b_experts"]).then_inc(*landed["small"].up("all", by=16))
                sp.dma_start(m1_w1[:], a["L1_ffn_w1"].rearrange("e d f -> d e f")).then_inc(*landed["rest"].up(by=16))
                sp.dma_start(m1_w3[:], a["L1_ffn_w3"].rearrange("e d f -> d e f")).then_inc(*landed["rest"].up(by=16))
                sp.dma_start(m1_w2[:], a["L1_ffn_w2"].rearrange("e (c p) d -> p e c d", p=P)) \
                    .then_inc(*landed["rest"].up("all", by=16))
                for name in ("small", "rest", "gates"):
                    sp.wait_ge(*landed[name].at("all"))

            @block.scalar
            def _(act):
                act.dma_start(graw[:, 0, :], a["g_xattn"].partition_broadcast(P)).then_inc(*landed["gates"].up(by=16))
                act.dma_start(graw[:, 1, :], a["g_ffn"].partition_broadcast(P)).then_inc(*landed["gates"].up("all", by=16))
                act.dma_start(m8[:], a["mask_SxS2_bk0"].rearrange("(p t) k -> p t k", t=T)) \
                    .then_inc(*landed["mask"].up("all", by=16))
                for i, n in enumerate(("Wq", "Wk", "Wv")):
                    act.dma_start(nat1[i][:], a[f"L1_xattn_{n}"]).then_inc(*landed["turn"].up(by=16))
                act.dma_start(nat3x[:], a["L3_xattn_W"]).then_inc(*landed["turn"].up(by=16))
                act.dma_start(natwo[:], a["L1_xattn_Wo"]).then_inc(*landed["turn"].up(by=16))
                act.dma_start(nat_t1[:], a["L1_xattn_w1"]).then_inc(*landed["turn"].up(by=16))
                act.dma_start(nat_t2[:], a["L1_xattn_w2"]).then_inc(*landed["turn"].up(by=16))
                act.dma_start(nat_r[:, 0, :], a["L2_ffn_gate_w"]).then_inc(*landed["turn"].up(by=16))
                act.dma_start(nat_r[:, 1, :], a["L3_ffn_W_router"]).then_inc(*landed["turn"].up(by=16))
                for i, n in enumerate(("W1", "b1", "W2")):
                    act.dma_start(nat_f0[:, i, :], a[f"L0_ffn_{n}"].rearrange("(c m) i -> c (m i)", c=C0)) \
                        .then_inc(*landed["turn"].up(by=16))
                act.dma_start(nat_bin[:], a["L0_ffn_bin_"].rearrange("(c m) -> c m", c=C0)) \
                    .then_inc(*landed["turn"].up("all", by=16))
                act.dma_start(nat_e[:], a["L3_ffn_W_experts"].rearrange("e o i -> o e i")).then_inc(*landed["m2"].up(by=16))
                act.dma_start(nat_m1[:], a["L2_ffn_W1"].rearrange("e n d -> (e n) d").rearrange("(c p) d -> p c d", p=P)) \
                    .then_inc(*landed["m2"].up(by=16))
                act.dma_start(nat_m2[:], a["L2_ffn_W2"].rearrange("e n d -> (e n) d").rearrange("(c p) d -> p c d", p=P)) \
                    .then_inc(*landed["m2"].up(by=16))
                act.dma_start(nat_m3[:], a["L2_ffn_W3"].rearrange("e m n -> m e n")).then_inc(*landed["m2"].up("all", by=16))
                act.wait_ge(*landed["gates"].at("all"))
                act.activation(gates_col[:], graw[:], ACT.Tanh)
                for i, (_, row) in enumerate(groups):
                    if i % 2:
                        act.wait_ge(*turned.at(i))
                        for n, (src, dst, at) in enumerate(row):
                            k, m = src.shape
                            op = act.activation(dst, bank[i % 8][0:m, at:at + k], ACT.Copy)
                        op.then_inc(*keptA.up(i))

            @block.gpsimd
            def _(pool):
                pool.memset(ident[:], 0.0)
                pool.memset(ones[:], 1.0)
                pool.memset(quad[:], 1.0)
                pool.memset(pick_f[:], 1.0)
                pool.memset(pick8[:], 1.0)
                pool.memset(spread[:], 1.0)
                pool.memset(minus_half[:], -0.5)
                pool.memset(onesb[:], 1.0)
                pool.memset(natwo_g[:], 0.0)
                pool.memset(Wo[0][:], 0.0)
                pool.memset(Wo[2][:], 0.0).then_inc(*zeroed.up("all"))
                pool.wait_ge(*zeroed.at("all"))
                pool.affine_select(out=ident[:], in_=ident[:], compare_op=ALU.not_equal, fill=1.0, base=0,
                                   pattern=[[-1, P]], channel_multiplier=1).then_inc(*const.up("ident"))
                pool.affine_select(out=pick_f[:], in_=pick_f[:], compare_op=ALU.is_equal, fill=0.0, base=0,
                                   pattern=[[1, H], [0, S2]], channel_multiplier=-1).then_inc(*const.up("pick"))
                pool.affine_select(out=pick8[:], in_=pick8[:], compare_op=ALU.is_equal, fill=0.0, base=0,
                                   pattern=[[1, EMAX], [0, P]], channel_multiplier=-1).then_inc(*const.up("pick8"))
                pool.affine_select(out=spread[:], in_=spread[:], compare_op=ALU.is_equal, fill=0.0, base=HD,
                                   pattern=[[32, 4], [0, 32]], channel_multiplier=-1).then_inc(*const.up("spread"))
                pool.affine_select(out=quad_b[:], in_=quad[:], compare_op=ALU.is_ge, fill=0.0, base=0,
                                   pattern=[[-32, 4], [-HD, J]], channel_multiplier=1).then_inc(*const.up("quad_low"))
                pool.wait_ge(*const.at("quad_low"))
                pool.affine_select(out=quad[:], in_=quad_b[:], compare_op=ALU.is_ge, fill=0.0, base=HD - 1,
                                   pattern=[[32, 4], [HD, J]], channel_multiplier=-1).then_inc(*const.up("quad"))
                for l in (0, 2):
                    wo = a[f"L{l}_xattn_Wo"].rearrange("(g j d) n -> j d g n", g=G, j=J)
                    for j in range(J):
                        pool.dma_start(Wo[l][32 * j:32 * j + HD, :, :], wo[j]).then_inc(*landed["wo"].up(by=16))
                    pool.dma_start(Wo[l][HD:HD + 1, 0, :], a[f"L{l}_xattn_bo"].rearrange("(o n) -> o n", o=1)) \
                        .then_inc(*landed["wo"].up(by=16))
                pool.wait_ge(*keptA.at(1))
                pool.dma_start(Wo[1][HD:HD + 1, 0, :], a["L1_xattn_bo"].rearrange("(o n) -> o n", o=1)) \
                    .then_inc(*landed["wo"].up("all", by=16))
                pool.wait_ge(*landed["wo"].at("all"))

            @block.vector
            def _(dve):
                dve.wait_ge(*zeroed.at("all"))
                dve.wait_ge(*landed["mask"].at("all"))
                dve.tensor_copy(mf[:], m8[:]).then_inc(*folded.up("mask8"))
                dve.wait_ge(*folded.at("mask8"))
                dve.tensor_scalar(mf[:], mf[:], -1.0, OFF, ALU.add, ALU.mult).then_inc(*folded.up("mask"))
                dve.wait_ge(*folded.at("mask"))
                dve.tensor_copy(mask_q[:], mf[:])
                dve.wait_ge(*landed["turn"].at("all"))
                dve.tensor_copy(natwo_g[:, :, :, 0:HD], natwo[:].rearrange("p (g j d) -> p g j d", g=G, j=J)) \
                    .then_inc(*folded.up("natwo"))
                dve.tensor_tensor(nat_f0[:, 3, :].rearrange("c (m i) -> c m i", i=I0),
                                  nat_f0[:, 0, :].rearrange("c (m i) -> c m i", i=I0),
                                  nat_bin[:].unsqueeze(2).to_broadcast([C0, M0 // C0, I0]), ALU.mult) \
                    .then_inc(*folded.up("binw"))
                dve.wait_ge(*folded.at("binw"))
                dve.tensor_tensor(nat_f0[:, 3, :], nat_f0[:, 3, :], nat_f0[:, 1, :], ALU.add).then_inc(*folded.up("b1"))
                dve.wait_ge(*const.at("ident"))
                dve.tensor_copy(identb[:], ident[:])
                dve.wait_ge(*const.at("pick"))
                dve.tensor_copy(pick_r[:], pick_f[:])
                dve.wait_ge(*const.at("quad"))
                dve.tensor_reduce(hmask[:], quad[:].rearrange("p q j -> p j q"), AX.X, ALU.add)
                for i, (_, row) in enumerate(groups):
                    if i % 2 == 0:
                        dve.wait_ge(*turned.at(i))
                        for n, (src, dst, at) in enumerate(row):
                            k, m = src.shape
                            op = dve.tensor_copy(dst, bank[i % 8][0:m, at:at + k])
                        op.then_inc(*keptD.up(i))
                dve.wait_ge(*landed["small"].at("all"))
                dve.wait_ge(*keptD.at(2))
                for l in range(3):
                    for wide, w in ((WqR, Wq), (WkR, Wk)):
                        dve.tensor_copy(wide[l][:].rearrange("p g (q c) -> p g q c", c=32),
                                        w[l][:].rearrange("p (g c) -> p g c", c=32).unsqueeze(2).to_broadcast([P, G, 4, 32]))
                dve.tensor_copy(f0_in[:].rearrange("p (m i) -> p m i", i=I0), nat_in[:].unsqueeze(2).to_broadcast([P, M0, I0]))
                for c in range(C0):
                    dve.tensor_scalar(f0_out[:, c, :], f0_out[:, c, :], f0_cols[:, 2, c:c + 1], None, ALU.mult)
                dve.wait_ge(*turned.at("columns"))
                dve.tensor_copy(bcol[:], bank[0][:, 0:24].rearrange("p (l i g) -> p l i g", l=3, i=2))
                dve.tensor_tensor(f0_bias[:], bank[0][:, 24:25], f0_bout[:], ALU.add)
                for f, s in enumerate((ROOT / (N * S2), -ROOT / N, 1.0 / (N * (S2 - 1)))):
                    dve.tensor_scalar(t_w1b[:, f, :], bank[1][:, f * 64:(f + 1) * 64], s, None, ALU.mult)

            @block.tensor
            def _(pe):
                pe.wait_ge(*const.at("ident"))
                for i, (load, row) in enumerate(groups):
                    pe.wait_ge(*landed[load].at("all"))
                    if i == 1:
                        pe.wait_ge(*folded.at("natwo"))
                    if i == 2:
                        pe.wait_ge(*folded.at("b1"))
                    if load == "mask":
                        pe.wait_ge(*folded.at("mask"))
                    if i >= 8:
                        pe.wait_ge(*(keptA if i % 2 else keptD).at(i - 8))
                    for src, dst, at in row:
                        k, m = src.shape
                        op = pe.transpose(bank[i % 8][0:m, at:at + k], src, ident[0:k, 0:k])
                    op.then_inc(*turned.up(i))
                last = len(groups) - 1
                for i in range(max(0, last - 7), last + 1):
                    pe.wait_ge(*(keptA if i % 2 else keptD).at(i))
                pe.wait_ge(*landed["small"].at("all"))
                pe.wait_ge(*const.at("pick8"))
                for l in range(3):
                    for i in range(2):
                        for g in range(G):
                            c = (l * 2 + i) * G + g
                            for q in range(4):
                                pe.matmul(bank[0][32 * q:32 * q + 32, c:c + 1], brow[0:1, l, i, 32 * g:32 * g + 32],
                                          ones[0:1, 0:1], start=True, stop=True, tile_position=(0, 32 * q))
                pe.matmul(bank[0][:, 24:25], f0_wout[:], f0_b2[:], start=True, stop=True)
                for f in range(3):
                    op = pe.matmul(bank[1][:, f * 64:(f + 1) * 64], pick8[0:3, f, :], t_w1T[:], start=True, stop=True)
                op.then_inc(*turned.up("columns"))

        main(nc, a, out, dict(locals()))


def main(nc, a, out, v):
    ctx, sb, sig, sems, bank = v["ctx"], v["sb"], v["sig"], v["sems"], v["bank"]
    ident, identb, spread, pick_r, pick8 = v["ident"], v["identb"], v["spread"], v["pick_r"], v["pick8"]
    quad, hmask, ones, onesb, minus_half, gates_col = (v[n] for n in (
        "quad", "hmask", "ones", "onesb", "minus_half", "gates_col"))
    WqR, WkR, Wv, Wo, brow, bcol, W3x, diag = (v[n] for n in ("WqR", "WkR", "Wv", "Wo", "brow", "bcol", "W3x", "diag"))
    t_w1b, t_b1, t_b2, t_w2T, t_w3, t_b3 = (v[n] for n in ("t_w1b", "t_b1", "t_b2", "t_w2T", "t_w3", "t_b3"))
    f0_in, f0_out, f0_cols, f0_bias = (v[n] for n in ("f0_in", "f0_out", "f0_cols", "f0_bias"))
    mask_q, mask_k = v["mask_q"], v["mask_k"]
    router = {"F1": (v["m1_router"], v["m1_rb"], MOE1), "F2": (v["m2_router"], None, MOE2),
              "F3": (v["m3_router"], v["m3_rb"], MOE3)}
    m1_w1, m1_w3, m1_w2, m2_w1, m2_w2, m2_w3, m2_rms, m3_w, m3_b = (v[n] for n in (
        "m1_w1", "m1_w3", "m1_w2", "m2_w1", "m2_w2", "m2_w3", "m2_rms", "m3_w", "m3_b"))

    def two(name, shape, dt=F32):
        return [sb(f"{name}{s}", shape, dt) for s in range(STREAMS)]

    x = two("x", [P, T, P])
    ctxn = two("ctxn", [S2, P])
    ctxT = two("ctxT", [P, S2])
    xn = [sb("xn", [P, T, P])] * STREAMS
    xf = two("xf", [P, N])
    stats = two("stats", [P, T, 6])
    mv = two("mv", [P, T, 2])
    rstd = two("rstd", [P, 4, T])
    KT = two("KT", [P, H, S2], F32R)
    Ksp = [sb("Ksp", [P, G, S2])] * STREAMS
    VP = two("VP", [S2, H, 32])
    VM = two("VM", [S2, H, 32])
    mk_i = two("mk_i", [S2, 2], mybir.dt.int32)
    mr_i = two("mr_i", [1, 2, S2], mybir.dt.int32)
    mk = two("mk", [S2, 4])
    mr_f = two("mr_f", [1, 2, S2])
    mr = two("mr", [1, 2, S2], BF16)
    ksum = two("ksum", [P, G])
    lg = two("lg", [P, T, LG])
    top = two("top", [P, T, 8])
    rep = two("rep", [P, T, LG])
    gw = two("gw", [P, T, EMAX])
    gs = two("gs", [P, 2, T])
    gT = two("gT", [EMAX, N])
    Qs = sb("Qs", [P, G, N], F32R)
    qsum = sb("qsum", [P, G])
    nm = sb("nm", [P, T, H])
    nmT = sb("nmT", [H, N], F32R)
    PT = [sb(f"PT{i}", [S2, N]) for i in range(4)]
    Os = sb("Os", [P, G, N])
    R = sb("R", [P, 2, N])
    oT = sb("oT", [P, N])
    scratch = sb("scratch", [P, 5 * N])
    hb = [scratch[:, i * N:(i + 1) * N] for i in range(3)]
    xw = [scratch[:, i * N:(i + 1) * N] for i in (3, 4)]
    EW = 2 * J * S2
    Eb = scratch[:, 0:2 * EW].rearrange("p (i k) -> p i k", i=2)
    Eq = scratch[:, 2 * EW:4 * EW].rearrange("p (i k) -> p i k", i=2)
    Z = sb("Z", [P, 2, T, H])
    feat = sb("feat", [P, 3, H])
    pk = sb("pk", [P, G])
    zt = sb("zt", [P, 2, T, H])
    hid = sb("hid", [64, 2, H])
    invt = sb("invt", [S2, 3, H])
    x1r, x2r = Os[:, 0, :], sb("x2r", [P, 2, S2])
    nm3 = sb("nm3", [P, T])
    nmT3 = sb("nmT3", [1, N])

    in_x, in_ctx, in_mask = ([sig(f"{n}{i}") for i in range(STREAMS)] for n in ("in_x", "in_ctx", "in_mask"))
    (xT_ps, xf_s, stat_s, mv_s, rs_s, xn_s, done_x, kps, ksp, kt_s, vps, vp_s, cps, c_s,
     maskd, qps, qs_s, qlo, sps, nm_s, nmps, nmT_s, st, pt, ops, os_s, dps, r_s, at_s, fps, oT_s, ft, chk, chkA,
     chkV, lps, lg_s, gx, ge, gps, gT_s, wbps, xw_s, esub, eexp, esq, temp, tps, tact, stored, mskv, oT3) = (sig(n) for n in (
        "xT_ps xf_s stat_s mv_s rs_s xn_s done_x kps ksp kt_s vps vp_s cps c_s "
        "maskd qps qs_s qlo sps nm_s nmps nmT_s st pt ops os_s dps r_s at_s fps oT_s ft chk chkA "
        "chkV lps lg_s gx ge gps gT_s wbps xw_s esub eexp esq temp tps tact stored mskv oT3").split())
    mine = sorted(s.num for s in (in_x[0].sem, oT3.sem))
    to_clear = range(mine[0], mine[1] + 1)

    def prev(u):
        return u - STREAMS

    xv = a["x"].rearrange("(i s) (p t) d -> i s p t d", s=STREAMS, t=T)
    ov = out.rearrange("(i s) (p t) d -> i s p t d", s=STREAMS, t=T)
    cv = a["ctx_1024"].rearrange("(i s) k d -> i s k d", s=STREAMS)
    ik = a["mask_BxS2_ik0"].rearrange("(i s) k -> i s k", s=STREAMS)
    jf = a["mask_BxS2_if1"].rearrange("(i s) k -> i s k", s=STREAMS)

    it = ctx.enter_context(nc.Fori(0, B // STREAMS))
    with nc.Block() as block:

        @block.sync
        def _(sp):
            for s in range(STREAMS):
                sp.dma_start(x[s][:], xv[it, s]).then_inc(*in_x[s].up("all", by=16))
                sp.dma_start(ctxn[s][:], cv[it, s]).then_inc(*in_ctx[s].up("all", by=16))
                for i, m in enumerate((ik, jf)):
                    sp.dma_start(mk_i[s][:, i:i + 1], m[it, s].rearrange("(k o) -> k o", o=1)).then_inc(*in_mask[s].up(i, 0, by=16))
                    sp.dma_start(mr_i[s][:, i, :], m[it, s].rearrange("(o k) -> o k", o=1)).then_inc(*in_mask[s].up(i, 1, by=16))
            for s in range(STREAMS):
                sp.wait_ge(*done_x.at(UNITS - STREAMS + s))
                sp.dma_start(ov[it, s], x[s][:]).then_inc(*stored.up(s, by=16))
            sp.wait_ge(*stored.at(STREAMS - 1))

        @block.gpsimd
        def _(pool):
            def head(u):
                s, k = u % STREAMS, kind(u)
                pool.wait_ge(*mv_s.at(u))
                pool.tensor_scalar_add(rstd[s][:, 0, :], mv[s][:, :, 1], LN_EPS).then_inc(*rs_s.up(u, "eps"))
                pool.wait_ge(*rs_s.at(u, "eps"))
                pool.tensor_tensor(rstd[s][:, 1, :], rstd[s][:, 0, :], minus_half[:], ALU.pow).then_inc(*rs_s.up(u))
                if k == "F2":
                    pool.wait_ge(*rs_s.at(u))
                    pool.tensor_tensor(rstd[s][:, 2, :], rstd[s][:, 1, :], rstd[s][:, 1, :], ALU.mult).then_inc(*rs_s.up(u, "sq"))
                    pool.wait_ge(*rs_s.at(u, "sq"))
                    pool.tensor_tensor(rstd[s][:, 2, :], rstd[s][:, 2, :], mv[s][:, :, 1], ALU.mult).then_inc(*rs_s.up(u, "ms"))
                    pool.wait_ge(*rs_s.at(u, "ms"))
                    pool.tensor_scalar_add(rstd[s][:, 2, :], rstd[s][:, 2, :], RMS_EPS).then_inc(*rs_s.up(u, "ms_eps"))
                    pool.wait_ge(*rs_s.at(u, "ms_eps"))
                    pool.tensor_tensor(rstd[s][:, 3, :], rstd[s][:, 2, :], minus_half[:], ALU.pow).then_inc(*rs_s.up(u, "rms"))

            def first(u):
                pass

            def second(u):
                k = kind(u)
                if k in ("A0", "A1", "A2"):
                    for g in range(G):
                        pool.wait_ge(*r_s.at(u, g))
                        pool.tensor_tensor(Os[:, g, :], Os[:, g, :], R[:, g % 2, :], ALU.mult).then_inc(*at_s.up(u, g))

            for s in range(STREAMS):
                pool.memset(VP[s][:], 0.0)
                pool.memset(VM[s][:], 0.0).then_inc(*maskd.up("zero", s))
                pool.wait_ge(*maskd.at("zero", s))
                pool.memset(VP[s][:, :, HD:2 * HD], 1.0)
                pool.memset(lg[s][:], PAD).then_inc(*maskd.up("pads", s))
            head(0)
            for u in range(UNITS):
                first(u)
                if u + 1 < UNITS:
                    head(u + 1)
                second(u)

        @block.scalar
        def _(act):
            def head(u):
                s, k = u % STREAMS, kind(u)
                if k == "A0":
                    act.wait_ge(*cps.at(s))
                    act.activation(ctxT[s][:], bank[5][:, 0:S2], ACT.Copy).then_inc(*c_s.up(s))
                act.wait_ge(*xT_ps.at(u, T - 1))
                act.activation(xf[s][:], bank[4][:], ACT.Copy, scale=m2_rms[:, 0:1] if k == "F2" else 1.0) \
                    .then_inc(*xf_s.up(u))
                if k in ("A0", "A1", "A2"):
                    l = int(k[1])
                    act.wait_ge(*kps.at(u, G - 1))
                    if u >= 1 and kind(u - 1) == k:
                        act.wait_ge(*kt_s.at(u - 1, J - 1))
                    for g in range(G):
                        act.activation(Ksp[s][:, g, :].bitcast(F32R), bank[5][:, g * S2:(g + 1) * S2], ACT.Identity,
                                       bias=bcol[:, l, 1, g:g + 1], accum_out=ksum[s][:, g:g + 1]).then_inc(*ksp.up(u, g))
                    if u >= STREAMS:
                        act.wait_ge(*done_x.at(prev(u)))
                    act.wait_ge(*vps.at(u))
                    act.activation(VP[s][:, :, 0:HD] if l != 2 else VM[s][:, :, 0:HD],
                                   bank[4][0:S2, 0:P].rearrange("p (h d) -> p h d", d=HD), ACT.Copy,
                                   scale=mk[s][:, 1:2] if l == 2 else 1.0).then_inc(*vp_s.up(u))
                if k in router:
                    act.wait_ge(*gx.at(u, "sub"))
                    act.activation(gw[s][:, :, 0:router[k][2]], gw[s][:, :, 0:router[k][2]], ACT.Exp).then_inc(*ge.up(u))
                    act.wait_ge(*gps.at(u))
                    act.activation(gT[s][0:router[k][2], :], bank[5][0:router[k][2], :], ACT.Copy).then_inc(*gT_s.up(u))

            def first(u):
                k = kind(u)
                l = int(k[1])
                if k in ("A0", "A1", "A2"):
                    for g in range(G):
                        act.wait_ge(*qps.at(u, g))
                        act.activation(Qs[:, g, :], bank[g][:], ACT.Identity, bias=bcol[:, l, 0, g:g + 1],
                                       accum_out=qsum[:, g:g + 1]).then_inc(*qs_s.up(u, g))
                    if l == 1:
                        for n in range(2 * T):
                            act.wait_ge(*esub.at(u, n))
                            act.activation(Eb[:, n % 2, :], Eb[:, n % 2, :], ACT.Exp, scale=ROOT).then_inc(*eexp.up(u, n))
                            act.wait_ge(*eexp.at(u, n))
                            act.activation(Eq[:, n % 2, :], Eb[:, n % 2, :], ACT.Square).then_inc(*esq.up(u, n))
                        act.wait_ge(*tps.at(u, 0))
                        act.activation(hid[:, 0, :], bank[0][0:64, 0:H], ACT.Gelu, bias=t_b1[:, 0:1]).then_inc(*tact.up(u, 0))
                        act.wait_ge(*tps.at(u, 1))
                        act.activation(hid[:, 1, :], bank[0][0:64, 32:32 + H], ACT.Gelu, bias=t_b2[:, 0:1]).then_inc(*tact.up(u, 1))
                        act.wait_ge(*temp.at(u, "clip"))
                        act.activation(invt[:, 1, :], invt[:, 0, :], ACT.Exp, scale=-1.0).then_inc(*tact.up(u, 2))
                    act.wait_ge(*nmps.at(u))
                    act.activation(nmT[:], bank[4][0:H, :], ACT.Copy).then_inc(*nmT_s.up(u))
                if k == "A3":
                    act.wait_ge(*qps.at(u, 0))
                    act.activation(x1r, bank[0][:], ACT.Relu).then_inc(*qs_s.up(u, 0))
                    act.activation(x2r[:, 0, :], bank[1][:, 0:S2], ACT.Relu).then_inc(*qs_s.up(u, 1))
                    act.wait_ge(*nmps.at(u))
                    act.activation(nmT3[:], bank[4][0:1, :], ACT.Copy).then_inc(*nmT_s.up(u))

            def second(u):
                s, k = u % STREAMS, kind(u)
                l = int(k[1])
                if k in ("A0", "A1", "A2"):
                    def copy_out(g):
                        act.wait_ge(*ops.at(u, g))
                        act.activation(Os[:, g, :], bank[g][:], ACT.Copy).then_inc(*os_s.up(u, g))
                    for h in range(H):
                        act.wait_ge(*st.at(u, h))
                        if h >= 4:
                            act.wait_ge(*ops.at(u, h // J - 1))
                        if l == 1:
                            act.wait_ge(*temp.at(u, "invt"))
                        act.activation(PT[h % 4][:], bank[6 + h % 2][0:S2, :], ACT.Exp,
                                       scale=invt[:, 2, h:h + 1] if l == 1 else ROOT,
                                       bias=mk[s][:, 2:3] if l == 2 else 0.0).then_inc(*pt.up(u, h))
                        if h % J == 1 and h > J:
                            copy_out(h // J - 1)
                    copy_out(G - 1)
                if k == "A3":
                    act.wait_ge(*st.at(u, 0))
                    act.activation(PT[0][:], bank[6][0:S2, :], ACT.Exp, bias=mk[s][:, 3:4]).then_inc(*pt.up(u, 0))
                if k == "F0":
                    for c in range(C0):
                        act.wait_ge(*chk.at(u, c))
                        if c >= 3:
                            act.wait_ge(*fps.at(u, c - 3))
                        act.activation(hb[c % 3], bank[c % 4][:], ACT.Relu, scale=f0_cols[:, 0, c:c + 1],
                                       bias=f0_cols[:, 1, c:c + 1]).then_inc(*chkA.up(u, c))
                if k in ("F1", "F2"):
                    w = F1 if k == "F1" else F2
                    n = 0
                    for e in range(router[k][2]):
                        for o, m in pieces(w):
                            act.wait_ge(*chk.at(u, n))
                            if n >= 3:
                                act.wait_ge(*fps.at(u, n - 3))
                            act.activation(hb[n % 3][0:m, :], bank[2 * (n % 2)][0:m, :], ACT.Silu).then_inc(*chkA.up(u, n))
                            n += 1
                if k != "A3":
                    act.wait_ge(*fps.at(u, "end"))
                    src = bank[0] if k[0] == "A" else bank[6]
                    act.activation(oT[:], src[:], ACT.Identity, bias=f0_bias[:, 0:1] if k == "F0" else 0.0) \
                        .then_inc(*oT_s.up(u))

            head(0)
            for u in range(UNITS):
                first(u)
                if u + 1 < UNITS:
                    head(u + 1)
                second(u)

        @block.vector
        def _(dve):
            def head(u):
                s, k = u % STREAMS, kind(u)
                if u < STREAMS:
                    dve.wait_ge(*in_x[s].at("all"))
                else:
                    dve.wait_ge(*done_x.at(prev(u)))
                for t in range(T):
                    dve.bn_stats(stats[s][:, t, :], x[s][:, t, :]).then_inc(*stat_s.up(u, t))
                for t in range(T):
                    dve.wait_ge(*stat_s.at(u, t))
                    op = dve.bn_aggr(mv[s][:, t, :], stats[s][:, t, :])
                op.then_inc(*mv_s.up(u))
                if k == "A0":
                    dve.wait_ge(*in_mask[s].at(1, 1))
                    dve.tensor_copy(mk[s][:, 0:1], mk_i[s][:, 0:1])
                    dve.tensor_copy(mk[s][:, 3:4], mk_i[s][:, 1:2])
                    dve.tensor_copy(mr_f[s][:], mr_i[s][:]).then_inc(*mskv.up("raw", s))
                    dve.wait_ge(*mskv.at("raw", s))
                    dve.tensor_scalar(mk[s][:, 1:2], mk[s][:, 0:1], 0.0, None, ALU.not_equal)
                    dve.tensor_scalar(mk[s][:, 3:4], mk[s][:, 3:4], -1.0, 1.0e4, ALU.add, ALU.mult)
                    dve.tensor_scalar(mr_f[s][:, 0, :], mr_f[s][:, 0, :], 0.0, None, ALU.not_equal).then_inc(*mskv.up("kept", s))
                    dve.wait_ge(*mskv.at("kept", s))
                    dve.tensor_scalar(mk[s][:, 2:3], mk[s][:, 1:2], -1.0, OFF, ALU.add, ALU.mult)
                    dve.tensor_scalar(mr[s][:, 0, :], mr_f[s][:, 0, :], -1.0, OFF, ALU.add, ALU.mult)
                    dve.tensor_scalar(mr[s][:, 1, :], mr_f[s][:, 1, :], -1.0, 1.0e4, ALU.add, ALU.mult) \
                        .then_inc(*mskv.up("all", s))
                    dve.wait_ge(*mskv.at("all", s))
                    dve.wait_ge(*maskd.at("pads", s))
                    dve.tensor_copy(VM[s][:, :, HD:2 * HD], mk[s][:, 1:2].unsqueeze(2).to_broadcast([S2, H, HD])) \
                        .then_inc(*mskv.up("vm", s))
                dve.wait_ge(*rs_s.at(u))
                if u >= 1:
                    dve.wait_ge(*xT_ps.at(u - 1, T - 1))
                for t in range(T):
                    dve.tensor_scalar(xn[s][:, t, :], x[s][:, t, :], mv[s][:, t, 0:1], rstd[s][:, 1, t:t + 1],
                                      ALU.subtract, ALU.mult).then_inc(*xn_s.up(u, t))
                if k == "F2":
                    for t in range(T):
                        dve.wait_ge(*xn_s.at(u, t))
                        dve.scalar_tensor_tensor(out=x[s][:, t, :], in0=xn[s][:, t, :], scalar=gates_col[:, 1, 2:3],
                                                 in1=x[s][:, t, :], op0=ALU.mult, op1=ALU.add).then_inc(*xn_s.up(u, t, "x"))
                    dve.wait_ge(*rs_s.at(u, "rms"))
                    for t in range(T):
                        dve.wait_ge(*xn_s.at(u, t, "x"))
                        dve.tensor_scalar(xn[s][:, t, :], xn[s][:, t, :], rstd[s][:, 3, t:t + 1], None, ALU.mult) \
                            .then_inc(*xn_s.up(u, t, "y"))
                if k in ("A0", "A1", "A2"):
                    l = int(k[1])
                    dve.wait_ge(*ksp.at(u, G - 1))
                    for q in (1, 3):
                        for g in range(G):
                            r = slice(32 * q, 32 * q + 32)
                            dve.scalar_tensor_tensor(out=Ksp[s][r, g, :], in0=bank[5][r, g * S2:(g + 1) * S2],
                                                     scalar=bcol[r, l, 1, g:g + 1], in1=Ksp[s][r, g, :],
                                                     op0=ALU.add, op1=ALU.subtract).then_inc(*kt_s.up(u, "lo", q, g))
                    dve.wait_ge(*kt_s.at(u, "lo", 3, G - 1))
                    if u >= STREAMS:
                        dve.wait_ge(*done_x.at(prev(u)))
                    ktv = KT[s][:].rearrange("p (g j) k -> p g j k", j=J)
                    for j in range(J):
                        dve.tensor_scalar(ktv[:, :, j, :], Ksp[s][:], hmask[:, j:j + 1], None, ALU.mult) \
                            .then_inc(*kt_s.up(u, j))
                if k in router:
                    E = router[k][2]
                    dve.wait_ge(*maskd.at("pads", s))
                    dve.wait_ge(*lps.at(u))
                    dve.tensor_copy(lg[s][:, :, 0:E], bank[5][:, 0:T * E].rearrange("p (t e) -> p t e", e=E)) \
                        .then_inc(*lg_s.up(u, "logits"))
                    dve.wait_ge(*lg_s.at(u, "logits"))
                    for t in range(T):
                        dve.max(top[s][:, t, :], lg[s][:, t, :]).then_inc(*lg_s.up(u, "top", t))
                    dve.wait_ge(*lg_s.at(u, "top", T - 1))
                    dve.tensor_tensor(gw[s][:, :, 0:E], lg[s][:, :, 0:E], top[s][:, :, 0:1].to_broadcast([P, T, E]),
                                      ALU.subtract).then_inc(*gx.up(u, "sub"))
                    dve.memset(top[s][:, :, 2:8], PAD).then_inc(*lg_s.up(u, "two"))
                    dve.wait_ge(*lg_s.at(u, "two"))
                    for t in range(T):
                        dve.match_replace(rep[s][:, t, :], in_to_replace=top[s][:, t, :], in_values=lg[s][:, t, :],
                                          imm_value=-PAD).then_inc(*lg_s.up(u, "rep", t))
                    dve.wait_ge(*lg_s.at(u, "rep", T - 1))
                    dve.tensor_tensor(rep[s][:, :, 0:E], rep[s][:, :, 0:E], lg[s][:, :, 0:E], ALU.not_equal) \
                        .then_inc(*lg_s.up(u, "sel"))
                    dve.wait_ge(*ge.at(u))
                    dve.wait_ge(*lg_s.at(u, "sel"))
                    if k == "F3":
                        dve.tensor_reduce(gs[s][:, 0, :], gw[s][:, :, 0:E], AX.X, ALU.add).then_inc(*lg_s.up(u, "sum"))
                        dve.wait_ge(*lg_s.at(u, "sum"))
                    dve.tensor_tensor(gw[s][:, :, 0:E], gw[s][:, :, 0:E], rep[s][:, :, 0:E], ALU.mult) \
                        .then_inc(*lg_s.up(u, "kept"))
                    dve.wait_ge(*lg_s.at(u, "kept"))
                    if k != "F3":
                        dve.tensor_reduce(gs[s][:, 0, :], gw[s][:, :, 0:E], AX.X, ALU.add).then_inc(*lg_s.up(u, "sum"))
                        dve.wait_ge(*lg_s.at(u, "sum"))
                    dve.reciprocal(gs[s][:, 1, :], gs[s][:, 0, :]).then_inc(*lg_s.up(u, "inv"))
                    dve.wait_ge(*lg_s.at(u, "inv"))
                    dve.tensor_tensor(gw[s][:, :, 0:E], gw[s][:, :, 0:E], gs[s][:, 1, :].unsqueeze(2).to_broadcast([P, T, E]),
                                      ALU.mult).then_inc(*lg_s.up(u, "gates"))

            def first(u):
                s, k = u % STREAMS, kind(u)
                l = int(k[1])
                if k in ("A0", "A1", "A2"):
                    for g in range(G):
                        dve.wait_ge(*qs_s.at(u, g))
                        dve.scalar_tensor_tensor(out=Qs[64:128, g, :], in0=bank[g][64:128, :],
                                                 scalar=bcol[64:128, l, 0, g:g + 1], in1=Qs[64:128, g, :].bitcast(F32),
                                                 op0=ALU.add, op1=ALU.subtract).then_inc(*qlo.up(u, g))

                    def sums(n):
                        t, p = n // 2, n % 2
                        dve.wait_ge(*esq.at(u, n))
                        dve.tensor_reduce(Z[:, 0, t, 8 * p:8 * p + 8], Eb[:, p, :].rearrange("p (h k) -> p h k", k=S2),
                                          AX.X, ALU.add)
                        dve.tensor_reduce(Z[:, 1, t, 8 * p:8 * p + 8], Eq[:, p, :].rearrange("p (h k) -> p h k", k=S2),
                                          AX.X, ALU.add).then_inc(*temp.up(u, "sums", n))

                    for n in range(2 * T):
                        t, p = n // 2, n % 2
                        for i in range(2):
                            g = 2 * p + i
                            dve.wait_ge(*sps.at(u, n, i))
                            op = dve.tensor_reduce(nm[:, t, J * g:J * g + J],
                                                   bank[g][:, 0:J * S2].rearrange("p (h k) -> p h k", k=S2),
                                                   AX.X, ALU.max, negate=True)
                            op.then_inc(*nm_s.up(u, n, i))
                        if l == 1:
                            if n >= 2:
                                sums(n - 2)
                                dve.wait_ge(*temp.at(u, "sums", n - 2))
                            for i in range(2):
                                g = 2 * p + i
                                dve.wait_ge(*nm_s.at(u, n, i))
                                op = dve.tensor_tensor(
                                    Eb[:, p, i * J * S2:(i + 1) * J * S2].rearrange("p (h k) -> p h k", k=S2),
                                    bank[g][:, 0:J * S2].rearrange("p (h k) -> p h k", k=S2),
                                    nm[:, t, J * g:J * g + J].unsqueeze(2).to_broadcast([P, J, S2]), ALU.add)
                            op.then_inc(*esub.up(u, n))
                    if l == 1:
                        sums(2 * T - 2)
                        sums(2 * T - 1)
                        dve.wait_ge(*temp.at(u, "sums", 2 * T - 1))
                        dve.reciprocal(zt[:, 0], Z[:, 0]).then_inc(*temp.up(u, "inv"))
                        dve.tensor_reduce(feat[:, 1, :], nm[:].rearrange("p t h -> p h t"), AX.X, ALU.add)
                        dve.tensor_tensor(pk[:], qsum[:], ksum[s][:], ALU.mult).then_inc(*temp.up(u, "pk"))
                        dve.wait_ge(*temp.at(u, "inv"))
                        dve.tensor_tensor(zt[:, 1], Z[:, 1], zt[:, 0], ALU.mult).then_inc(*temp.up(u, "z1"))
                        dve.wait_ge(*temp.at(u, "z1"))
                        dve.tensor_tensor(zt[:, 1], zt[:, 1], zt[:, 0], ALU.mult).then_inc(*temp.up(u, "z2"))
                        dve.wait_ge(*temp.at(u, "z2"))
                        dve.tensor_scalar(zt[:, 1], zt[:, 1], 1.0 / S2, None, ALU.subtract).then_inc(*temp.up(u, "z3"))
                        dve.tensor_tensor(feat[:, 0, :].rearrange("p (g j) -> p g j", j=J),
                                          pk[:].unsqueeze(2).to_broadcast([P, G, J]),
                                          quad[:, 0:1, :].to_broadcast([P, G, J]), ALU.mult)
                        dve.wait_ge(*temp.at(u, "z3"))
                        dve.tensor_reduce(feat[:, 2, :], zt[:, 1].rearrange("p t h -> p h t"), AX.X, ALU.add) \
                            .then_inc(*temp.up(u, "feat"))
                        dve.wait_ge(*tps.at(u, 2))
                        dve.tensor_scalar(invt[:, 0, :], bank[0][0:S2, 64:64 + H], t_b3[:, 0:1], LOG_T_MIN, ALU.add, ALU.max) \
                            .then_inc(*temp.up(u, "low"))
                        dve.wait_ge(*temp.at(u, "low"))
                        dve.tensor_scalar(invt[:, 0, :], invt[:, 0, :], LOG_T_MAX, None, ALU.min).then_inc(*temp.up(u, "clip"))
                        dve.wait_ge(*tact.at(u, 2))
                        dve.tensor_scalar(invt[:, 2, :], invt[:, 1, :], 0.5, None, ALU.mult).then_inc(*temp.up(u, "invt"))
                if k == "A3":
                    dve.wait_ge(*qs_s.at(u, 1))
                    dve.tensor_scalar(x2r[:, 1, :], x2r[:, 0, :], diag[:, 0:1], None, ALU.mult).then_inc(*qlo.up(u, 1))
                    dve.wait_ge(*sps.at(u, 0))
                    dve.tensor_reduce(nm3[:], bank[2][:, 0:T * S2].rearrange("p (t k) -> p t k", k=S2), AX.X, ALU.max,
                                      negate=True).then_inc(*nm_s.up(u, 0))

            def second(u):
                s, k = u % STREAMS, kind(u)
                l = int(k[1])
                if k in ("A0", "A1", "A2"):
                    for g in range(G):
                        dve.wait_ge(*dps.at(u, g))
                        if g >= 2:
                            dve.wait_ge(*at_s.at(u, g - 2))
                        dve.reciprocal(R[:, g % 2, :], bank[g][:]).then_inc(*r_s.up(u, g))
                if k == "A3":
                    dve.wait_ge(*dps.at(u, 0))
                    dve.reciprocal(R[:, 0, :], bank[3][:]).then_inc(*r_s.up(u, 0))
                    dve.wait_ge(*r_s.at(u, 0))
                    dve.tensor_tensor(oT[:], bank[0][:], R[:, 0, :], ALU.mult).then_inc(*oT3.up(u))
                if k in ("F1", "F2"):
                    w = F1 if k == "F1" else F2
                    n = 0
                    for e in range(router[k][2]):
                        dve.wait_ge(*wbps.at(u, e))
                        if n >= 2:
                            dve.wait_ge(*chk.at(u, n - 1))
                        dve.tensor_tensor(xw[e % 2], xf[s][:], bank[7][:], ALU.mult).then_inc(*xw_s.up(u, e))
                        for o, m in pieces(w):
                            dve.wait_ge(*chkA.at(u, n))
                            dve.tensor_tensor(hb[n % 3][0:m, :], hb[n % 3][0:m, :], bank[2 * (n % 2) + 1][0:m, :], ALU.mult) \
                                .then_inc(*chkV.up(u, n))
                            n += 1
                if k == "F3":
                    for e in range(MOE3):
                        dve.wait_ge(*wbps.at(u, e))
                        if e >= 2:
                            dve.wait_ge(*fps.at(u, e - 2))
                        dve.tensor_tensor(xw[e % 2], xf[s][:], bank[7][:] if e % 2 else bank[0][:], ALU.mult) \
                            .then_inc(*xw_s.up(u, e))
                dve.wait_ge(*ft.at(u))
                dve.scalar_tensor_tensor(out=x[s][:].rearrange("p t d -> p (t d)"), in0=(bank[1])[:],
                                         scalar=gates_col[:, 0 if k[0] == "A" else 1, l:l + 1],
                                         in1=x[s][:].rearrange("p t d -> p (t d)"), op0=ALU.mult, op1=ALU.add) \
                    .then_inc(*done_x.up(u))

            head(0)
            for u in range(UNITS):
                first(u)
                if u + 1 < UNITS:
                    head(u + 1)
                second(u)

        @block.tensor
        def _(pe):
            def head(u):
                s, k = u % STREAMS, kind(u)
                if k == "A0":
                    pe.wait_ge(*in_ctx[s].at("all"))
                    if s:
                        pe.wait_ge(*kt_s.at(u - 1, "lo", 3, G - 1))
                    pe.transpose(bank[5][:, 0:S2], ctxn[s][:], ident[0:S2, 0:S2]).then_inc(*cps.up(s))
                free4(u)
                for t in range(T):
                    pe.wait_ge(*(xn_s.at(u, t, "y") if k == "F2" else xn_s.at(u, t)))
                    pe.transpose(bank[4][:, t * P:(t + 1) * P], xn[s][:, t, :], ident[:]).then_inc(*xT_ps.up(u, t))
                if k in ("A0", "A1", "A2"):
                    l = int(k[1])
                    pe.wait_ge(*c_s.at(s))
                    free5(u)
                    for g in range(G):
                        pe.matmul(bank[5][:, g * S2:(g + 1) * S2],
                                  WkR[l][:, g, :], ctxT[s][:],
                                  start=True, stop=True).then_inc(*kps.up(u, g))
                    pe.wait_ge(*xf_s.at(u))
                    pe.matmul(bank[4][0:S2, 0:P], ctxT[s][:], Wv[l][:], start=True, stop=False)
                    pe.matmul(bank[4][0:S2, 0:P], ones[0:1, 0:S2], brow[0:1, l, 2, :], start=False, stop=True) \
                        .then_inc(*vps.up(u))
                if k in router:
                    w, b, E = router[k]
                    free5(u)
                    pe.wait_ge(*xf_s.at(u))
                    for t in range(T):
                        dst = bank[5][:, t * E:(t + 1) * E]
                        op = pe.matmul(dst, xf[s][:, t * P:(t + 1) * P], w[:], start=True, stop=b is None)
                        if b is not None:
                            op = pe.matmul(dst, ones[0:1, 0:P], b[:], start=False, stop=True)
                    op.then_inc(*lps.up(u))
                    pe.wait_ge(*lg_s.at(u, "gates"))
                    for t in range(T):
                        op = pe.transpose(bank[5][0:E, t * P:(t + 1) * P], gw[s][:, t, 0:E], ident[:])
                    op.then_inc(*gps.up(u))

            def free4(u):
                if u >= 1:
                    if kind(u - 1) in ("A0", "A1", "A2"):
                        pe.wait_ge(*vp_s.at(u - 1))
                    pe.wait_ge(*xf_s.at(u - 1))
                    if kind(u - 1)[0] == "A":
                        pe.wait_ge(*nmT_s.at(u - 1))

            def free5(u):
                if u >= 1:
                    if kind(u - 1) in router:
                        pe.wait_ge(*gT_s.at(u - 1))
                    elif kind(u - 1) in ("A0", "A1", "A2"):
                        pe.wait_ge(*kt_s.at(u - 1, "lo", 3, G - 1))

            def free_work(u):
                if u >= 1:
                    pe.wait_ge(*done_x.at(u - 1))

            def first(u):
                s, k = u % STREAMS, kind(u)
                l = int(k[1])
                pe.wait_ge(*xf_s.at(u))
                free_work(u)
                if k in ("A0", "A1", "A2"):
                    for g in range(G):
                        pe.matmul(bank[g][:], WqR[l][:, g, :], xf[s][:],
                                  start=True, stop=True).then_inc(*qps.up(u, g))
                    pe.wait_ge(*kt_s.at(u, J - 1))
                    for n in range(2 * T):
                        t, p = n // 2, n % 2
                        for i in range(2):
                            g = 2 * p + i
                            if n < 2:
                                pe.wait_ge(*qlo.at(u, g))
                            elif l == 1:
                                pe.wait_ge(*esub.at(u, n - 2))
                            else:
                                pe.wait_ge(*nm_s.at(u, n - 2, i))
                            dst = bank[g][:, 0:J * S2]
                            op = pe.matmul(dst, Qs[:, g, t * P:(t + 1) * P],
                                           KT[s][:, J * g:J * g + J, :].rearrange("p h k -> p (h k)"),
                                           start=True, stop=l == 1)
                            if l == 0:
                                op = pe.matmul(dst, identb[:], mask_q[:, t:t + 1, :].to_broadcast([P, J, S2]),
                                               start=False, stop=True)
                            if l == 2:
                                op = pe.matmul(dst, onesb[:], mr[s][0:1, 0:1, :].to_broadcast([1, J, S2]),
                                               start=False, stop=True)
                            op.then_inc(*sps.up(u, n, i))
                    if l == 1:
                        pe.wait_ge(*temp.at(u, "feat"))
                        for f in range(3):
                            op = pe.matmul(bank[0][0:64, 0:H], t_w1b[:, f, :], feat[:, f, :], start=f == 0, stop=f == 2)
                        op.then_inc(*tps.up(u, 0))
                        pe.wait_ge(*tact.at(u, 0))
                        pe.matmul(bank[0][0:64, 32:32 + H], t_w2T[:], hid[:, 0, :], start=True, stop=True).then_inc(*tps.up(u, 1))
                        pe.wait_ge(*tact.at(u, 1))
                        pe.matmul(bank[0][0:S2, 64:64 + H], t_w3[:, 0:1].to_broadcast([64, S2]), hid[:, 1, :],
                                  start=True, stop=True).then_inc(*tps.up(u, 2))
                    pe.wait_ge(*nm_s.at(u, 2 * T - 1, 1))
                    pe.wait_ge(*vp_s.at(u))
                    for t in range(T):
                        op = pe.transpose(bank[4][0:H, t * P:(t + 1) * P], nm[:, t, :], ident[:])
                    op.then_inc(*nmps.up(u))
                if k == "A3":
                    pe.matmul(bank[0][:], W3x[:], xf[s][:], start=True, stop=True)
                    pe.matmul(bank[1][:, 0:S2], W3x[:], ctxT[s][:], start=True, stop=True).then_inc(*qps.up(u, 0))
                    pe.wait_ge(*qlo.at(u, 1))
                    for t in range(T):
                        dst = bank[2][:, t * S2:(t + 1) * S2]
                        pe.matmul(dst, x1r[:, t * P:(t + 1) * P], x2r[:, 1, :], start=True, stop=False)
                        op = pe.matmul(dst, onesb[:], mr[s][0:1, 1, :], start=False, stop=True)
                    op.then_inc(*sps.up(u, 0))
                    pe.wait_ge(*nm_s.at(u, 0))
                    for t in range(T):
                        op = pe.transpose(bank[4][0:1, t * P:(t + 1) * P], nm3[:, t:t + 1], ident[:])
                    op.then_inc(*nmps.up(u))

            def second(u):
                s, k = u % STREAMS, kind(u)
                l = int(k[1])
                if k in ("A0", "A1", "A2"):
                    vals = VM[s] if l == 2 else VP[s]
                    pe.wait_ge(*nmT_s.at(u))
                    if l == 1:
                        pe.wait_ge(*temp.at(u, "clip"))

                    def weigh(g):
                        for j in range(J):
                            h = g * J + j
                            pe.wait_ge(*pt.at(u, h))
                            op = pe.matmul(bank[g][32 * j:32 * j + 32, :], vals[:, h, :], PT[h % 4][:], start=True, stop=True,
                                           tile_position=(0, 32 * j))
                        op.then_inc(*ops.up(u, g))

                    def denominators(g):
                        pe.wait_ge(*os_s.at(u, g))
                        pe.matmul(bank[g][:], spread[:], Os[:, g, :], start=True, stop=True).then_inc(*dps.up(u, g))

                    for h in range(H):
                        if h >= 2:
                            pe.wait_ge(*pt.at(u, h - 2))
                        dst = bank[6 + h % 2][0:S2, :]
                        pe.matmul(dst, KT[s][:, h, :], Qs[:, h // J, :], start=True, stop=False)
                        if l == 0:
                            pe.matmul(dst, identb[0:S2, 0:S2], mask_k[:], start=False, stop=False)
                        pe.matmul(dst, pick_r[:, h, :], nmT[:], start=False, stop=True).then_inc(*st.up(u, h))
                        if h % J == J - 1:
                            weigh(h // J)
                        if h % J == 2 and h > J:
                            denominators(h // J - 1)
                    denominators(G - 1)
                    pe.wait_ge(*r_s.at(u, 0))
                    for g in range(G):
                        pe.wait_ge(*at_s.at(u, g))
                        op = pe.matmul(bank[0][:], Wo[l][:, g, :], Os[:, g, :], start=g == 0, stop=g == G - 1)
                    op.then_inc(*fps.up(u, "end"))
                if k == "A3":
                    pe.wait_ge(*nmT_s.at(u))
                    pe.matmul(bank[6][0:S2, :], x2r[:, 1, :], x1r, start=True, stop=False)
                    pe.matmul(bank[6][0:S2, :], ones[0:1, 0:S2], nmT3[:], start=False, stop=True).then_inc(*st.up(u, 0))
                    pe.wait_ge(*pt.at(u, 0))
                    pe.matmul(bank[0][:], ctxn[s][:], PT[0][:], start=True, stop=True)
                    pe.matmul(bank[3][:], ones[0:S2, 0:P], PT[0][:], start=True, stop=True).then_inc(*dps.up(u, 0))
                if k == "F0":
                    def down(c):
                        pe.wait_ge(*chkA.at(u, c))
                        pe.matmul(bank[6][:], f0_out[:, c, :], hb[c % 3], start=c == 0, stop=c == C0 - 1) \
                            .then_inc(*fps.up(u, c))
                    for c in range(C0):
                        if c >= 4:
                            pe.wait_ge(*chkA.at(u, c - 4))
                        pe.matmul(bank[c % 4][:], f0_in[:, c * P:(c + 1) * P], xf[s][:],
                                  start=True, stop=True).then_inc(*chk.up(u, c))
                        if c >= 2:
                            down(c - 2)
                    down(C0 - 2)
                    down(C0 - 1)
                    fps.counts[(u, "end")] = fps.counts[(u, C0 - 1)]
                if k in ("F1", "F2"):
                    E = router[k][2]
                    w = F1 if k == "F1" else F2
                    todo = [(e, i, o, m) for e in range(E) for i, (o, m) in enumerate(pieces(w))]
                    pe.wait_ge(*gT_s.at(u))

                    def broadcast(e):
                        if e:
                            pe.wait_ge(*xw_s.at(u, e - 1))
                        pe.matmul(bank[7][:], pick8[0:E, e, :], gT[s][0:E, :], start=True, stop=True).then_inc(*wbps.up(u, e))

                    def down(n):
                        e, i, o, m = todo[n]
                        pe.wait_ge(*chkV.at(u, n))
                        wd = m1_w2[0:m, e, i, :] if k == "F1" else m2_w3[0:m, e, i, :]
                        pe.matmul(bank[6][:], wd, hb[n % 3][0:m, :], start=n == 0, stop=n == len(todo) - 1) \
                            .then_inc(*fps.up(u, n))

                    broadcast(0)
                    for n, (e, i, o, m) in enumerate(todo):
                        if k == "F1":
                            wu, wg = m1_w1[:, e, o:o + m], m1_w3[:, e, o:o + m]
                        else:
                            wu, wg = m2_w1[:, e * F2 + o:e * F2 + o + m], m2_w2[:, e * F2 + o:e * F2 + o + m]
                        if n >= 2:
                            pe.wait_ge(*chkV.at(u, n - 2))
                        if i == 1 and e + 1 < E:
                            broadcast(e + 1)
                        pe.matmul(bank[2 * (n % 2)][0:m, :], wu, xf[s][:], start=True, stop=True)
                        pe.wait_ge(*xw_s.at(u, e))
                        pe.matmul(bank[2 * (n % 2) + 1][0:m, :], wg, xw[e % 2], start=True, stop=True).then_inc(*chk.up(u, n))
                        if n >= 1:
                            down(n - 1)
                    down(len(todo) - 1)
                    fps.counts[(u, "end")] = fps.counts[(u, len(todo) - 1)]
                if k == "F3":
                    pe.wait_ge(*gT_s.at(u))
                    pe.matmul(bank[6][:], m3_b[:], gT[s][:], start=True, stop=False)
                    for e in range(MOE3 + 1):
                        if e < MOE3:
                            if e >= 2:
                                pe.wait_ge(*xw_s.at(u, e - 2))
                            pe.matmul((bank[7] if e % 2 else bank[0])[:], pick8[:, e, :], gT[s][:], start=True, stop=True) \
                                .then_inc(*wbps.up(u, e))
                        if e:
                            pe.wait_ge(*xw_s.at(u, e - 1))
                            pe.matmul(bank[6][:], m3_w[:, e - 1, :], xw[(e - 1) % 2], start=False, stop=e == MOE3) \
                                .then_inc(*fps.up(u, e - 1))
                    fps.counts[(u, "end")] = fps.counts[(u, MOE3 - 1)]
                pe.wait_ge(*(oT3 if k == "A3" else oT_s).at(u))
                for t in range(T):
                    op = pe.transpose(bank[1][:, t * P:(t + 1) * P], oT[:, t * P:(t + 1) * P], ident[:])
                op.then_inc(*ft.up(u))

            head(0)
            for u in range(UNITS):
                first(u)
                if u + 1 < UNITS:
                    head(u + 1)
                second(u)

    nc.all_engine_barrier(sems_to_clear=to_clear)


_INS = """x ctx_1024 mask_SxS2_bk0 mask_BxS2_ik0 mask_BxS2_if1 g_xattn g_ffn
L0_xattn_Wq L0_xattn_bq L0_xattn_Wk L0_xattn_bk L0_xattn_Wv L0_xattn_bv L0_xattn_Wo L0_xattn_bo
L0_ffn_Win L0_ffn_bin_ L0_ffn_W1 L0_ffn_b1 L0_ffn_W2 L0_ffn_b2 L0_ffn_Wout L0_ffn_bout
L1_xattn_Wq L1_xattn_bq L1_xattn_Wk L1_xattn_bk L1_xattn_Wv L1_xattn_bv L1_xattn_Wo L1_xattn_bo
L1_xattn_w1 L1_xattn_b1 L1_xattn_w2 L1_xattn_b2 L1_xattn_w3 L1_xattn_b3
L1_ffn_router_w L1_ffn_router_b L1_ffn_w1 L1_ffn_w3 L1_ffn_w2
L2_xattn_Wq L2_xattn_bq L2_xattn_Wk L2_xattn_bk L2_xattn_Wv L2_xattn_bv L2_xattn_Wo L2_xattn_bo
L2_ffn_gate_w L2_ffn_rms_w L2_ffn_W1 L2_ffn_W2 L2_ffn_W3
L3_xattn_W L3_xattn_diagonal L3_ffn_W_experts L3_ffn_b_experts L3_ffn_W_router L3_ffn_b_router""".split()


def kernel(**inputs):
    import numpy as _np
    import concourse.bacc as _bacc
    from concourse import mybir as _mybir
    from concourse.bass_utils import run_bass_kernel_spmd as _run

    def program(seen, counts):
        nc = _bacc.Bacc("TRN2", target_bir_lowering=False, num_devices=1)
        arrays, args = {}, {}
        for name in _INS:
            arr = _np.ascontiguousarray(inputs[name])
            arrays[f"in_{name}_dram"] = arr
            args[name] = nc.dram_tensor(f"in_{name}_dram", arr.shape, _mybir.dt.from_np(arr.dtype),
                                        kind="ExternalInput").ap()
        out = nc.dram_tensor("out_0_dram", (B, N, P), _mybir.dt.float32, kind="ExternalOutput").ap()
        build(nc, args, out, seen, counts)
        return nc, arrays

    counts = {}
    program({}, counts)
    nc, arrays = program(counts, {})
    r = _run(nc, [arrays], core_ids=[0])
    return r.results[0]["out_0_dram"]
```

```python
import math
from contextlib import ExitStack

import concourse.bass as bass
from concourse import mybir

F32 = mybir.dt.float32
F32R = mybir.dt.float32r
BF16 = mybir.dt.bfloat16
ALU = mybir.AluOpType
ACT = mybir.ActivationFunctionType
AX = mybir.AxisListType

P = 128
T = 4
N = P * T
B = 4
STREAMS = 2
S2 = 77
H = 16
HD = 8
G = 4
J = H // G
ROOT = float(HD) ** -0.5
OFF = float(2.0 ** 100)
PAD = -3.0e38
LOG_T_MIN, LOG_T_MAX = math.log(0.1), math.log(10.0)
LN_EPS = 1e-5
RMS_EPS = 1e-6
LAYERS = 4
UNITS = 2 * LAYERS * STREAMS

MOE1 = 4
F1 = 512
MOE2 = 8
F2 = 352
MOE3 = 8
EMAX = 8
QK = 96
LG = 16
M0, I0 = 64, 16
C0 = M0 * I0 // P


def kind(u):
    return "AF"[(u // STREAMS) % 2] + str(u // STREAMS // 2)


def pieces(width):
    return [(o, min(P, width - o)) for o in range(0, width, P)]


class Signal:

    def __init__(self, sem, seen, counts, name):
        self.sem, self.counts = sem, counts.setdefault(name, {})
        self.seen, self.total = seen.get(name, {}), 0

    def up(self, *key, by=1):
        self.total += by
        self.counts[key] = self.total
        return (self.sem, by)

    def at(self, *key):
        return (self.sem, self.seen[key] if self.seen else 1)


def build(nc, a, out, seen, counts):
    with ExitStack() as ctx:
        sems = []

        def sb(name, shape, dt=F32):
            return ctx.enter_context(nc.sbuf_tensor(name, shape, dt))

        def sig(name):
            s = ctx.enter_context(nc.semaphore(name))
            sems.append(s)
            return Signal(s, seen, counts, name)

        bank = [ctx.enter_context(nc.psum_tensor(f"bank{i}", [P, 512], F32)) for i in range(8)]

        ident = sb("ident", [P, P])
        identb = sb("identb", [P, P], BF16)
        pick1 = sb("pick1", [2 * MOE1, MOE1], F32R)
        pick2 = sb("pick2", [2 * MOE2, MOE2], F32R)
        quad = sb("quad", [P, 4, J])
        hmask = sb("hmask", [P, J])
        ones = sb("ones", [P, P])
        ones_r = sb("ones_r", [2, P], F32R)
        onesb = sb("onesb", [1, P], BF16)
        minus_half = sb("minus_half", [P, T])
        gates_col = sb("gates_col", [P, 2, LAYERS])
        graw = sb("graw", [P, 2, LAYERS])

        WqR = [sb(f"WqR{l}", [P, G, 4 * 32]) for l in range(3)]
        WkR = [sb(f"WkR{l}", [P, G, 4 * 32]) for l in range(3)]
        Wv = [sb(f"Wv{l}", [P, P]) for l in range(3)]
        Wo = [sb(f"Wo{l}", [P, P]) for l in range(3)]
        bv = sb("bv", [1, 3, P])
        bo = sb("bo", [2, 3, P], F32R)
        bcol = sb("bcol", [P, 3, 2, G])
        W3x = sb("W3x", [P, P])
        diag = sb("diag", [P, 1])
        t_w1b = sb("t_w1b", [P, 3, 64])
        t_w1T = sb("t_w1T", [3, 64])
        t_b1 = sb("t_b1", [64, 1])
        t_b2 = sb("t_b2", [64, 1])
        t_w2T = sb("t_w2T", [64, 64])
        t_w3 = sb("t_w3", [64, 1])
        t_b3 = sb("t_b3", [S2, 1])
        f0_in = sb("f0_in", [P, M0 * I0])
        f0_out = sb("f0_out", [P, C0, P])
        f0_cols = sb("f0_cols", [P, 3, C0])
        f0_bias = sb("f0_bias", [P, 1])
        m1_router = sb("m1_router", [P, MOE1])
        m1_rb = sb("m1_rb", [1, MOE1])
        m1_w1 = sb("m1_w1", [P, MOE1, F1])
        m1_w3 = sb("m1_w3", [P, MOE1, F1])
        m1_w2 = sb("m1_w2", [P, MOE1, F1 // P, P])
        m2_router = sb("m2_router", [P, MOE2])
        m2_rms = sb("m2_rms", [P, 1])
        m2_w1 = sb("m2_w1", [P, MOE2 * F2])
        m2_w2 = sb("m2_w2", [P, MOE2 * F2])
        m2_w3 = sb("m2_w3", [P, MOE2, 3, P])
        m3_router = sb("m3_router", [P, MOE3])
        m3_rb = sb("m3_rb", [1, MOE3])
        m3_w = sb("m3_w", [P, MOE3, P])
        m3_b = sb("m3_b", [2 * MOE3, P])
        mask_q = sb("mask_q", [P, T, S2], BF16)
        mask_k = sb("mask_k", [S2, N], BF16)

        KT = [sb(f"KT{s}", [QK + H, H, S2], F32R) for s in range(STREAMS)]
        VP = [sb(f"VP{s}", [S2, H, 32]) for s in range(STREAMS)]
        VM = [sb(f"VM{s}", [S2, H, 32]) for s in range(STREAMS)]
        lg = [sb(f"lg{s}", [P, T, LG]) for s in range(STREAMS)]
        pk = sb("pk", [P, G])
        ctxn = [sb(f"ctxn{s}", [S2, P + 1]) for s in range(STREAMS)]

        with ExitStack() as pro:
            def tmp(name, shape, dt=F32):
                return pro.enter_context(nc.sbuf_tensor(name, shape, dt))

            nat1 = [tmp(f"nat1{i}", [P, P]) for i in range(3)]
            Wq = [tmp(f"Wq{l}", [P, P]) for l in range(3)]
            Wk = [tmp(f"Wk{l}", [P, P]) for l in range(3)]
            nat_in = tmp("nat_in", [P, M0])
            natwo = tmp("natwo", [P, P])
            brow = tmp("brow", [1, 2, 3, P])
            bo_f = tmp("bo_f", [2, 3, P])
            bo_p = tmp("bo_p", [2, 2, 3, P])
            nat3x = tmp("nat3x", [P, P])
            nat_t1 = tmp("nat_t1", [64, 3])
            nat_t2 = tmp("nat_t2", [64, 64])
            NCH = MOE2 * F2 // P
            nat_m1 = tmp("nat_m1", [P, NCH, P])
            nat_m2 = tmp("nat_m2", [P, NCH, P])
            nat_m3 = tmp("nat_m3", [P, MOE2, F2])
            nat_e = tmp("nat_e", [P, MOE3, P])
            nat_r = tmp("nat_r", [MOE2, 2, P])
            nat_f0 = tmp("nat_f0", [C0, 4, P])
            nat_bin = tmp("nat_bin", [C0, M0 // C0])
            f0_wout = tmp("f0_wout", [M0, P])
            f0_b2 = tmp("f0_b2", [M0, 1])
            f0_bout = tmp("f0_bout", [P, 1])
            m8 = tmp("m8", [P, T, S2], mybir.dt.uint8)
            mf = tmp("mf", [P, T, S2])
            quad_b = tmp("quad_b", [P, 4, J])

            landed = {n: sig("landed_" + n) for n in ("small", "gates", "turn", "m2", "rest", "mask")}
            zeroed = sig("zeroed")
            const = sig("const")
            turned = sig("turned")
            keptA, keptD = sig("kept_act"), sig("kept_dve")
            folded = sig("folded")

            groups = []

            def grouped(load, items):
                row, width = [], 0
                for src, dst in items:
                    k = src.shape[0]
                    if row and (width + k > 512):
                        groups.append((load, row))
                        row, width = [], 0
                    row.append((src, dst, width))
                    width += k
                groups.append((load, row))

            grouped("turn", [(nat1[0][:], Wq[1][:]), (nat1[1][:], Wk[1][:]), (nat1[2][:], Wv[1][:]), (nat3x[:], W3x[:])])
            grouped("turn", [(natwo[:], Wo[1][:])])
            grouped("turn", [(nat_t1[:], t_w1T[:]), (nat_t2[:], t_w2T[:]), (nat_r[:, 0, :], m2_router[:]),
                             (nat_r[:, 1, :], m3_router[:]), (nat_f0[:, 0, :], f0_cols[:, 0, :]),
                             (nat_f0[:, 3, :], f0_cols[:, 1, :]), (nat_f0[:, 2, :], f0_cols[:, 2, :])])
            grouped("mask", [(mf[:, t, :], mask_k[:, t * P:(t + 1) * P]) for t in range(T)])
            grouped("m2", [(nat_e[:, e, :], m3_w[:, e, :]) for e in range(MOE3)])
            for nat, w in ((nat_m1, m2_w1), (nat_m2, m2_w2)):
                grouped("m2", [(nat[:, c, :], w[:, c * P:(c + 1) * P]) for c in range(NCH)])
            grouped("m2", [(nat_m3[:, e, o:o + w], m2_w3[0:w, e, i, :]) for e in range(MOE2)
                           for i, (o, w) in enumerate(pieces(F2))])

            block = pro.enter_context(nc.Block())

            @block.sync
            def _(sp):
                for l in (0, 2):
                    for n, w in (("Wq", Wq), ("Wk", Wk), ("Wv", Wv), ("Wo", Wo)):
                        sp.dma_start(w[l][:], a[f"L{l}_xattn_{n}"]).then_inc(*landed["small"].up(by=16))
                for l in range(3):
                    for n, row in (("bq", brow[0:1, 0, l, :]), ("bk", brow[0:1, 1, l, :]),
                                   ("bv", bv[0:1, l, :]), ("bo", bo_f[0:1, l, :]), ("bo", bo_f[1:2, l, :])):
                        sp.dma_start(row, a[f"L{l}_xattn_{n}"].rearrange("(o n) -> o n", o=1)) \
                            .then_inc(*landed["small"].up(by=16))
                for src, dst in ((a["L3_xattn_diagonal"], diag), (a["L1_xattn_b1"], t_b1), (a["L1_xattn_b2"], t_b2),
                                 (a["L0_ffn_b2"], f0_b2), (a["L0_ffn_bout"], f0_bout), (a["L2_ffn_rms_w"], m2_rms)):
                    sp.dma_start(dst[:], src.rearrange("(n o) -> n o", o=1)).then_inc(*landed["small"].up(by=16))
                sp.dma_start(t_w3[:], a["L1_xattn_w3"].rearrange("o n -> n o")).then_inc(*landed["small"].up(by=16))
                sp.dma_start(t_b3[:], a["L1_xattn_b3"].partition_broadcast(S2)).then_inc(*landed["small"].up(by=16))
                sp.dma_start(nat_in[:], a["L0_ffn_Win"]).then_inc(*landed["small"].up(by=16))
                sp.dma_start(f0_wout[:], a["L0_ffn_Wout"]).then_inc(*landed["small"].up(by=16))
                for c in range(C0):
                    sp.dma_start(f0_out[:, c, :],
                                 a["L0_ffn_Wout"][c * 8:c * 8 + 8, :].unsqueeze(1).to_broadcast([8, I0, P])) \
                        .then_inc(*landed["small"].up(by=16))
                sp.dma_start(m1_router[:], a["L1_ffn_router_w"]).then_inc(*landed["small"].up(by=16))
                sp.dma_start(m1_rb[:], a["L1_ffn_router_b"].rearrange("(o n) -> o n", o=1)).then_inc(*landed["small"].up(by=16))
                sp.dma_start(m3_rb[:], a["L3_ffn_b_router"].rearrange("(o n) -> o n", o=1)).then_inc(*landed["small"].up(by=16))
                sp.dma_start(m3_b[0:MOE3, :], a["L3_ffn_b_experts"]).then_inc(*landed["small"].up(by=16))
                sp.dma_start(m3_b[MOE3:2 * MOE3, :], a["L3_ffn_b_experts"]).then_inc(*landed["small"].up("all", by=16))
                sp.dma_start(m1_w1[:], a["L1_ffn_w1"].rearrange("e d f -> d e f")).then_inc(*landed["rest"].up(by=16))
                sp.dma_start(m1_w3[:], a["L1_ffn_w3"].rearrange("e d f -> d e f")).then_inc(*landed["rest"].up(by=16))
                sp.dma_start(m1_w2[:], a["L1_ffn_w2"].rearrange("e (c p) d -> p e c d", p=P)) \
                    .then_inc(*landed["rest"].up("all", by=16))
                for name in ("small", "rest", "gates"):
                    sp.wait_ge(*landed[name].at("all"))

            @block.scalar
            def _(act):
                act.dma_start(graw[:, 0, :], a["g_xattn"].partition_broadcast(P)).then_inc(*landed["gates"].up(by=16))
                act.dma_start(graw[:, 1, :], a["g_ffn"].partition_broadcast(P)).then_inc(*landed["gates"].up("all", by=16))
                act.dma_start(m8[:], a["mask_SxS2_bk0"].rearrange("(p t) k -> p t k", t=T)) \
                    .then_inc(*landed["mask"].up("all", by=16))
                for i, n in enumerate(("Wq", "Wk", "Wv")):
                    act.dma_start(nat1[i][:], a[f"L1_xattn_{n}"]).then_inc(*landed["turn"].up(by=16))
                act.dma_start(nat3x[:], a["L3_xattn_W"]).then_inc(*landed["turn"].up(by=16))
                act.dma_start(natwo[:], a["L1_xattn_Wo"]).then_inc(*landed["turn"].up(by=16))
                act.dma_start(nat_t1[:], a["L1_xattn_w1"]).then_inc(*landed["turn"].up(by=16))
                act.dma_start(nat_t2[:], a["L1_xattn_w2"]).then_inc(*landed["turn"].up(by=16))
                act.dma_start(nat_r[:, 0, :], a["L2_ffn_gate_w"]).then_inc(*landed["turn"].up(by=16))
                act.dma_start(nat_r[:, 1, :], a["L3_ffn_W_router"]).then_inc(*landed["turn"].up(by=16))
                for i, n in enumerate(("W1", "b1", "W2")):
                    act.dma_start(nat_f0[:, i, :], a[f"L0_ffn_{n}"].rearrange("(c m) i -> c (m i)", c=C0)) \
                        .then_inc(*landed["turn"].up(by=16))
                act.dma_start(nat_bin[:], a["L0_ffn_bin_"].rearrange("(c m) -> c m", c=C0)) \
                    .then_inc(*landed["turn"].up("all", by=16))
                act.dma_start(nat_e[:], a["L3_ffn_W_experts"].rearrange("e o i -> o e i")).then_inc(*landed["m2"].up(by=16))
                act.dma_start(nat_m1[:], a["L2_ffn_W1"].rearrange("e n d -> (e n) d").rearrange("(c p) d -> p c d", p=P)) \
                    .then_inc(*landed["m2"].up(by=16))
                act.dma_start(nat_m2[:], a["L2_ffn_W2"].rearrange("e n d -> (e n) d").rearrange("(c p) d -> p c d", p=P)) \
                    .then_inc(*landed["m2"].up(by=16))
                act.dma_start(nat_m3[:], a["L2_ffn_W3"].rearrange("e m n -> m e n")).then_inc(*landed["m2"].up("all", by=16))
                act.wait_ge(*landed["gates"].at("all"))
                act.activation(gates_col[:], graw[:], ACT.Tanh)
                for i, (_, row) in enumerate(groups):
                    if i % 2:
                        act.wait_ge(*turned.at(i))
                        for n, (src, dst, at) in enumerate(row):
                            k, m = src.shape
                            op = act.activation(dst, bank[i % 8][0:m, at:at + k], ACT.Copy)
                        op.then_inc(*keptA.up(i))

            @block.gpsimd
            def _(pool):
                pool.memset(ident[:], 0.0)
                pool.memset(ones[:], 1.0)
                pool.memset(quad[:], 1.0)
                pool.memset(minus_half[:], -0.5)
                pool.memset(onesb[:], 1.0).then_inc(*zeroed.up("all"))
                pool.wait_ge(*zeroed.at("all"))
                pool.affine_select(out=ident[:], in_=ident[:], compare_op=ALU.not_equal, fill=1.0, base=0,
                                   pattern=[[-1, P]], channel_multiplier=1).then_inc(*const.up("ident"))
                pool.affine_select(out=quad_b[:], in_=quad[:], compare_op=ALU.is_ge, fill=0.0, base=0,
                                   pattern=[[-32, 4], [-HD, J]], channel_multiplier=1).then_inc(*const.up("quad_low"))
                pool.wait_ge(*const.at("quad_low"))
                pool.affine_select(out=quad[:], in_=quad_b[:], compare_op=ALU.is_ge, fill=0.0, base=HD - 1,
                                   pattern=[[32, 4], [HD, J]], channel_multiplier=-1).then_inc(*const.up("quad"))
                for s in range(STREAMS):
                    pool.memset(lg[s][:], PAD)
                    pool.memset(ctxn[s][:, P:P + 1], 1.0)
                    pool.memset(VM[s][:], 0.0)
                    pool.memset(VP[s][:], 0.0).then_inc(*zeroed.up("values", s))
                    pool.wait_ge(*zeroed.at("values", s))
                    pool.memset(VP[s][:, :, HD:HD + 1], 1.0)
                pool.memset(pk[:], 0.0).then_inc(*zeroed.up("last"))
                pool.wait_ge(*zeroed.at("last"))
                for s in range(STREAMS):
                    pool.tensor_copy(KT[s][QK:QK + H, :, :], ident[QK:QK + H, QK:QK + H].unsqueeze(2).to_broadcast([H, H, S2])) \
                        .then_inc(*zeroed.up("heads", s))
                    pool.wait_ge(*zeroed.at("heads", s))

            @block.vector
            def _(dve):
                dve.wait_ge(*zeroed.at("all"))
                dve.wait_ge(*landed["mask"].at("all"))
                dve.tensor_copy(mf[:], m8[:]).then_inc(*folded.up("mask8"))
                dve.wait_ge(*folded.at("mask8"))
                dve.tensor_scalar(mf[:], mf[:], -1.0, OFF, ALU.add, ALU.mult).then_inc(*folded.up("mask"))
                dve.wait_ge(*folded.at("mask"))
                dve.tensor_copy(mask_q[:], mf[:])
                dve.wait_ge(*landed["turn"].at("all"))
                dve.tensor_tensor(nat_f0[:, 3, :].rearrange("c (m i) -> c m i", i=I0),
                                  nat_f0[:, 0, :].rearrange("c (m i) -> c m i", i=I0),
                                  nat_bin[:].unsqueeze(2).to_broadcast([C0, M0 // C0, I0]), ALU.mult) \
                    .then_inc(*folded.up("binw"))
                dve.wait_ge(*folded.at("binw"))
                dve.tensor_tensor(nat_f0[:, 3, :], nat_f0[:, 3, :], nat_f0[:, 1, :], ALU.add).then_inc(*folded.up("b1"))
                dve.wait_ge(*const.at("ident"))
                dve.tensor_copy(identb[:], ident[:])
                dve.tensor_copy(ones_r[:], ones[0:2, :])
                for pick, e in ((pick1, MOE1), (pick2, MOE2)):
                    dve.tensor_tensor(pick[:], ident[0:2 * e, 0:e], ident[0:2 * e, e:2 * e], ALU.add)
                dve.wait_ge(*const.at("quad"))
                dve.tensor_reduce(hmask[:], quad[:].rearrange("p q j -> p j q"), AX.X, ALU.add)
                for i, (_, row) in enumerate(groups):
                    if i % 2 == 0:
                        dve.wait_ge(*turned.at(i))
                        for n, (src, dst, at) in enumerate(row):
                            k, m = src.shape
                            op = dve.tensor_copy(dst, bank[i % 8][0:m, at:at + k])
                        op.then_inc(*keptD.up(i))
                dve.wait_ge(*landed["small"].at("all"))
                dve.wait_ge(*keptD.at(2))
                for l in range(3):
                    for wide, w in ((WqR, Wq), (WkR, Wk)):
                        dve.tensor_copy(wide[l][:].rearrange("p g (q c) -> p g q c", c=32),
                                        w[l][:].rearrange("p (g c) -> p g c", c=32).unsqueeze(2).to_broadcast([P, G, 4, 32]))
                dve.tensor_copy(bo_p[:, 0].bitcast(F32R), bo_f[:]).then_inc(*folded.up("bo_high"))
                dve.wait_ge(*folded.at("bo_high"))
                dve.tensor_tensor(bo_p[:, 1], bo_f[:], bo_p[:, 0], ALU.subtract)
                dve.tensor_scalar(bo_p[:, 0], bo_p[:, 0], ident[0:2, 0:1], None, ALU.mult).then_inc(*folded.up("bo_low"))
                dve.wait_ge(*folded.at("bo_low"))
                dve.scalar_tensor_tensor(out=bo[:], in0=bo_p[:, 1], scalar=ident[0:2, 1:2], in1=bo_p[:, 0],
                                         op0=ALU.mult, op1=ALU.add)
                dve.tensor_copy(f0_in[:].rearrange("p (m i) -> p m i", i=I0), nat_in[:].unsqueeze(2).to_broadcast([P, M0, I0]))
                for c in range(C0):
                    dve.tensor_scalar(f0_out[:, c, :], f0_out[:, c, :], f0_cols[:, 2, c:c + 1], None, ALU.mult)
                dve.wait_ge(*turned.at("columns"))
                dve.tensor_copy(bcol[:], bank[0][:, 0:24].rearrange("p (l i g) -> p l i g", l=3, i=2))
                dve.tensor_tensor(f0_bias[:], bank[0][:, 24:25], f0_bout[:], ALU.add)
                for f, s in enumerate((ROOT / (N * S2), -ROOT / N, 1.0 / (N * (S2 - 1)))):
                    dve.tensor_scalar(t_w1b[:, f, :], bank[1][:, f * 64:(f + 1) * 64], s, None, ALU.mult)

            @block.tensor
            def _(pe):
                pe.wait_ge(*const.at("ident"))
                for i, (load, row) in enumerate(groups):
                    pe.wait_ge(*landed[load].at("all"))
                    if i == 2:
                        pe.wait_ge(*folded.at("b1"))
                    if load == "mask":
                        pe.wait_ge(*folded.at("mask"))
                    if i >= 8:
                        pe.wait_ge(*(keptA if i % 2 else keptD).at(i - 8))
                    for src, dst, at in row:
                        k, m = src.shape
                        op = pe.transpose(bank[i % 8][0:m, at:at + k], src, ident[0:k, 0:k])
                    op.then_inc(*turned.up(i))
                last = len(groups) - 1
                for i in range(max(0, last - 7), last + 1):
                    pe.wait_ge(*(keptA if i % 2 else keptD).at(i))
                pe.wait_ge(*landed["small"].at("all"))
                for l in range(3):
                    for i in range(2):
                        for g in range(G):
                            c = (l * 2 + i) * G + g
                            for q in range(4):
                                pe.matmul(bank[0][32 * q:32 * q + 32, c:c + 1], brow[0:1, i, l, 32 * g:32 * g + 32],
                                          ones[0:1, 0:1], start=True, stop=True, tile_position=(0, 32 * q))
                pe.matmul(bank[0][:, 24:25], f0_wout[:], f0_b2[:], start=True, stop=True)
                for f in range(3):
                    op = pe.matmul(bank[1][:, f * 64:(f + 1) * 64], ident[0:3, f:f + 1].to_broadcast([3, P]), t_w1T[:], start=True, stop=True)
                op.then_inc(*turned.up("columns"))

        main(nc, a, out, dict(locals()))


def main(nc, a, out, v):
    ctx, sb, sig, bank = v["ctx"], v["sb"], v["sig"], v["bank"]
    ident, identb = v["ident"], v["identb"]
    quad, hmask, ones, onesb, minus_half, gates_col = (v[n] for n in (
        "quad", "hmask", "ones", "onesb", "minus_half", "gates_col"))
    WqR, WkR, Wv, Wo, bv, bo, ones_r, bcol, W3x, diag = (v[n] for n in (
        "WqR", "WkR", "Wv", "Wo", "bv", "bo", "ones_r", "bcol", "W3x", "diag"))
    t_w1b, t_b1, t_b2, t_w2T, t_w3, t_b3 = (v[n] for n in ("t_w1b", "t_b1", "t_b2", "t_w2T", "t_w3", "t_b3"))
    f0_in, f0_out, f0_cols, f0_bias = (v[n] for n in ("f0_in", "f0_out", "f0_cols", "f0_bias"))
    mask_q, mask_k = v["mask_q"], v["mask_k"]
    router = {"F1": (v["m1_router"], v["m1_rb"], MOE1), "F2": (v["m2_router"], None, MOE2),
              "F3": (v["m3_router"], v["m3_rb"], MOE3)}
    KT, VP, VM, lg, pk = (v[n] for n in ("KT", "VP", "VM", "lg", "pk"))
    pick = {"F1": v["pick1"], "F2": v["pick2"], "F3": v["pick2"]}
    m1_w1, m1_w3, m1_w2, m2_w1, m2_w2, m2_w3, m2_rms, m3_w, m3_b = (v[n] for n in (
        "m1_w1", "m1_w3", "m1_w2", "m2_w1", "m2_w2", "m2_w3", "m2_rms", "m3_w", "m3_b"))

    def two(name, shape, dt=F32):
        return [sb(f"{name}{s}", shape, dt) for s in range(STREAMS)]

    x = two("x", [P, T, P])
    ctxn = v["ctxn"]
    ctxT = two("ctxT", [P, S2])
    xf = two("xf", [P, N])
    stats = two("stats", [P, T, 6])
    mv = two("mv", [P, T, 2])
    rstd = two("rstd", [P, 4, T])
    Qs = two("Qs", [QK + H, G, N], F32R)
    nm = two("nm", [P, T, H])
    mk_i = two("mk_i", [S2, 2], mybir.dt.int32)
    mr_i = two("mr_i", [1, 2, S2], mybir.dt.int32)
    mk = two("mk", [S2, 4])
    mr_f = two("mr_f", [1, 2, S2])
    mr = two("mr", [1, 2, S2], BF16)
    ksum = two("ksum", [P, G])
    top = two("top", [P, T, 8])
    rep = two("rep", [P, T, LG])
    gw = two("gw", [P, T, EMAX])
    gp = two("gp", [P, T, 2 * EMAX])
    gs = two("gs", [P, 2, T])
    gT = two("gT", [2 * EMAX, N], F32R)
    x2r = two("x2r", [P, 2, S2])
    nm3 = two("nm3", [P, T])
    nmT3 = two("nmT3", [1, N], F32R)
    xn = sb("xn", [P, T, P])
    Ksp = sb("Ksp", [P, G, S2])
    qsum = sb("qsum", [P, G])
    NPT = 6
    PT = [sb(f"PT{i}", [S2, N]) for i in range(NPT)]
    Os = sb("Os", [P, 2, N])
    x1r = [Os[:, s, :] for s in range(STREAMS)]
    rden = sb("rden", [P, G, T, J])
    att = sb("att", [P, T, P])
    attT = sb("attT", [P, N])
    oT = sb("oT", [P, N])
    hb = [sb(f"hb{i}", [P, N]) for i in range(3)]
    xw = [sb(f"xw{i}", [P, N]) for i in range(2)]
    Eb = sb("Eb", [P, 3, J * S2])
    Eq = sb("Eq", [P, 3, J * S2])
    Z = sb("Z", [P, 2, T, H])
    nms = sb("nms", [P, T, H])
    feat = sb("feat", [P, 3, H])
    zt = sb("zt", [P, 2, T, H])
    hid = sb("hid", [64, 2, H])
    invt = sb("invt", [S2, 3, H])

    in_x, in_ctx, in_mask = ([sig(f"{n}{i}") for i in range(STREAMS)] for n in ("in_x", "in_ctx", "in_mask"))
    (ctx_ps, ctx_t, stat_s, mv_s, rs_s, xn_s, xT_ps, xf_s, done_x, kps, ksp, klo, kt_s, vps, vp_s, msk,
     qps, qhi, qlo, sps, nm_s, nmps, nmT_s, esub, eexp, esq, temp, tps, tact, st, pt, ops, os_s, tops, norm, aps,
     at_s, lps, lg_s, less, ge, gps, gT_s, wbps, xw_s, chk, chkA, chkV, fps, oT_s, ft, x2_s, x3_s, stored) = (
        sig(n) for n in (
            "ctx_ps ctx_t stat_s mv_s rs_s xn_s xT_ps xf_s done_x kps ksp klo kt_s vps vp_s msk "
            "qps qhi qlo sps nm_s nmps nmT_s esub eexp esq temp tps tact st pt ops os_s tops norm aps "
            "at_s lps lg_s less ge gps gT_s wbps xw_s chk chkA chkV fps oT_s ft x2_s x3_s stored").split())
    mine = sorted(s.num for s in (in_x[0].sem, stored.sem))
    to_clear = range(mine[0], mine[1] + 1)

    xv = a["x"].rearrange("(i s) (p t) d -> i s p t d", s=STREAMS, t=T)
    ov = out.rearrange("(i s) (p t) d -> i s p t d", s=STREAMS, t=T)
    cv = a["ctx_1024"].rearrange("(i s) k d -> i s k d", s=STREAMS)
    ik = a["mask_BxS2_ik0"].rearrange("(i s) k -> i s k", s=STREAMS)
    jf = a["mask_BxS2_if1"].rearrange("(i s) k -> i s k", s=STREAMS)

    MHA = ("A0", "A1", "A2")
    NS = T * G
    chunks = {"F1": [(e, i, o, m) for e in range(MOE1) for i, (o, m) in enumerate(pieces(F1))],
              "F2": [(e, i, o, m) for e in range(MOE2) for i, (o, m) in enumerate(pieces(F2))]}

    Q0 = 5
    S0 = Q0 + G
    S1 = S0 + NS
    RING = (1, 0, 4)

    def steps_pre(k):
        if k in MHA:
            return S1 + (13 if k == "A1" else 3)
        return 5 if k == "F0" else 11

    def steps_main(k):
        return {"A": H + 4, "F": 0}[k[0]] if k in MHA else {"A3": 3, "F0": C0 + 4, "F3": MOE3 + 3}.get(k) or len(chunks[k]) + 3

    def run(pre, body):
        for _ in pre(0):
            pass
        for u in range(UNITS):
            main_part = body(u)
            nxt = pre(u + 1) if u + 1 < UNITS else iter(())
            n, m = steps_main(kind(u)), steps_pre(kind(u + 1)) if u + 1 < UNITS else 0
            sent = 0
            for i in range(n):
                next(main_part)
                while sent < m and (sent + 1) * n <= (i + 1) * m:
                    next(nxt)
                    sent += 1
            assert sent == m and next(main_part, None) is None and next(nxt, None) is None

    it = ctx.enter_context(nc.Fori(0, B // STREAMS))
    with nc.Block() as block:

        @block.sync
        def _(sp):
            for s in range(STREAMS):
                sp.dma_start(x[s][:], xv[it, s]).then_inc(*in_x[s].up("all", by=16))
                sp.dma_start(ctxn[s][:, 0:P], cv[it, s]).then_inc(*in_ctx[s].up("all", by=16))
                for i, m in enumerate((ik, jf)):
                    sp.dma_start(mk_i[s][:, i:i + 1], m[it, s].rearrange("(k o) -> k o", o=1)).then_inc(*in_mask[s].up(i, 0, by=16))
                    sp.dma_start(mr_i[s][:, i, :], m[it, s].rearrange("(o k) -> o k", o=1)).then_inc(*in_mask[s].up(i, 1, by=16))
            for s in range(STREAMS):
                sp.wait_ge(*done_x.at(UNITS - STREAMS + s))
                sp.dma_start(ov[it, s], x[s][:]).then_inc(*stored.up(s, by=16))
            sp.wait_ge(*stored.at(STREAMS - 1))

        @block.gpsimd
        def _(pool):
            def pre(u):
                s, k = u % STREAMS, kind(u)
                pool.wait_ge(*mv_s.at(u))
                pool.tensor_scalar_add(rstd[s][:, 0, :], mv[s][:, :, 1], LN_EPS).then_inc(*rs_s.up(u, "eps"))
                pool.wait_ge(*rs_s.at(u, "eps"))
                pool.tensor_tensor(rstd[s][:, 1, :], rstd[s][:, 0, :], minus_half[:], ALU.pow).then_inc(*rs_s.up(u))
                if k == "F2":
                    pool.wait_ge(*rs_s.at(u))
                    pool.tensor_tensor(rstd[s][:, 2, :], rstd[s][:, 1, :], rstd[s][:, 1, :], ALU.mult).then_inc(*rs_s.up(u, "sq"))
                    pool.wait_ge(*rs_s.at(u, "sq"))
                    pool.tensor_tensor(rstd[s][:, 2, :], rstd[s][:, 2, :], mv[s][:, :, 1], ALU.mult).then_inc(*rs_s.up(u, "ms"))
                    pool.wait_ge(*rs_s.at(u, "ms"))
                    pool.tensor_scalar_add(rstd[s][:, 2, :], rstd[s][:, 2, :], RMS_EPS).then_inc(*rs_s.up(u, "ms_eps"))
                    pool.wait_ge(*rs_s.at(u, "ms_eps"))
                    pool.tensor_tensor(rstd[s][:, 3, :], rstd[s][:, 2, :], minus_half[:], ALU.pow).then_inc(*rs_s.up(u, "rms"))
                for i in range(steps_pre(k)):
                    if k == "A1" and S0 + 3 <= i < S1 + 3:
                        n = i - S0 - 3
                        pool.wait_ge(*eexp.at(u, n))
                        if n >= 3:
                            pool.wait_ge(*temp.at(u, "sums", n - 3))
                        pool.tensor_tensor(Eq[:, n % 3, :], Eb[:, n % 3, :], Eb[:, n % 3, :], ALU.mult).then_inc(*esq.up(u, n))
                    yield

            def body(u):
                for _ in range(steps_main(kind(u))):
                    yield

            run(pre, body)

        @block.scalar
        def _(act):
            def pre(u):
                s, k = u % STREAMS, kind(u)
                l = int(k[1])

                def normalized():
                    act.wait_ge(*xT_ps.at(u, T - 1))
                    act.activation(xf[s][:], bank[4][:], ACT.Copy, scale=m2_rms[:, 0:1] if k == "F2" else 1.0) \
                        .then_inc(*xf_s.up(u))

                for i in range(steps_pre(k)):
                    if k in MHA:
                        if i == 1 and k == "A0":
                            act.wait_ge(*ctx_ps.at(s))
                            act.activation(ctxT[s][:], bank[1][:, 0:S2], ACT.Copy).then_inc(*ctx_t.up(s))
                        if i == 3:
                            if u >= 1 and kind(u - 1) == k:
                                act.wait_ge(*kt_s.at(u - 1, J - 1))
                            act.wait_ge(*kps.at(u))
                            for g in range(G):
                                act.activation(Ksp[:, g, :].bitcast(F32R), bank[0][:, g * S2:(g + 1) * S2], ACT.Identity,
                                               bias=bcol[:, l, 1, g:g + 1],
                                               accum_out=ksum[s][:, g:g + 1] if l == 1 else None).then_inc(*ksp.up(u, g))
                            act.wait_ge(*vps.at(u))
                            act.activation(VP[s][:, :, 0:HD] if l != 2 else VM[s][:, :, 0:HD],
                                           bank[1][0:S2, 0:P].rearrange("p (h d) -> p h d", d=HD), ACT.Copy,
                                           scale=mk[s][:, 1:2] if l == 2 else 1.0).then_inc(*vp_s.up(u))
                        if i == 4:
                            normalized()
                        if Q0 < i <= Q0 + G:
                            g = i - Q0 - 1
                            act.wait_ge(*qps.at(u, g))
                            act.activation(Qs[s][0:QK, g, :], bank[RING[g % 3]][0:QK, :], ACT.Identity, bias=bcol[0:QK, l, 0, g:g + 1],
                                           accum_out=qsum[0:QK, g:g + 1] if l == 1 else None).then_inc(*qhi.up(u, g))
                        if l == 1 and S0 + 2 <= i < S1 + 2:
                            n = i - S0 - 2
                            t, g = n // G, n % G
                            act.wait_ge(*esub.at(u, n))
                            if n >= 3:
                                act.wait_ge(*temp.at(u, "sums", n - 3))
                            if n % 2:
                                op = act.activation(Eb[:, n % 3, :], Eb[:, n % 3, :], ACT.Exp, scale=ROOT)
                            for j in range(0 if n % 2 else J):
                                op = act.activation(Eb[:, n % 3, j * S2:(j + 1) * S2],
                                                    bank[RING[(G + n) % 3]][:, j * S2:(j + 1) * S2], ACT.Exp, scale=ROOT,
                                                    bias=nms[:, t, g * J + j:g * J + j + 1],
                                                    accum_out=Z[:, 0, t, g * J + j:g * J + j + 1])
                            op.then_inc(*eexp.up(u, n))
                        if i == S1 + 2:
                            act.wait_ge(*nmps.at(u))
                            for g in range(G):
                                act.activation(Qs[s][QK:QK + H, g, :], bank[4][QK:QK + H, :], ACT.Copy).then_inc(*nmT_s.up(u, g))
                        if i == S1 + 6:
                            act.wait_ge(*tps.at(u, 0))
                            act.activation(hid[:, 0, :], bank[0][0:64, 0:H], ACT.Gelu, bias=t_b1[:, 0:1]).then_inc(*tact.up(u, 0))
                        if i == S1 + 8:
                            act.wait_ge(*tps.at(u, 1))
                            act.activation(hid[:, 1, :], bank[1][0:64, 0:H], ACT.Gelu, bias=t_b2[:, 0:1]).then_inc(*tact.up(u, 1))
                        if i == S1 + 11:
                            act.wait_ge(*temp.at(u, "clip"))
                            act.activation(invt[:, 1, :], invt[:, 0, :], ACT.Exp, scale=-1.0).then_inc(*tact.up(u, 2))
                    elif i == 4:
                        normalized()
                        if k == "A3":
                            act.wait_ge(*qps.at(u, 1))
                            act.activation(x2r[s][:, 0, :], bank[1][:, 0:S2], ACT.Relu).then_inc(*x2_s.up(u))
                    elif k == "A3":
                        if i == 6:
                            act.wait_ge(*qps.at(u, 0))
                            act.activation(x1r[s], bank[0][:], ACT.Relu).then_inc(*qhi.up(u, 0))
                        if i == 10:
                            act.wait_ge(*nmps.at(u))
                            act.activation(nmT3[s][:], bank[4][0:1, :], ACT.Copy).then_inc(*nmT_s.up(u))
                    elif k in router:
                        E = router[k][2]
                        if i == 7:
                            act.wait_ge(*less.at(u))
                            act.activation(gw[s][:, :, 0:E], gw[s][:, :, 0:E], ACT.Exp).then_inc(*ge.up(u))
                        if i == 10:
                            act.wait_ge(*gps.at(u))
                            act.activation(gT[s][0:2 * E, :], bank[4][0:2 * E, :], ACT.Copy).then_inc(*gT_s.up(u))
                    yield

            def body(u):
                s, k = u % STREAMS, kind(u)
                l = int(k[1])
                if k in MHA:
                    def copy_out(g):
                        act.wait_ge(*ops.at(u, g))
                        if g >= 2:
                            act.wait_ge(*tops.at(u, g - 2))
                        act.activation(Os[:, g % 2, :], bank[6 + g % 2][:], ACT.Copy).then_inc(*os_s.up(u, g))
                    for h in range(H):
                        act.wait_ge(*st.at(u, h))
                        if h >= NPT:
                            act.wait_ge(*ops.at(u, (h - NPT) // J))
                        if l == 1:
                            act.wait_ge(*temp.at(u, "invt"))
                        act.activation(PT[h % NPT][:], bank[(2, 3, 5)[h % 3]][0:S2, :], ACT.Exp,
                                       scale=invt[:, 2, h:h + 1] if l == 1 else ROOT,
                                       bias=mk[s][:, 2:3] if l == 2 else 0.0).then_inc(*pt.up(u, h))
                        if h % J == 0 and h:
                            copy_out(h // J - 1)
                        yield
                    copy_out(G - 1)
                    yield
                    yield
                    act.wait_ge(*aps.at(u))
                    act.activation(attT[:], bank[6][:], ACT.Copy).then_inc(*at_s.up(u))
                    yield
                    yield
                    return
                if k == "A3":
                    act.wait_ge(*st.at(u, 0))
                    act.activation(PT[0][:], bank[2][0:S2, :], ACT.Exp, bias=mk[s][:, 3:4]).then_inc(*pt.up(u, 0))
                    yield
                    yield
                    yield
                    return
                if k == "F0":
                    for c in range(C0):
                        act.wait_ge(*chk.at(u, c))
                        if c >= 3:
                            act.wait_ge(*fps.at(u, c - 3))
                        act.activation(hb[c % 3][:], bank[(2, 3, 6)[c % 3]][:], ACT.Relu, scale=f0_cols[:, 0, c:c + 1],
                                       bias=f0_cols[:, 1, c:c + 1]).then_inc(*chkA.up(u, c))
                        yield
                    yield
                if k in chunks:
                    for n, (e, i, o, m) in enumerate(chunks[k]):
                        act.wait_ge(*chk.at(u, n, "up"))
                        if n >= 3:
                            act.wait_ge(*fps.at(u, n - 3))
                        act.activation(hb[n % 3][0:m, :], bank[(2, 3, 6)[2 * n % 3]][0:m, :], ACT.Silu).then_inc(*chkA.up(u, n))
                        yield
                if k == "F3":
                    for e in range(MOE3):
                        yield
                act.wait_ge(*fps.at(u, "end"))
                act.activation(oT[:], bank[5][:], ACT.Identity, bias=f0_bias[:, 0:1] if k == "F0" else 0.0) \
                    .then_inc(*oT_s.up(u))
                yield
                yield
                yield

            run(pre, body)

        @block.vector
        def _(dve):
            def pre(u):
                s, k = u % STREAMS, kind(u)
                l = int(k[1])

                def statistics():
                    if u < STREAMS:
                        dve.wait_ge(*in_x[s].at("all"))
                    else:
                        dve.wait_ge(*done_x.at(u - STREAMS))
                    for t in range(T):
                        dve.bn_stats(stats[s][:, t, :], x[s][:, t, :]).then_inc(*stat_s.up(u, t))
                    for t in range(T):
                        dve.wait_ge(*stat_s.at(u, t))
                        op = dve.bn_aggr(mv[s][:, t, :], stats[s][:, t, :])
                    op.then_inc(*mv_s.up(u))

                def masks():
                    dve.wait_ge(*in_mask[s].at(1, 1))
                    dve.tensor_copy(mk[s][:, 0:1], mk_i[s][:, 0:1])
                    dve.tensor_copy(mk[s][:, 3:4], mk_i[s][:, 1:2])
                    dve.tensor_copy(mr_f[s][:], mr_i[s][:]).then_inc(*msk.up("raw", s))
                    dve.wait_ge(*msk.at("raw", s))
                    dve.tensor_scalar(mk[s][:, 1:2], mk[s][:, 0:1], 0.0, None, ALU.not_equal)
                    dve.tensor_scalar(mk[s][:, 3:4], mk[s][:, 3:4], -1.0, 1.0e4, ALU.add, ALU.mult)
                    dve.tensor_scalar(mr_f[s][:, 0, :], mr_f[s][:, 0, :], 0.0, None, ALU.not_equal).then_inc(*msk.up("kept", s))
                    dve.wait_ge(*msk.at("kept", s))
                    dve.tensor_scalar(mk[s][:, 2:3], mk[s][:, 1:2], -1.0, OFF, ALU.add, ALU.mult)
                    dve.tensor_scalar(mr[s][:, 0, :], mr_f[s][:, 0, :], -1.0, OFF, ALU.add, ALU.mult)
                    dve.tensor_scalar(mr[s][:, 1, :], mr_f[s][:, 1, :], -1.0, 1.0e4, ALU.add, ALU.mult)
                    dve.tensor_copy(VM[s][:, :, HD:HD + 1], mk[s][:, 1:2].unsqueeze(2).to_broadcast([S2, H, 1])) \
                        .then_inc(*msk.up("all", s))

                def normalize():
                    dve.wait_ge(*rs_s.at(u))
                    if u >= 1:
                        dve.wait_ge(*xT_ps.at(u - 1, T - 1))
                    for t in range(T):
                        dve.tensor_scalar(xn[:, t, :], x[s][:, t, :], mv[s][:, t, 0:1], rstd[s][:, 1, t:t + 1],
                                          ALU.subtract, ALU.mult).then_inc(*xn_s.up(u, t))
                    if k == "F2":
                        for t in range(T):
                            dve.wait_ge(*xn_s.at(u, t))
                            dve.scalar_tensor_tensor(out=x[s][:, t, :], in0=xn[:, t, :], scalar=gates_col[:, 1, 2:3],
                                                     in1=x[s][:, t, :], op0=ALU.mult, op1=ALU.add).then_inc(*xn_s.up(u, t, "x"))
                        dve.wait_ge(*rs_s.at(u, "rms"))
                        for t in range(T):
                            dve.wait_ge(*xn_s.at(u, t, "x"))
                            dve.tensor_scalar(xn[:, t, :], xn[:, t, :], rstd[s][:, 3, t:t + 1], None, ALU.mult) \
                                .then_inc(*xn_s.up(u, t, "y"))

                def two_largest(E):
                    dve.wait_ge(*lps.at(u))
                    if E < EMAX:
                        dve.memset(lg[s][:, :, E:EMAX], PAD)
                    dve.tensor_copy(lg[s][:, :, 0:E], bank[0][:, 0:T * E].rearrange("p (t e) -> p t e", e=E)) \
                        .then_inc(*lg_s.up(u, "logits"))
                    dve.wait_ge(*lg_s.at(u, "logits"))
                    for t in range(T):
                        dve.max(top[s][:, t, :], lg[s][:, t, :]).then_inc(*lg_s.up(u, "top", t))
                    dve.wait_ge(*lg_s.at(u, "top", T - 1))
                    dve.tensor_tensor(gw[s][:, :, 0:E], lg[s][:, :, 0:E], top[s][:, :, 0:1].to_broadcast([P, T, E]),
                                      ALU.subtract).then_inc(*less.up(u))
                    dve.memset(top[s][:, :, 2:8], PAD).then_inc(*lg_s.up(u, "two"))
                    dve.wait_ge(*lg_s.at(u, "two"))
                    for t in range(T):
                        dve.match_replace(rep[s][:, t, :], in_to_replace=top[s][:, t, :], in_values=lg[s][:, t, :],
                                          imm_value=-PAD).then_inc(*lg_s.up(u, "rep", t))
                    dve.wait_ge(*lg_s.at(u, "rep", T - 1))
                    dve.tensor_tensor(rep[s][:, :, 0:E], rep[s][:, :, 0:E], lg[s][:, :, 0:E], ALU.not_equal) \
                        .then_inc(*lg_s.up(u, "sel"))

                def weigh_experts(E):
                    dve.wait_ge(*ge.at(u))
                    dve.wait_ge(*lg_s.at(u, "sel"))
                    if k == "F3":
                        dve.tensor_reduce(gs[s][:, 0, :], gw[s][:, :, 0:E], AX.X, ALU.add).then_inc(*lg_s.up(u, "sum"))
                        dve.wait_ge(*lg_s.at(u, "sum"))
                    dve.tensor_tensor(gw[s][:, :, 0:E], gw[s][:, :, 0:E], rep[s][:, :, 0:E], ALU.mult) \
                        .then_inc(*lg_s.up(u, "kept"))
                    dve.wait_ge(*lg_s.at(u, "kept"))
                    if k != "F3":
                        dve.tensor_reduce(gs[s][:, 0, :], gw[s][:, :, 0:E], AX.X, ALU.add).then_inc(*lg_s.up(u, "sum"))
                        dve.wait_ge(*lg_s.at(u, "sum"))
                    dve.reciprocal(gs[s][:, 1, :], gs[s][:, 0, :]).then_inc(*lg_s.up(u, "inv"))
                    dve.wait_ge(*lg_s.at(u, "inv"))
                    dve.tensor_tensor(gw[s][:, :, 0:E], gw[s][:, :, 0:E],
                                      gs[s][:, 1, :].unsqueeze(2).to_broadcast([P, T, E]), ALU.mult) \
                        .then_inc(*lg_s.up(u, "whole"))
                    dve.wait_ge(*lg_s.at(u, "whole"))
                    dve.tensor_copy(gp[s][:, :, 0:E].bitcast(F32R), gw[s][:, :, 0:E]).then_inc(*lg_s.up(u, "high"))
                    dve.wait_ge(*lg_s.at(u, "high"))
                    dve.tensor_tensor(gp[s][:, :, E:2 * E], gw[s][:, :, 0:E], gp[s][:, :, 0:E], ALU.subtract) \
                        .then_inc(*lg_s.up(u, "gates"))

                for i in range(steps_pre(k)):
                    if i == 0:
                        statistics()
                        if k == "A0":
                            masks()
                    if i == 2:
                        normalize()
                    if k in MHA:
                        if i == 4:
                            dve.wait_ge(*ksp.at(u, G - 1))
                            for g in range(G):
                                dve.scalar_tensor_tensor(out=Ksp[32:64, g, :], in0=bank[0][32:64, g * S2:(g + 1) * S2],
                                                         scalar=bcol[32:64, l, 1, g:g + 1], in1=Ksp[32:64, g, :],
                                                         op0=ALU.add, op1=ALU.subtract).then_inc(*klo.up(u, g))
                        if i == 5:
                            dve.wait_ge(*klo.at(u, G - 1))
                            ktv = KT[s][0:QK].rearrange("p (g j) k -> p g j k", j=J)
                            for j in range(J):
                                dve.tensor_scalar(ktv[:, :, j, :], Ksp[0:QK], hmask[0:QK, j:j + 1], None, ALU.mult) \
                                    .then_inc(*kt_s.up(u, j))
                        if Q0 + 2 <= i < Q0 + 2 + G:
                            g = i - Q0 - 2
                            dve.wait_ge(*qhi.at(u, g))
                            dve.scalar_tensor_tensor(out=Qs[s][64:QK, g, :], in0=bank[RING[g % 3]][64:QK, :],
                                                     scalar=bcol[64:QK, l, 0, g:g + 1], in1=Qs[s][64:QK, g, :].bitcast(F32),
                                                     op0=ALU.add, op1=ALU.subtract).then_inc(*qlo.up(u, g))
                        if S0 < i <= S1:
                            n = i - S0 - 1
                            t, g = n // G, n % G
                            dve.wait_ge(*sps.at(u, n))
                            dve.tensor_reduce(nm[s][:, t, J * g:J * g + J],
                                              bank[RING[(G + n) % 3]][:, 0:J * S2].rearrange("p (h k) -> p h k", k=S2),
                                              AX.X, ALU.max, negate=True).then_inc(*nm_s.up(u, n))
                        if l == 1 and S0 + 4 <= i < S1 + 4:
                            n = i - S0 - 4
                            t, g = n // G, n % G
                            if n % 2:
                                dve.wait_ge(*eexp.at(u, n))
                                dve.tensor_reduce(Z[:, 0, t, J * g:J * g + J], Eb[:, n % 3, :].rearrange("p (h k) -> p h k", k=S2),
                                                  AX.X, ALU.add)
                            dve.wait_ge(*esq.at(u, n))
                            dve.tensor_reduce(Z[:, 1, t, J * g:J * g + J], Eq[:, n % 3, :].rearrange("p (h k) -> p h k", k=S2),
                                              AX.X, ALU.add).then_inc(*temp.up(u, "sums", n))
                        if l == 1 and S0 < i <= S1:
                            n = i - S0 - 1
                            t, g = n // G, n % G
                            dve.wait_ge(*nm_s.at(u, n))
                            if n % 2 == 0:
                                dve.tensor_scalar(nms[:, t, J * g:J * g + J], nm[s][:, t, J * g:J * g + J], ROOT, None, ALU.mult) \
                                    .then_inc(*esub.up(u, n))
                            else:
                                if n >= 3:
                                    dve.wait_ge(*temp.at(u, "sums", n - 3))
                                dve.tensor_tensor(Eb[:, n % 3, :].rearrange("p (h k) -> p h k", k=S2),
                                                  bank[RING[(G + n) % 3]][:, 0:J * S2].rearrange("p (h k) -> p h k", k=S2),
                                                  nm[s][:, t, J * g:J * g + J].unsqueeze(2).to_broadcast([P, J, S2]), ALU.add) \
                                    .then_inc(*esub.up(u, n))
                        if i == S1 + 4:
                            dve.wait_ge(*temp.at(u, "sums", NS - 1))
                            dve.reciprocal(zt[:, 0], Z[:, 0]).then_inc(*temp.up(u, "inv"))
                            dve.tensor_reduce(feat[:, 1, :], nm[s][:].rearrange("p t h -> p h t"), AX.X, ALU.add)
                            dve.tensor_tensor(pk[0:QK], qsum[0:QK], ksum[s][0:QK], ALU.mult).then_inc(*temp.up(u, "pk"))
                            dve.wait_ge(*temp.at(u, "inv"))
                            dve.tensor_tensor(zt[:, 1], Z[:, 1], zt[:, 0], ALU.mult).then_inc(*temp.up(u, "z1"))
                            dve.wait_ge(*temp.at(u, "z1"))
                            dve.tensor_tensor(zt[:, 1], zt[:, 1], zt[:, 0], ALU.mult).then_inc(*temp.up(u, "z2"))
                            dve.wait_ge(*temp.at(u, "z2"))
                            dve.tensor_scalar(zt[:, 1], zt[:, 1], 1.0 / S2, None, ALU.subtract).then_inc(*temp.up(u, "z3"))
                            dve.tensor_tensor(feat[:, 0, :].rearrange("p (g j) -> p g j", j=J),
                                              pk[:].unsqueeze(2).to_broadcast([P, G, J]),
                                              quad[:, 0:1, :].to_broadcast([P, G, J]), ALU.mult)
                            dve.wait_ge(*temp.at(u, "z3"))
                            dve.tensor_reduce(feat[:, 2, :], zt[:, 1].rearrange("p t h -> p h t"), AX.X, ALU.add) \
                                .then_inc(*temp.up(u, "feat"))
                        if i == S1 + 10:
                            dve.wait_ge(*tps.at(u, 2))
                            dve.tensor_scalar(invt[:, 0, :], bank[0][0:S2, 0:H], t_b3[:, 0:1], LOG_T_MIN, ALU.add, ALU.max) \
                                .then_inc(*temp.up(u, "low"))
                            dve.wait_ge(*temp.at(u, "low"))
                            dve.tensor_scalar(invt[:, 0, :], invt[:, 0, :], LOG_T_MAX, None, ALU.min).then_inc(*temp.up(u, "clip"))
                        if i == S1 + 12:
                            dve.wait_ge(*tact.at(u, 2))
                            if u >= 1 and kind(u - 1) == k:
                                dve.wait_ge(*pt.at(u - 1, H - 1))
                            dve.tensor_scalar(invt[:, 2, :], invt[:, 1, :], 0.5, None, ALU.mult).then_inc(*temp.up(u, "invt"))
                    elif k == "A3":
                        if i == 5:
                            dve.wait_ge(*x2_s.at(u))
                            dve.tensor_scalar(x2r[s][:, 1, :], x2r[s][:, 0, :], diag[:, 0:1], None, ALU.mult).then_inc(*qlo.up(u, 1))
                        if i == 8:
                            dve.wait_ge(*sps.at(u, 0))
                            dve.tensor_reduce(nm3[s][:], bank[1][:, 0:T * S2].rearrange("p (t k) -> p t k", k=S2), AX.X, ALU.max,
                                              negate=True).then_inc(*nm_s.up(u, 0))
                    elif k in router:
                        E = router[k][2]
                        if i == 6:
                            two_largest(E)
                        if i == 8:
                            weigh_experts(E)
                    yield

            def body(u):
                s, k = u % STREAMS, kind(u)
                l = int(k[1])
                gate = gates_col[:, 0 if k[0] == "A" else 1, l:l + 1]

                def residual(src, after):
                    dve.wait_ge(*after.at(u))
                    dve.scalar_tensor_tensor(out=x[s][:].rearrange("p t d -> p (t d)"), in0=src[:], scalar=gate,
                                             in1=x[s][:].rearrange("p t d -> p (t d)"), op0=ALU.mult, op1=ALU.add) \
                        .then_inc(*done_x.up(u))

                if k in MHA:
                    def divide(g):
                        dve.wait_ge(*tops.at(u, g))
                        if g == 0 and u >= 1 and kind(u - 1) in MHA:
                            dve.wait_ge(*aps.at(u - 1))
                        turned = bank[6 + g % 2][:].rearrange("p (t j c) -> p t j c", t=T, j=J)
                        dve.reciprocal(rden[:, g], turned[:, :, :, HD]).then_inc(*norm.up(u, g, "inv"))
                        dve.wait_ge(*norm.at(u, g, "inv"))
                        dve.tensor_tensor(att[:, :, 32 * g:32 * g + 32].rearrange("p t (j d) -> p t j d", d=HD),
                                          turned[:, :, :, 0:HD], rden[:, g].unsqueeze(3).to_broadcast([P, T, J, HD]),
                                          ALU.mult).then_inc(*norm.up(u, g))
                    for h in range(H):
                        if h % J == 3 and h > J:
                            divide(h // J - 1)
                        yield
                    yield
                    divide(G - 1)
                    yield
                    yield
                    residual(bank[7], ft)
                    yield
                    return
                if k == "A3":
                    yield
                    dve.wait_ge(*ops.at(u, 0))
                    for b in (6, 7):
                        op = dve.reciprocal(gs[s][:, 0, 2 * (b - 6):2 * (b - 6) + 2],
                                            bank[b][:].rearrange("p (t c) -> p t c", t=2)[:, :, P])
                    op.then_inc(*x3_s.up(u, "inv"))
                    dve.wait_ge(*x3_s.at(u, "inv"))
                    dve.tensor_scalar(gs[s][:, 1, :], gs[s][:, 0, :], gate, None, ALU.mult).then_inc(*x3_s.up(u, "gate"))
                    yield
                    dve.wait_ge(*x3_s.at(u, "gate"))
                    for t in range(T):
                        op = dve.scalar_tensor_tensor(out=x[s][:, t, :], in0=bank[6 + t // 2][:, t % 2 * 256:t % 2 * 256 + P],
                                                      scalar=gs[s][:, 1, t:t + 1], in1=x[s][:, t, :],
                                                      op0=ALU.mult, op1=ALU.add)
                    op.then_inc(*done_x.up(u))
                    yield
                    return
                if k == "F0":
                    for c in range(C0 + 1):
                        yield
                if k in chunks:
                    def share(e):
                        dve.wait_ge(*wbps.at(u, e))
                        dve.tensor_tensor(xw[e % 2][:], xf[s][:], bank[7][:], ALU.mult).then_inc(*xw_s.up(u, e))

                    share(0)
                    for n, (e, i, o, m) in enumerate(chunks[k]):
                        dve.wait_ge(*chkA.at(u, n))
                        dve.wait_ge(*chk.at(u, n))
                        dve.tensor_tensor(hb[n % 3][0:m, :], hb[n % 3][0:m, :], bank[(2, 3, 6)[(2 * n + 1) % 3]][0:m, :],
                                          ALU.mult).then_inc(*chkV.up(u, n))
                        if i == 1 and e + 1 < router[k][2]:
                            share(e + 1)
                        yield
                if k == "F3":
                    for e in range(MOE3):
                        dve.wait_ge(*wbps.at(u, e))
                        if e >= 2:
                            dve.wait_ge(*fps.at(u, e - 2))
                        dve.tensor_tensor(xw[e % 2][:], xf[s][:], bank[(2, 7)[e % 2]][:], ALU.mult).then_inc(*xw_s.up(u, e))
                        yield
                yield
                yield
                residual(bank[7], ft)
                yield

            run(pre, body)

        @block.tensor
        def _(pe):
            reader = {}

            def free(b):
                if b in reader:
                    signal, *key = reader[b]
                    pe.wait_ge(*signal.at(*key))

            def pre(u):
                s, k = u % STREAMS, kind(u)
                l = int(k[1])

                def transpose_x():
                    free(4)
                    for t in range(T):
                        pe.wait_ge(*(xn_s.at(u, t, "y") if k == "F2" else xn_s.at(u, t)))
                        pe.transpose(bank[4][:, t * P:(t + 1) * P], xn[:, t, :], ident[:]).then_inc(*xT_ps.up(u, t))
                    reader[4] = (xf_s, u)

                for i in range(steps_pre(k)):
                    if k in MHA:
                        if i == 0 and k == "A0":
                            pe.wait_ge(*in_ctx[s].at("all"))
                            free(1)
                            pe.transpose(bank[1][:, 0:S2], ctxn[s][:, 0:P], ident[0:S2, 0:S2]).then_inc(*ctx_ps.up(s))
                            reader[1] = (ctx_t, s)
                        if i == 2:
                            free(0)
                            pe.wait_ge(*ctx_t.at(s))
                            for g in range(G):
                                op = pe.matmul(bank[0][:, g * S2:(g + 1) * S2], WkR[l][:, g, :], ctxT[s][:], start=True, stop=True)
                            op.then_inc(*kps.up(u))
                            reader[0] = (klo, u, G - 1)
                            free(1)
                            pe.matmul(bank[1][0:S2, 0:P], ctxT[s][:], Wv[l][:], start=True, stop=False)
                            pe.matmul(bank[1][0:S2, 0:P], ones[0:1, 0:S2], bv[0:1, l, :], start=False, stop=True) \
                                .then_inc(*vps.up(u))
                            reader[1] = (vp_s, u)
                        if i == 3:
                            transpose_x()
                        if Q0 <= i < S0:
                            g = i - Q0
                            b = RING[g % 3]
                            pe.wait_ge(*xf_s.at(u))
                            free(b)
                            pe.matmul(bank[b][:], WqR[l][:, g, :], xf[s][:], start=True, stop=True).then_inc(*qps.up(u, g))
                            reader[b] = (qlo, u, g)
                        if S0 <= i < S1:
                            n = i - S0
                            t, g = n // G, n % G
                            b = RING[(G + n) % 3]
                            free(b)
                            if n == 0:
                                pe.wait_ge(*kt_s.at(u, J - 1))
                            if n < G:
                                pe.wait_ge(*qlo.at(u, g))
                            dst = bank[b][:, 0:J * S2]
                            op = pe.matmul(dst, Qs[s][0:QK, g, t * P:(t + 1) * P],
                                           KT[s][0:QK, J * g:J * g + J, :].rearrange("p h k -> p (h k)"),
                                           start=True, stop=l == 1)
                            if l == 0:
                                op = pe.matmul(dst, identb[:], mask_q[:, t:t + 1, :].to_broadcast([P, J, S2]),
                                               start=False, stop=True)
                            if l == 2:
                                pe.wait_ge(*msk.at("all", s))
                                op = pe.matmul(dst, onesb[:], mr[s][0:1, 0:1, :].to_broadcast([1, J, S2]),
                                               start=False, stop=True)
                            op.then_inc(*sps.up(u, n))
                            reader[b] = (nm_s, u, n) if l != 1 else (esub, u, n) if n % 2 else (eexp, u, n)
                        if i == S1 + 1:
                            pe.wait_ge(*nm_s.at(u, NS - 1))
                            free(4)
                            for t in range(T):
                                op = pe.matmul(bank[4][QK:QK + H, t * P:(t + 1) * P], nm[s][:, t, :], ident[:],
                                               start=True, stop=True, tile_position=(0, QK))
                            op.then_inc(*nmps.up(u))
                            reader[4] = (nmT_s, u, G - 1)
                        if i == S1 + 5:
                            free(0)
                            pe.wait_ge(*temp.at(u, "feat"))
                            for f in range(3):
                                op = pe.matmul(bank[0][0:64, 0:H], t_w1b[:, f, :], feat[:, f, :], start=f == 0, stop=f == 2)
                            op.then_inc(*tps.up(u, 0))
                        if i == S1 + 7:
                            free(1)
                            pe.wait_ge(*tact.at(u, 0))
                            pe.matmul(bank[1][0:64, 0:H], t_w2T[:], hid[:, 0, :], start=True, stop=True).then_inc(*tps.up(u, 1))
                        if i == S1 + 9:
                            pe.wait_ge(*tact.at(u, 1))
                            pe.matmul(bank[0][0:S2, 0:H], t_w3[:, 0:1].to_broadcast([64, S2]), hid[:, 1, :],
                                      start=True, stop=True).then_inc(*tps.up(u, 2))
                            reader[0] = (temp, u, "low")
                            reader[1] = (tact, u, 1)
                    elif i == 3:
                        transpose_x()
                        if k == "A3":
                            free(1)
                            pe.matmul(bank[1][:, 0:S2], W3x[:], ctxT[s][:], start=True, stop=True).then_inc(*qps.up(u, 1))
                            reader[1] = (x2_s, u)
                    elif k == "A3":
                        if i == 5:
                            free(0)
                            pe.wait_ge(*xf_s.at(u))
                            pe.matmul(bank[0][:], W3x[:], xf[s][:], start=True, stop=True).then_inc(*qps.up(u, 0))
                            reader[0] = (qhi, u, 0)
                        if i == 7:
                            free(1)
                            pe.wait_ge(*qlo.at(u, 1))
                            pe.wait_ge(*qhi.at(u, 0))
                            pe.matmul(bank[1][:, 0:T * S2], onesb[:], mr[s][0:1, 1:2, :].to_broadcast([1, T, S2]),
                                      start=True, stop=False)
                            for t in range(T):
                                op = pe.matmul(bank[1][:, t * S2:(t + 1) * S2], x1r[s][:, t * P:(t + 1) * P], x2r[s][:, 1, :],
                                               start=False, stop=t == T - 1)
                            op.then_inc(*sps.up(u, 0))
                            reader[1] = (nm_s, u, 0)
                        if i == 9:
                            free(4)
                            pe.wait_ge(*nm_s.at(u, 0))
                            for t in range(T):
                                op = pe.transpose(bank[4][0:1, t * P:(t + 1) * P], nm3[s][:, t:t + 1], ident[:])
                            op.then_inc(*nmps.up(u))
                            reader[4] = (nmT_s, u)
                    elif k in router:
                        w, b, E = router[k]
                        if i == 5:
                            free(0)
                            pe.wait_ge(*xf_s.at(u))
                            if b is not None:
                                pe.matmul(bank[0][:, 0:T * E], ones[0:1, 0:P], b[0:1, None, :].to_broadcast([1, T, E]),
                                          start=True, stop=False)
                            for t in range(T):
                                op = pe.matmul(bank[0][:, t * E:(t + 1) * E], xf[s][:, t * P:(t + 1) * P], w[:],
                                               start=b is None, stop=b is None or t == T - 1)
                            op.then_inc(*lps.up(u))
                            reader[0] = (lg_s, u, "logits")
                        if i == 9:
                            free(4)
                            pe.wait_ge(*lg_s.at(u, "gates"))
                            for t in range(T):
                                op = pe.transpose(bank[4][0:2 * E, t * P:(t + 1) * P], gp[s][:, t, 0:2 * E], ident[:])
                            op.then_inc(*gps.up(u))
                            reader[4] = (gT_s, u)
                    yield

            def body(u):
                s, k = u % STREAMS, kind(u)
                l = int(k[1])
                if k in MHA:
                    vals = VM[s] if l == 2 else VP[s]

                    def weigh(g):
                        free(6 + g % 2)
                        for j in range(J):
                            h = g * J + j
                            pe.wait_ge(*pt.at(u, h))
                            op = pe.matmul(bank[6 + g % 2][32 * j:32 * j + 32, :], vals[:, h, :], PT[h % NPT][:],
                                           start=True, stop=True, tile_position=(0, 32 * j))
                        op.then_inc(*ops.up(u, g))
                        reader[6 + g % 2] = (os_s, u, g)

                    def turn(g):
                        free(6 + g % 2)
                        for t in range(T):
                            op = pe.transpose(bank[6 + g % 2][:, t * P:(t + 1) * P], Os[:, g % 2, t * P:(t + 1) * P], ident[:])
                        op.then_inc(*tops.up(u, g))
                        reader[6 + g % 2] = (norm, u, g)

                    for h in range(H):
                        b = (2, 3, 5)[h % 3]
                        free(b)
                        dst = bank[b][0:S2, :]
                        if l == 0:
                            pe.matmul(dst, identb[0:S2, 0:S2], mask_k[:], start=True, stop=False)
                        pe.wait_ge(*nmT_s.at(u, h // J))
                        pe.matmul(dst, KT[s][:, h, :], Qs[s][:, h // J, :], start=l != 0, stop=True).then_inc(*st.up(u, h))
                        reader[b] = (pt, u, h)
                        if h % J == 0 and h:
                            weigh(h // J - 1)
                        if h % J == 2 and h > J:
                            turn(h // J - 1)
                        yield
                    weigh(G - 1)
                    yield
                    turn(G - 1)
                    yield
                    free(6)
                    pe.wait_ge(*norm.at(u, G - 1))
                    for t in range(T):
                        op = pe.transpose(bank[6][:, t * P:(t + 1) * P], att[:, t, :], ident[:])
                    op.then_inc(*aps.up(u))
                    reader[6] = (at_s, u)
                    yield
                    free(7)
                    pe.wait_ge(*at_s.at(u))
                    pe.matmul(bank[7][:], ones_r[:], bo[:, l:l + 1, :].to_broadcast([2, T, P]), start=True, stop=False)
                    for t in range(T):
                        op = pe.matmul(bank[7][:, t * P:(t + 1) * P], attT[:, t * P:(t + 1) * P], Wo[l][:],
                                       start=False, stop=t == T - 1)
                    op.then_inc(*ft.up(u))
                    reader[7] = (done_x, u)
                    yield
                    return
                if k == "A3":
                    free(2)
                    pe.wait_ge(*nmT_s.at(u))
                    pe.matmul(bank[2][0:S2, :], x2r[s][:, 1, :], x1r[s], start=True, stop=False)
                    pe.matmul(bank[2][0:S2, :], ones_r[0:1, 0:S2], nmT3[s][:], start=False, stop=True).then_inc(*st.up(u, 0))
                    reader[2] = (pt, u, 0)
                    yield
                    free(6)
                    free(7)
                    pe.wait_ge(*pt.at(u, 0))
                    for t in range(T):
                        op = pe.matmul(bank[6 + t // 2][:, t % 2 * 256:t % 2 * 256 + P + 1], PT[0][:, t * P:(t + 1) * P],
                                       ctxn[s][:], start=True, stop=True)
                    op.then_inc(*ops.up(u, 0))
                    reader[6] = reader[7] = (done_x, u)
                    yield
                    yield
                    return
                if k == "F0":
                    def down(c):
                        if c == 0:
                            free(5)
                        pe.wait_ge(*chkA.at(u, c))
                        pe.matmul(bank[5][:], f0_out[:, c, :], hb[c % 3][:], start=c == 0, stop=c == C0 - 1) \
                            .then_inc(*fps.up(u, c))
                    pe.wait_ge(*xf_s.at(u))
                    for c in range(C0):
                        free((2, 3, 6)[c % 3])
                        pe.matmul(bank[(2, 3, 6)[c % 3]][:], f0_in[:, c * P:(c + 1) * P], xf[s][:], start=True, stop=True) \
                            .then_inc(*chk.up(u, c))
                        reader[(2, 3, 6)[c % 3]] = (chkA, u, c)
                        if c >= 1:
                            down(c - 1)
                        yield
                    down(C0 - 1)
                    yield
                    fps.counts[(u, "end")] = fps.counts[(u, C0 - 1)]
                if k in chunks:
                    todo = chunks[k]
                    E = router[k][2]
                    pe.wait_ge(*gT_s.at(u))

                    def broadcast(e):
                        free(7)
                        pe.matmul(bank[7][:], pick[k][:, e:e + 1].to_broadcast([2 * E, P]), gT[s][0:2 * E, :], start=True, stop=True) \
                            .then_inc(*wbps.up(u, e))
                        reader[7] = (xw_s, u, e)

                    def down(n):
                        e, i, o, m = todo[n]
                        if n == 0:
                            free(5)
                        pe.wait_ge(*chkV.at(u, n))
                        wd = m1_w2[0:m, e, i, :] if k == "F1" else m2_w3[0:m, e, i, :]
                        pe.matmul(bank[5][:], wd, hb[n % 3][0:m, :], start=n == 0, stop=n == len(todo) - 1) \
                            .then_inc(*fps.up(u, n))

                    broadcast(0)
                    for n, (e, i, o, m) in enumerate(todo):
                        if k == "F1":
                            wu, wg = m1_w1[:, e, o:o + m], m1_w3[:, e, o:o + m]
                        else:
                            wu, wg = m2_w1[:, e * F2 + o:e * F2 + o + m], m2_w2[:, e * F2 + o:e * F2 + o + m]
                        bu, bg = (2, 3, 6)[2 * n % 3], (2, 3, 6)[(2 * n + 1) % 3]
                        free(bu)
                        pe.matmul(bank[bu][0:m, :], wu, xf[s][:], start=True, stop=True).then_inc(*chk.up(u, n, "up"))
                        reader[bu] = (chkA, u, n)
                        if i == 1 and e + 1 < E:
                            broadcast(e + 1)
                        free(bg)
                        pe.wait_ge(*xw_s.at(u, e))
                        pe.matmul(bank[bg][0:m, :], wg, xw[e % 2][:], start=True, stop=True).then_inc(*chk.up(u, n))
                        reader[bg] = (chkV, u, n)
                        if n >= 1:
                            down(n - 1)
                        yield
                    down(len(todo) - 1)
                    fps.counts[(u, "end")] = fps.counts[(u, len(todo) - 1)]
                if k == "F3":
                    pe.wait_ge(*gT_s.at(u))
                    free(5)
                    pe.matmul(bank[5][:], m3_b[:], gT[s][:].bitcast(F32), start=True, stop=False)
                    for e in range(MOE3):
                        b = (2, 7)[e % 2]
                        free(b)
                        pe.matmul(bank[b][:], pick[k][:, e:e + 1].to_broadcast([2 * MOE3, P]), gT[s][:], start=True, stop=True) \
                            .then_inc(*wbps.up(u, e))
                        reader[b] = (xw_s, u, e)
                        if e:
                            pe.wait_ge(*xw_s.at(u, e - 1))
                            pe.matmul(bank[5][:], m3_w[:, e - 1, :], xw[(e - 1) % 2][:], start=False, stop=False) \
                                .then_inc(*fps.up(u, e - 1))
                        yield
                    pe.wait_ge(*xw_s.at(u, MOE3 - 1))
                    pe.matmul(bank[5][:], m3_w[:, MOE3 - 1, :], xw[(MOE3 - 1) % 2][:], start=False, stop=True) \
                        .then_inc(*fps.up(u, MOE3 - 1))
                    fps.counts[(u, "end")] = fps.counts[(u, MOE3 - 1)]
                reader[5] = (oT_s, u)
                yield
                free(7)
                pe.wait_ge(*oT_s.at(u))
                for t in range(T):
                    op = pe.transpose(bank[7][:, t * P:(t + 1) * P], oT[:, t * P:(t + 1) * P], ident[:])
                op.then_inc(*ft.up(u))
                reader[7] = (done_x, u)
                yield
                yield

            run(pre, body)

    nc.all_engine_barrier(sems_to_clear=to_clear)


_INS = """x ctx_1024 mask_SxS2_bk0 mask_BxS2_ik0 mask_BxS2_if1 g_xattn g_ffn
L0_xattn_Wq L0_xattn_bq L0_xattn_Wk L0_xattn_bk L0_xattn_Wv L0_xattn_bv L0_xattn_Wo L0_xattn_bo
L0_ffn_Win L0_ffn_bin_ L0_ffn_W1 L0_ffn_b1 L0_ffn_W2 L0_ffn_b2 L0_ffn_Wout L0_ffn_bout
L1_xattn_Wq L1_xattn_bq L1_xattn_Wk L1_xattn_bk L1_xattn_Wv L1_xattn_bv L1_xattn_Wo L1_xattn_bo
L1_xattn_w1 L1_xattn_b1 L1_xattn_w2 L1_xattn_b2 L1_xattn_w3 L1_xattn_b3
L1_ffn_router_w L1_ffn_router_b L1_ffn_w1 L1_ffn_w3 L1_ffn_w2
L2_xattn_Wq L2_xattn_bq L2_xattn_Wk L2_xattn_bk L2_xattn_Wv L2_xattn_bv L2_xattn_Wo L2_xattn_bo
L2_ffn_gate_w L2_ffn_rms_w L2_ffn_W1 L2_ffn_W2 L2_ffn_W3
L3_xattn_W L3_xattn_diagonal L3_ffn_W_experts L3_ffn_b_experts L3_ffn_W_router L3_ffn_b_router""".split()


def kernel(**inputs):
    import numpy as _np
    import concourse.bacc as _bacc
    from concourse import mybir as _mybir
    from concourse.bass_utils import run_bass_kernel_spmd as _run

    def program(seen, counts):
        nc = _bacc.Bacc("TRN2", target_bir_lowering=False, num_devices=1)
        arrays, args = {}, {}
        for name in _INS:
            arr = _np.ascontiguousarray(inputs[name])
            arrays[f"in_{name}_dram"] = arr
            args[name] = nc.dram_tensor(f"in_{name}_dram", arr.shape, _mybir.dt.from_np(arr.dtype),
                                        kind="ExternalInput").ap()
        out = nc.dram_tensor("out_0_dram", (B, N, P), _mybir.dt.float32, kind="ExternalOutput").ap()
        build(nc, args, out, seen, counts)
        return nc, arrays

    counts = {}
    program({}, counts)
    nc, arrays = program(counts, {})
    r = _run(nc, [arrays], core_ids=[0])
    return r.results[0]["out_0_dram"]
```

```python
import math
from contextlib import ExitStack
from itertools import chain

import concourse.bass as bass
from concourse import mybir

F32 = mybir.dt.float32
F32R = mybir.dt.float32r
BF16 = mybir.dt.bfloat16
ALU = mybir.AluOpType
ACT = mybir.ActivationFunctionType
AX = mybir.AxisListType

P = 128
T = 4
N = P * T
B = 4
STREAMS = 2
S2 = 77
S2E = S2 + S2 % 2
H = 16
HD = 8
G = 4
J = H // G
ROOT = float(HD) ** -0.5
OFF = float(2.0 ** 100)
PAD = -3.0e38
LOG_T_MIN, LOG_T_MAX = math.log(0.1), math.log(10.0)
LN_EPS = 1e-5
RMS_EPS = 1e-6
LAYERS = 4
UNITS = 2 * LAYERS * STREAMS

MOE1 = 4
F1 = 512
MOE2 = 8
F2 = 352
MOE3 = 8
EMAX = 8
QK = 96
LG = 16
M0, I0 = 64, 16
C0 = M0 * I0 // P


def kind(u):
    return "AF"[(u // STREAMS) % 2] + str(u // STREAMS // 2)


def pieces(width):
    return [(o, min(P, width - o)) for o in range(0, width, P)]


class Signal:

    def __init__(self, sem, seen, counts, name):
        self.sem, self.counts = sem, counts.setdefault(name, {})
        self.seen, self.total = seen.get(name, {}), 0

    def up(self, *key, by=1):
        self.total += by
        self.counts[key] = self.total
        return (self.sem, by)

    def at(self, *key):
        return (self.sem, self.seen[key] if self.seen else 1)


def build(nc, a, out, seen, counts):
    with ExitStack() as ctx:
        sems = []

        def sb(name, shape, dt=F32):
            return ctx.enter_context(nc.sbuf_tensor(name, shape, dt))

        def sig(name):
            s = ctx.enter_context(nc.semaphore(name))
            sems.append(s)
            return Signal(s, seen, counts, name)

        bank = [ctx.enter_context(nc.psum_tensor(f"bank{i}", [P, 512], F32)) for i in range(8)]

        ident = sb("ident", [P, P])
        identb = sb("identb", [P, P], BF16)
        pick1 = sb("pick1", [2 * MOE1, MOE1], F32R)
        pick2 = sb("pick2", [2 * MOE2, MOE2], F32R)
        quad = sb("quad", [P, 4, J])
        hmask = sb("hmask", [P, J])
        ones = sb("ones", [P, P])
        ones_r = sb("ones_r", [2, P], F32R)
        onesb = sb("onesb", [1, P], BF16)
        minus_half = sb("minus_half", [P, T])
        gates_col = sb("gates_col", [P, 2, LAYERS])
        graw = sb("graw", [P, 2, LAYERS])

        WqR = [sb(f"WqR{l}", [P, G, QK]) for l in range(3)]
        WkR = [sb(f"WkR{l}", [P, G, QK]) for l in range(3)]
        Wv = [sb(f"Wv{l}", [P, P]) for l in range(3)]
        Wo = [sb(f"Wo{l}", [P, P]) for l in range(3)]
        bv = sb("bv", [1, 3, P])
        bo = sb("bo", [2, 3, P], F32R)
        bcol = sb("bcol", [P, 3, 2, G])
        W3x = sb("W3x", [P, P])
        diag = sb("diag", [P, 1])
        t_w1b = sb("t_w1b", [P, 3, 64])
        t_b1 = sb("t_b1", [64, 1])
        t_b2 = sb("t_b2", [64, 1])
        t_w2T = sb("t_w2T", [64, 64])
        t_w3 = sb("t_w3", [64, 1])
        t_b3 = sb("t_b3", [S2, 1])
        f0_in = sb("f0_in", [P, M0 * I0])
        f0_out = sb("f0_out", [P, C0, P])
        f0_cols = sb("f0_cols", [P, 3, C0])
        f0_bias = sb("f0_bias", [P, 1])
        m1_router = sb("m1_router", [P, MOE1])
        m1_rb = sb("m1_rb", [1, MOE1])
        m1_w1 = [sb(f"m1_w1_{part}", [P, MOE1, F1], F32R) for part in ("hi", "lo")]
        m1_w3 = [sb(f"m1_w3_{part}", [P, MOE1, F1], F32R) for part in ("hi", "lo")]
        m1_w2 = sb("m1_w2", [P, MOE1, F1 // P, P])
        m2_router = sb("m2_router", [P, MOE2])
        m2_rms = sb("m2_rms", [P, 1])
        m2_w1 = [sb(f"m2_w1_{part}", [P, MOE2 * F2], F32R) for part in ("hi", "lo")]
        m2_w2 = [sb(f"m2_w2_{part}", [P, MOE2 * F2], F32R) for part in ("hi", "lo")]
        m2_w3 = sb("m2_w3", [P, MOE2, 3, P])
        m3_router = sb("m3_router", [P, MOE3])
        m3_rb = sb("m3_rb", [1, MOE3])
        m3_w = sb("m3_w", [P, MOE3, P])
        m3_b = sb("m3_b", [2 * MOE3, P])
        mask_q = sb("mask_q", [P, T, S2], BF16)
        mask_k = sb("mask_k", [S2, N], BF16)

        KT = [sb(f"KT{s}", [QK + H, H, S2], F32R) for s in range(STREAMS)]
        VP = [sb(f"VP{s}", [S2, H, 32]) for s in range(STREAMS)]
        lg = [sb(f"lg{s}", [P, T, LG]) for s in range(STREAMS)]
        pk = sb("pk", [P, G])
        ctxn = [sb(f"ctxn{s}", [S2, P + 1]) for s in range(STREAMS)]

        with ExitStack() as pro:
            def tmp(name, shape, dt=F32):
                return pro.enter_context(nc.sbuf_tensor(name, shape, dt))

            nat1 = [tmp(f"nat1{i}", [P, P]) for i in range(3)]
            Wq = [tmp(f"Wq{l}", [P, P]) for l in range(3)]
            Wk = [tmp(f"Wk{l}", [P, P]) for l in range(3)]
            nat_in = tmp("nat_in", [P, M0])
            natwo = tmp("natwo", [P, P])
            nat_b = tmp("nat_b", [3 * 2 * G, 32])
            nat_b3 = tmp("nat_b3", [3 * 2 * G, 3, 32])
            bo_f = tmp("bo_f", [2, 3, P])
            bo_p = tmp("bo_p", [2, 2, 3, P])
            nat3x = tmp("nat3x", [P, P])
            t_w1T = tmp("t_w1T", [3, 64])
            nat_t1 = tmp("nat_t1", [64, 3])
            nat_t2 = tmp("nat_t2", [64, 64])
            NCH = MOE2 * F2 // P
            early = m2_w3[:].rearrange("p e c d -> p (e c d)")
            raw_w1 = early[:, 0:MOE1 * F1].rearrange("p (e f) -> p e f", e=MOE1)
            nat_e = early[:, MOE1 * F1:MOE1 * F1 + MOE3 * P].rearrange("p (e f) -> p e f", e=MOE3)
            raw_w3 = tmp("raw_w3", [P, MOE1, F1])[:]
            nat_m1 = tmp("nat_m1", [P, NCH, P])
            nat_m2 = tmp("nat_m2", [P, NCH, P])
            nat_m3 = tmp("nat_m3", [P, MOE2, F2])
            nat_r = tmp("nat_r", [MOE2, 2, P])
            nat_f0 = tmp("nat_f0", [C0, 4, P])
            nat_bin = tmp("nat_bin", [C0, M0 // C0])
            f0_wout = tmp("f0_wout", [M0, P])
            f0_b2 = tmp("f0_b2", [M0, 1])
            f0_bout = tmp("f0_bout", [P, 1])
            m8 = tmp("m8", [P, T, S2], mybir.dt.uint8)
            mf = tmp("mf", [P, T, S2])
            quad_b = tmp("quad_b", [P, 4, J])

            landed = {n: sig("landed_" + n) for n in ("small", "gates", "turn", "m2_w1", "m2_w2", "m2_w3", "m3", "m1", "rest", "mask", "f0")}
            zeroed = sig("zeroed")
            const = sig("const")
            turned = sig("turned")
            keptA, keptD = sig("kept_act"), sig("kept_dve")
            folded = sig("folded")

            groups = []

            def grouped(load, items):
                row, width = [], 0
                for src, dst in items:
                    k = src.shape[0]
                    if row and (width + k > 512):
                        groups.append((load, row))
                        row, width = [], 0
                    row.append((src, dst, width))
                    width += k
                groups.append((load, row))

            def split_parts(load, nat, w):
                grouped(load, [(nat[:, c, :], [part[:, c * P:(c + 1) * P] for part in w]) for c in range(NCH)])
                return list(range(len(groups) - -(-NCH // 4), len(groups)))

            split = split_parts("m2_w1", nat_m1, m2_w1)
            split += split_parts("m2_w2", nat_m2, m2_w2)
            grouped("m3", [(nat_e[:, e, :], m3_w[:, e, :]) for e in range(MOE3)])
            first_turn = len(groups)
            grouped("turn", [(nat1[0][:], Wq[1][:]), (nat1[1][:], Wk[1][:]), (nat1[2][:], Wv[1][:]), (nat3x[:], W3x[:])])
            grouped("turn", [(nat_b3[:].rearrange("r q c -> r (q c)"), bcol[0:QK].rearrange("p l i g -> p (l i g)")),
                             (natwo[:], Wo[1][:])])
            grouped("turn", [(nat_t1[:], t_w1T[:]), (nat_t2[:], t_w2T[:]), (nat_r[:, 0, :], m2_router[:]),
                             (nat_r[:, 1, :], m3_router[:]), (nat_f0[:, 0, :], f0_cols[:, 0, :]),
                             (nat_f0[:, 3, :], f0_cols[:, 1, :]), (nat_f0[:, 2, :], f0_cols[:, 2, :])])
            last_turn = len(groups) - 1
            grouped("mask", [(mf[:, t, :], mask_k[:, t * P:(t + 1) * P]) for t in range(T)])
            m2_last = len(groups)
            grouped("m2_w3", [(nat_m3[:, e, o:o + w], m2_w3[0:w, e, i, :]) for e in range(MOE2)
                              for i, (o, w) in enumerate(pieces(F2))])

            def kept(i):
                return (keptA if i % 2 and i not in split else keptD).at(i)

            block = pro.enter_context(nc.Block())

            @block.sync
            def _(sp):
                for i, n in enumerate(("Wq", "Wk", "Wv")):
                    sp.dma_start(nat1[i][:], a[f"L1_xattn_{n}"]).then_inc(*landed["turn"].up(by=16))
                sp.dma_start(nat3x[:], a["L3_xattn_W"]).then_inc(*landed["turn"].up(by=16))
                sp.dma_start(natwo[:], a["L1_xattn_Wo"]).then_inc(*landed["turn"].up(by=16))
                sp.dma_start(nat_t1[:], a["L1_xattn_w1"]).then_inc(*landed["turn"].up(by=16))
                sp.dma_start(nat_t2[:], a["L1_xattn_w2"]).then_inc(*landed["turn"].up(by=16))
                sp.dma_start(nat_r[:, 0, :], a["L2_ffn_gate_w"]).then_inc(*landed["turn"].up(by=16))
                sp.dma_start(nat_r[:, 1, :], a["L3_ffn_W_router"]).then_inc(*landed["turn"].up(by=16))
                for l in range(3):
                    for i, n in enumerate(("bq", "bk")):
                        sp.dma_start(nat_b[(2 * l + i) * G:(2 * l + i + 1) * G, :],
                                     a[f"L{l}_xattn_{n}"].rearrange("(g c) -> g c", c=32)).then_inc(*landed["turn"].up(by=16))
                for i, n in enumerate(("W1", "b1", "W2")):
                    sp.dma_start(nat_f0[:, i, :], a[f"L0_ffn_{n}"].rearrange("(c m) i -> c (m i)", c=C0)) \
                        .then_inc(*landed["turn"].up(by=16))
                sp.dma_start(nat_bin[:], a["L0_ffn_bin_"].rearrange("(c m) -> c m", c=C0)) \
                    .then_inc(*landed["turn"].up("all", by=16))
                for l in (0, 2):
                    for n, w in (("Wq", Wq), ("Wk", Wk), ("Wv", Wv), ("Wo", Wo)):
                        sp.dma_start(w[l][:], a[f"L{l}_xattn_{n}"]).then_inc(*landed["small"].up(by=16))
                for l in range(3):
                    for n, row in (("bv", bv[0:1, l, :]), ("bo", bo_f[0:1, l, :]), ("bo", bo_f[1:2, l, :])):
                        sp.dma_start(row, a[f"L{l}_xattn_{n}"].rearrange("(o n) -> o n", o=1)) \
                            .then_inc(*landed["small"].up(by=16))
                for src, dst in ((a["L3_xattn_diagonal"], diag), (a["L1_xattn_b1"], t_b1), (a["L1_xattn_b2"], t_b2),
                                 (a["L0_ffn_b2"], f0_b2), (a["L0_ffn_bout"], f0_bout), (a["L2_ffn_rms_w"], m2_rms)):
                    sp.dma_start(dst[:], src.rearrange("(n o) -> n o", o=1)).then_inc(*landed["small"].up(by=16))
                sp.dma_start(t_w3[:], a["L1_xattn_w3"].rearrange("o n -> n o")).then_inc(*landed["small"].up(by=16))
                sp.dma_start(t_b3[:], a["L1_xattn_b3"].partition_broadcast(S2)).then_inc(*landed["small"].up(by=16))
                sp.dma_start(nat_in[:], a["L0_ffn_Win"]).then_inc(*landed["small"].up(by=16))
                sp.dma_start(f0_wout[:], a["L0_ffn_Wout"]).then_inc(*landed["small"].up(by=16))
                sp.dma_start(m1_router[:], a["L1_ffn_router_w"]).then_inc(*landed["small"].up(by=16))
                sp.dma_start(m1_rb[:], a["L1_ffn_router_b"].rearrange("(o n) -> o n", o=1)).then_inc(*landed["small"].up(by=16))
                sp.dma_start(m3_rb[:], a["L3_ffn_b_router"].rearrange("(o n) -> o n", o=1)).then_inc(*landed["small"].up(by=16))
                sp.dma_start(m3_b[0:MOE3, :], a["L3_ffn_b_experts"]).then_inc(*landed["small"].up(by=16))
                sp.dma_start(m3_b[MOE3:2 * MOE3, :], a["L3_ffn_b_experts"]).then_inc(*landed["small"].up("all", by=16))
                for name in ("small", "rest", "gates"):
                    sp.wait_ge(*landed[name].at("all"))

            @block.scalar
            def _(act):
                act.dma_start(m8[:], a["mask_SxS2_bk0"].rearrange("(p t) k -> p t k", t=T)) \
                    .then_inc(*landed["mask"].up("all", by=16))
                act.dma_start(nat_m1[:], a["L2_ffn_W1"].rearrange("e n d -> (e n) d").rearrange("(c p) d -> p c d", p=P)) \
                    .then_inc(*landed["m2_w1"].up("all", by=16))
                act.dma_start(nat_m2[:], a["L2_ffn_W2"].rearrange("e n d -> (e n) d").rearrange("(c p) d -> p c d", p=P)) \
                    .then_inc(*landed["m2_w2"].up("all", by=16))
                act.dma_start(nat_e, a["L3_ffn_W_experts"].rearrange("e o i -> o e i")).then_inc(*landed["m3"].up("all", by=16))
                act.dma_start(raw_w1, a["L1_ffn_w1"].rearrange("e d f -> d e f")).then_inc(*landed["m1"].up(by=16))
                act.dma_start(raw_w3, a["L1_ffn_w3"].rearrange("e d f -> d e f")).then_inc(*landed["m1"].up("all", by=16))
                act.dma_start(nat_m3[:], a["L2_ffn_W3"].rearrange("e m n -> m e n")).then_inc(*landed["m2_w3"].up("all", by=16))
                act.dma_start(m1_w2[:], a["L1_ffn_w2"].rearrange("e (c p) d -> p e c d", p=P)) \
                    .then_inc(*landed["rest"].up("all", by=16))
                act.dma_start(graw[:, 0, :], a["g_xattn"].partition_broadcast(P)).then_inc(*landed["gates"].up(by=16))
                act.dma_start(graw[:, 1, :], a["g_ffn"].partition_broadcast(P)).then_inc(*landed["gates"].up("all", by=16))
                for i, (_, row) in enumerate(groups):
                    if i == first_turn:
                        act.wait_ge(*landed["m1"].at("all"))
                        for raw, w in ((raw_w1, m1_w1), (raw_w3, m1_w3)):
                            act.activation(w[0][:], raw, ACT.Copy).then_inc(*keptA.up("m1", w[0].name))
                    if i == m2_last:
                        act.wait_ge(*landed["gates"].at("all"))
                        act.activation(gates_col[:], graw[:], ACT.Tanh)
                        act.wait_ge(*folded.at("m1"))
                    if i in split:
                        act.wait_ge(*turned.at(i))
                        for src, dst, at in row:
                            op = act.activation(dst[0], bank[i % 8][:, at:at + P], ACT.Copy)
                        op.then_inc(*keptA.up(i))
                    elif i % 2:
                        act.wait_ge(*turned.at(i))
                        for n, (src, dst, at) in enumerate(row):
                            k, m = src.shape
                            op = act.activation(dst, bank[i % 8][0:m, at:at + k], ACT.Copy)
                        op.then_inc(*keptA.up(i))

            @block.gpsimd
            def _(pool):
                pool.memset(ident[:], 0.0)
                pool.memset(ones[:], 1.0)
                pool.memset(quad[:], 1.0)
                pool.memset(minus_half[:], -0.5)
                pool.memset(onesb[:], 1.0).then_inc(*zeroed.up("all"))
                pool.wait_ge(*zeroed.at("all"))
                pool.affine_select(out=ident[:], in_=ident[:], compare_op=ALU.not_equal, fill=1.0, base=0,
                                   pattern=[[-1, P]], channel_multiplier=1).then_inc(*const.up("ident"))
                for c in range(C0):
                    pool.dma_start(f0_out[:, c, :],
                                 a["L0_ffn_Wout"][c * 8:c * 8 + 8, :].unsqueeze(1).to_broadcast([8, I0, P])) \
                        .then_inc(*landed["f0"].up("all", by=16))
                pool.affine_select(out=quad_b[:], in_=quad[:], compare_op=ALU.is_ge, fill=0.0, base=0,
                                   pattern=[[-32, 4], [-HD, J]], channel_multiplier=1).then_inc(*const.up("quad_low"))
                pool.wait_ge(*const.at("quad_low"))
                pool.affine_select(out=quad[:], in_=quad_b[:], compare_op=ALU.is_ge, fill=0.0, base=HD - 1,
                                   pattern=[[32, 4], [HD, J]], channel_multiplier=-1).then_inc(*const.up("quad"))
                for s in range(STREAMS):
                    pool.memset(lg[s][:], PAD)
                    pool.memset(ctxn[s][:, P:P + 1], 1.0)
                    pool.memset(VP[s][:], 0.0).then_inc(*zeroed.up("values", s))
                    pool.wait_ge(*zeroed.at("values", s))
                    pool.memset(VP[s][:, :, HD:HD + 1], 1.0)
                pool.memset(pk[:], 0.0).then_inc(*zeroed.up("last"))
                pool.wait_ge(*zeroed.at("last"))
                for s in range(STREAMS):
                    pool.tensor_copy(KT[s][QK:QK + H, :, :], ident[QK:QK + H, QK:QK + H].unsqueeze(2).to_broadcast([H, H, S2])) \
                        .then_inc(*zeroed.up("heads", s))
                    pool.wait_ge(*zeroed.at("heads", s))
                pool.wait_ge(*keptA.at("m1", m1_w3[0].name))
                pool.tensor_tensor(m1_w3[1][:], raw_w3, m1_w3[0][:].bitcast(F32), ALU.subtract)

            @block.vector
            def _(dve):
                dve.wait_ge(*zeroed.at("all"))
                dve.wait_ge(*landed["mask"].at("all"))
                dve.tensor_copy(mf[:], m8[:]).then_inc(*folded.up("mask8"))
                dve.wait_ge(*folded.at("mask8"))
                dve.tensor_scalar(mf[:], mf[:], -1.0, OFF, ALU.add, ALU.mult).then_inc(*folded.up("mask"))
                dve.wait_ge(*folded.at("mask"))
                dve.tensor_copy(mask_q[:], mf[:])
                dve.wait_ge(*const.at("ident"))
                dve.tensor_copy(identb[:], ident[:])
                dve.tensor_copy(ones_r[:], ones[0:2, :])
                for pick, e in ((pick1, MOE1), (pick2, MOE2)):
                    dve.tensor_tensor(pick[:], ident[0:2 * e, 0:e], ident[0:2 * e, e:2 * e], ALU.add)
                dve.wait_ge(*const.at("quad"))
                dve.tensor_reduce(hmask[:], quad[:].rearrange("p q j -> p j q"), AX.X, ALU.add)
                for i, (_, row) in enumerate(groups):
                    if i == first_turn:
                        dve.wait_ge(*keptA.at("m1", m1_w1[0].name))
                        dve.tensor_tensor(m1_w1[1][:], raw_w1, m1_w1[0][:].bitcast(F32), ALU.subtract) \
                            .then_inc(*folded.up("m1"))
                        dve.wait_ge(*folded.at("m1"))
                    if i == first_turn:
                        dve.wait_ge(*landed["turn"].at("all"))
                        dve.tensor_copy(nat_b3[:], nat_b[:].unsqueeze(1).to_broadcast([3 * 2 * G, 3, 32])).then_inc(*folded.up("b3"))
                        dve.tensor_tensor(nat_f0[:, 3, :].rearrange("c (m i) -> c m i", i=I0),
                                          nat_f0[:, 0, :].rearrange("c (m i) -> c m i", i=I0),
                                          nat_bin[:].unsqueeze(2).to_broadcast([C0, M0 // C0, I0]), ALU.mult) \
                            .then_inc(*folded.up("binw"))
                        dve.wait_ge(*folded.at("binw"))
                        dve.tensor_tensor(nat_f0[:, 3, :], nat_f0[:, 3, :], nat_f0[:, 1, :], ALU.add).then_inc(*folded.up("b1"))
                    if i == m2_last:
                        dve.wait_ge(*kept(last_turn))
                        dve.wait_ge(*kept(last_turn - 1))
                        dve.wait_ge(*kept(last_turn - 2))
                        dve.wait_ge(*landed["small"].at("all"))
                        for l in range(3):
                            for wide, w in ((WqR, Wq), (WkR, Wk)):
                                dve.tensor_copy(wide[l][:].rearrange("p g (q c) -> p g q c", c=32),
                                                w[l][:].rearrange("p (g c) -> p g c", c=32).unsqueeze(2).to_broadcast([P, G, QK // 32, 32]))
                        dve.tensor_copy(bo_p[:, 0].bitcast(F32R), bo_f[:]).then_inc(*folded.up("bo_high"))
                        dve.wait_ge(*folded.at("bo_high"))
                        dve.tensor_tensor(bo_p[:, 1], bo_f[:], bo_p[:, 0], ALU.subtract)
                        dve.tensor_scalar(bo_p[:, 0], bo_p[:, 0], ident[0:2, 0:1], None, ALU.mult).then_inc(*folded.up("bo_low"))
                        dve.wait_ge(*folded.at("bo_low"))
                        dve.scalar_tensor_tensor(out=bo[:], in0=bo_p[:, 1], scalar=ident[0:2, 1:2], in1=bo_p[:, 0],
                                                 op0=ALU.mult, op1=ALU.add)
                        dve.tensor_copy(f0_in[:].rearrange("p (m i) -> p m i", i=I0), nat_in[:].unsqueeze(2).to_broadcast([P, M0, I0]))
                        dve.wait_ge(*landed["f0"].at("all"))
                        for c in range(C0):
                            dve.tensor_scalar(f0_out[:, c, :], f0_out[:, c, :], f0_cols[:, 2, c:c + 1], None, ALU.mult)
                    if i in split:
                        dve.wait_ge(*keptA.at(i))
                        for src, dst, at in row:
                            op = dve.tensor_tensor(dst[1], bank[i % 8][:, at:at + P], dst[0].bitcast(F32), ALU.subtract)
                        op.then_inc(*keptD.up(i))
                    elif i % 2 == 0:
                        dve.wait_ge(*turned.at(i))
                        for n, (src, dst, at) in enumerate(row):
                            k, m = src.shape
                            op = dve.tensor_copy(dst, bank[i % 8][0:m, at:at + k])
                        op.then_inc(*keptD.up(i))
                dve.wait_ge(*turned.at("columns"))
                dve.tensor_tensor(f0_bias[:], bank[0][:, 0:1], f0_bout[:], ALU.add)
                for f, s in enumerate((ROOT / (N * S2), -ROOT / N, 1.0 / (N * (S2 - 1)))):
                    dve.tensor_scalar(t_w1b[:, f, :], bank[1][:, f * 64:(f + 1) * 64], s, None, ALU.mult)

            @block.tensor
            def _(pe):
                pe.wait_ge(*const.at("ident"))
                for i, (load, row) in enumerate(groups):
                    pe.wait_ge(*landed[load].at("all"))
                    if i == first_turn:
                        pe.wait_ge(*folded.at("b3"))
                        pe.wait_ge(*folded.at("b1"))
                    if load == "mask":
                        pe.wait_ge(*folded.at("mask"))
                    if i >= 8:
                        pe.wait_ge(*kept(i - 8))
                    for src, dst, at in row:
                        k, m = src.shape
                        op = pe.transpose(bank[i % 8][0:m, at:at + k], src, ident[0:k, 0:k])
                    op.then_inc(*turned.up(i))
                last = len(groups) - 1
                for i in range(max(0, last - 7), last + 1):
                    pe.wait_ge(*kept(i))
                pe.wait_ge(*landed["small"].at("all"))
                pe.matmul(bank[0][:, 0:1], f0_wout[:], f0_b2[:], start=True, stop=True)
                for f in range(3):
                    op = pe.matmul(bank[1][:, f * 64:(f + 1) * 64], ident[0:3, f:f + 1].to_broadcast([3, P]), t_w1T[:], start=True, stop=True)
                op.then_inc(*turned.up("columns"))

        main(nc, a, out, dict(locals()))


def main(nc, a, out, v):
    ctx, sb, sig, bank = v["ctx"], v["sb"], v["sig"], v["bank"]
    ident, identb = v["ident"], v["identb"]
    quad, hmask, ones, onesb, minus_half, gates_col = (v[n] for n in (
        "quad", "hmask", "ones", "onesb", "minus_half", "gates_col"))
    WqR, WkR, Wv, Wo, bv, bo, ones_r, bcol, W3x, diag = (v[n] for n in (
        "WqR", "WkR", "Wv", "Wo", "bv", "bo", "ones_r", "bcol", "W3x", "diag"))
    t_w1b, t_b1, t_b2, t_w2T, t_w3, t_b3 = (v[n] for n in ("t_w1b", "t_b1", "t_b2", "t_w2T", "t_w3", "t_b3"))
    f0_in, f0_out, f0_cols, f0_bias = (v[n] for n in ("f0_in", "f0_out", "f0_cols", "f0_bias"))
    mask_q, mask_k = v["mask_q"], v["mask_k"]
    router = {"F1": (v["m1_router"], v["m1_rb"], MOE1), "F2": (v["m2_router"], None, MOE2),
              "F3": (v["m3_router"], v["m3_rb"], MOE3)}
    KT, VP, lg, pk = (v[n] for n in ("KT", "VP", "lg", "pk"))
    pick = {"F1": v["pick1"], "F2": v["pick2"], "F3": v["pick2"]}
    m1_w1, m1_w3, m1_w2, m2_w1, m2_w2, m2_w3, m2_rms, m3_w, m3_b = (v[n] for n in (
        "m1_w1", "m1_w3", "m1_w2", "m2_w1", "m2_w2", "m2_w3", "m2_rms", "m3_w", "m3_b"))

    def two(name, shape, dt=F32):
        return [sb(f"{name}{s}", shape, dt) for s in range(STREAMS)]

    x = two("x", [P, T, P])
    ctxn = v["ctxn"]
    ctxT = two("ctxT", [P, S2])
    xf = two("xf", [P, N])
    stats = two("stats", [P, T, 6])
    mv = two("mv", [P, T, 2])
    rstd = two("rstd", [P, 4, T])
    Qs = two("Qs", [P, G, N], F32R)
    gT = [q[0:2 * EMAX, 2, :] for q in Qs]
    xf_hi = [q[:, 0, :] for q in Qs]
    xf_lo = [q[:, 3, :] for q in Qs]
    x1r = [(q[:, 0, :], q[:, 3, :]) for q in Qs]
    nmT3 = [q[0:1, 1, :] for q in Qs]
    nm = two("nm", [P, T, H])
    mk_i = two("mk_i", [S2, 2], mybir.dt.int32)
    mr_i = two("mr_i", [1, 2, S2], mybir.dt.int32)
    mk = two("mk", [S2, 4])
    mr_f = two("mr_f", [1, 2, S2])
    mr = two("mr", [1, 2, S2E], BF16)
    ksum = two("ksum", [P, G])
    top = [sb("top", [P, T, 8])] * STREAMS
    rep = [sb("rep", [P, T, LG])] * STREAMS
    gw = two("gw", [P, T, EMAX])
    gp = two("gp", [P, T, 2 * EMAX])
    gs = two("gs", [P, 2, T])
    x2r = two("x2r", [P, S2])
    x2p = two("x2p", [P, 2, S2E], F32R)
    nm3 = two("nm3", [P, T])
    xn = sb("xn", [P, T, P])
    Ksp = sb("Ksp", [QK, G, S2])
    qsum = sb("qsum", [P, G])
    NPT = 6
    PT = [sb(f"PT{i}", [P, N]) for i in range(NPT)]
    Os = sb("Os", [P, 2, N])
    rden = sb("rden", [P, G, T, J])
    att = sb("att", [P, T, P])
    attT = Os[:, 0, :]
    hb = [PT[i][:] for i in range(3)]
    xw = [PT[i][:] for i in (3, 4)]
    shares = xw
    oT = Os[:, 0, :]
    Eb = sb("Eb", [P, 3, J * S2])
    Eq = sb("Eq", [P, 3, J * S2])
    Z = sb("Z", [P, 2, T, H])
    nms = sb("nms", [P, T, H])
    feat = sb("feat", [P, 3, H])
    zt = sb("zt", [P, T, H])
    hid = sb("hid", [64, 2, H])
    invt = sb("invt", [S2, 3, H])

    in_x, in_ctx, in_mask = ([sig(f"{n}{i}") for i in range(STREAMS)] for n in ("in_x", "in_ctx", "in_mask"))
    (ctx_turned, ctx_ready, row_stats, mean_var, rstd_ready, x_normal,
     x_turned, xf_ready, xf_high, xf_low, x_done) = (sig(n) for n in (
        "ctx_turned ctx_ready row_stats mean_var rstd_ready x_normal "
        "x_turned xf_ready xf_high xf_low x_done").split())
    (k_psum, k_high, k_low, keys_ready, v_psum,
     values_ready, masks_ready, q_psum, q_high, q_low) = (sig(n) for n in (
        "k_psum k_high k_low keys_ready v_psum "
        "values_ready masks_ready q_psum q_high q_low").split())
    (block_psum, maxima, maxima_turned, maxima_ready, block_less_max,
     block_exp, block_squared, temp_vector, temp_psum, temp_scalar) = (sig(n) for n in (
        "block_psum maxima maxima_turned maxima_ready block_less_max "
        "block_exp block_squared temp_vector temp_psum temp_scalar").split())
    (scores_psum, probs_ready, out_psum, out_kept, out_turned, out_divided,
     att_turned, attT_ready, x1_parts, x2_relu, x3_inverse) = (sig(n) for n in (
        "scores_psum probs_ready out_psum out_kept out_turned out_divided "
        "att_turned attT_ready x1_parts x2_relu x3_inverse").split())
    (logits_psum, logits_vector, logits_less_max, gates_exp, gates_turned,
     gates_ready, share_psum, share_ready, share_used) = (sig(n) for n in (
        "logits_psum logits_vector logits_less_max gates_exp gates_turned "
        "gates_ready share_psum share_ready share_used").split())
    (chunk_psum, chunk_act, chunk_ready, ffn_psum,
     oT_ready, result_psum, stored) = (sig(n) for n in (
        "chunk_psum chunk_act chunk_ready ffn_psum "
        "oT_ready result_psum stored").split())
    mine = sorted(s.num for s in (in_x[0].sem, stored.sem))
    to_clear = range(mine[0], mine[1] + 1)

    xv = a["x"].rearrange("(i s) (p t) d -> i s p t d", s=STREAMS, t=T)
    ov = out.rearrange("(i s) (p t) d -> i s p t d", s=STREAMS, t=T)
    cv = a["ctx_1024"].rearrange("(i s) k d -> i s k d", s=STREAMS)
    ik = a["mask_BxS2_ik0"].rearrange("(i s) k -> i s k", s=STREAMS)
    jf = a["mask_BxS2_if1"].rearrange("(i s) k -> i s k", s=STREAMS)

    MHA = ("A0", "A1", "A2")
    NS = T * G
    chunks = {"F1": [(e, i, o, m) for e in range(MOE1) for i, (o, m) in enumerate(pieces(F1))],
              "F2": [(e, i, o, m) for e in range(MOE2) for i, (o, m) in enumerate(pieces(F2))]}

    Q0 = 5
    S0 = Q0 + G
    S1 = S0 + NS
    RING = (1, 0, 4)

    def by_dve(n):
        return n % 2 == 1

    def steps_pre(k):
        if k in MHA:
            return S1 + (13 if k == "A1" else 3)
        return {"F0": 5, "A3": 12}.get(k, 11)

    def steps_body(k):
        if k in MHA:
            return H + 1
        return {"A3": 3, "F0": C0 + 1, "F3": MOE3 + 1}.get(k) or len(chunks[k]) + 1

    def steps_tail(k):
        return 7 if k in MHA else 0 if k == "A3" else 2

    def later(u):
        return u >= 0 and steps_tail(kind(u)) > 0 and u + 1 < UNITS and kind(u + 1)[0] == "F" and kind(u) != "F0"

    def run(pre, body, tail):
        for _ in pre(0):
            pass
        for u in range(UNITS):
            last = u + 1 == UNITS
            n, main_part = steps_body(kind(u)), body(u)
            if not later(u):
                n, main_part = n + steps_tail(kind(u)), chain(body(u), tail(u))
            t, ends = (steps_tail(kind(u - 1)), tail(u - 1)) if later(u - 1) else (0, iter(()))
            m, first = (0, iter(())) if last else (steps_pre(kind(u + 1)), pre(u + 1))
            start, sent = max(t - 1, 0), 0
            for i in range(n):
                if i < t:
                    next(ends)
                next(main_part)
                while i >= start and sent < m and (sent + 1) * (n - start) <= (i - start + 1) * m:
                    next(first)
                    sent += 1
            assert sent == m and all(next(part, None) is None for part in (ends, main_part, first))

    it = ctx.enter_context(nc.Fori(0, B // STREAMS))
    with nc.Block() as block:

        @block.sync
        def _(sp):
            for s in range(STREAMS):
                sp.dma_start(x[s][:], xv[it, s]).then_inc(*in_x[s].up("all", by=16))
                sp.dma_start(ctxn[s][:, 0:P], cv[it, s]).then_inc(*in_ctx[s].up("all", by=16))
                for i, m in enumerate((ik, jf)):
                    sp.dma_start(mk_i[s][:, i:i + 1], m[it, s].rearrange("(k o) -> k o", o=1)).then_inc(*in_mask[s].up(i, 0, by=16))
                    sp.dma_start(mr_i[s][:, i, :], m[it, s].rearrange("(o k) -> o k", o=1)).then_inc(*in_mask[s].up(i, 1, by=16))
            for s in range(STREAMS):
                sp.wait_ge(*x_done.at(UNITS - STREAMS + s))
                sp.dma_start(ov[it, s], x[s][:]).then_inc(*stored.up(s, by=16))
            sp.wait_ge(*stored.at(STREAMS - 1))

        @block.gpsimd
        def _(pool):
            def pre(u):
                s, k = u % STREAMS, kind(u)
                pool.wait_ge(*mean_var.at(u))
                pool.tensor_scalar_add(rstd[s][:, 0, :], mv[s][:, :, 1], LN_EPS).then_inc(*rstd_ready.up(u, "eps"))
                pool.wait_ge(*rstd_ready.at(u, "eps"))
                pool.tensor_tensor(rstd[s][:, 1, :], rstd[s][:, 0, :], minus_half[:], ALU.pow).then_inc(*rstd_ready.up(u))
                if k == "F2":
                    pool.wait_ge(*rstd_ready.at(u))
                    pool.tensor_tensor(rstd[s][:, 2, :], rstd[s][:, 1, :], rstd[s][:, 1, :], ALU.mult).then_inc(*rstd_ready.up(u, "sq"))
                    pool.wait_ge(*rstd_ready.at(u, "sq"))
                    pool.tensor_tensor(rstd[s][:, 2, :], rstd[s][:, 2, :], mv[s][:, :, 1], ALU.mult).then_inc(*rstd_ready.up(u, "ms"))
                    pool.wait_ge(*rstd_ready.at(u, "ms"))
                    pool.tensor_scalar_add(rstd[s][:, 2, :], rstd[s][:, 2, :], RMS_EPS).then_inc(*rstd_ready.up(u, "ms_eps"))
                    pool.wait_ge(*rstd_ready.at(u, "ms_eps"))
                    pool.tensor_tensor(rstd[s][:, 3, :], rstd[s][:, 2, :], minus_half[:], ALU.pow).then_inc(*rstd_ready.up(u, "rms"))
                for i in range(steps_pre(k)):
                    if k == "A1" and S0 + 3 <= i < S1 + 3:
                        n = i - S0 - 3
                        pool.wait_ge(*block_exp.at(u, n))
                        if n >= 3:
                            pool.wait_ge(*temp_vector.at(u, "sums", n - 3))
                        pool.tensor_tensor(Eq[:, n % 3, :], Eb[:, n % 3, :], Eb[:, n % 3, :], ALU.mult).then_inc(*block_squared.up(u, n))
                    yield

            def body(u):
                for _ in range(steps_body(kind(u))):
                    yield

            def tail(u):
                for _ in range(steps_tail(kind(u))):
                    yield

            run(pre, body, tail)

        @block.scalar
        def _(act):
            def copy_out(u, g):
                act.wait_ge(*out_psum.at(u, g))
                if g >= 2:
                    act.wait_ge(*out_turned.at(u, g - 2))
                elif g == 0 and u >= 1 and kind(u - 1) != "A3":
                    act.wait_ge(*result_psum.at(u - 1))
                act.activation(Os[:, g % 2, :], bank[6 + g % 2][:], ACT.Copy).then_inc(*out_kept.up(u, g))

            def pre(u):
                s, k = u % STREAMS, kind(u)
                l = int(k[1])

                def normalized():
                    act.wait_ge(*x_turned.at(u, T - 1))
                    act.activation(xf[s][:], bank[4][:], ACT.Copy, scale=m2_rms[:, 0:1] if k == "F2" else 1.0) \
                        .then_inc(*xf_ready.up(u))

                for i in range(steps_pre(k)):
                    if k in MHA:
                        if i == 1 and k == "A0":
                            act.wait_ge(*ctx_turned.at(s))
                            act.activation(ctxT[s][:], bank[1][:, 0:S2], ACT.Copy).then_inc(*ctx_ready.up(s))
                        if i == 3:
                            if u >= 1 and kind(u - 1) == k:
                                act.wait_ge(*keys_ready.at(u - 1, J - 1))
                            act.wait_ge(*k_psum.at(u))
                            for g in range(G):
                                act.activation(Ksp[:, g, :].bitcast(F32R), bank[0][0:QK, g * S2:(g + 1) * S2], ACT.Identity,
                                               bias=bcol[0:QK, l, 1, g:g + 1],
                                               accum_out=ksum[s][0:QK, g:g + 1] if l == 1 else None).then_inc(*k_high.up(u, g))
                            act.wait_ge(*v_psum.at(u))
                            act.activation(VP[s][:, :, 0:HD],
                                           bank[1][0:S2, 0:P].rearrange("p (h d) -> p h d", d=HD), ACT.Copy,
                                           scale=mk[s][:, 1:2] if l == 2 else 1.0).then_inc(*values_ready.up(u))
                        if i == 4:
                            normalized()
                        if Q0 < i <= Q0 + G:
                            g = i - Q0 - 1
                            act.wait_ge(*q_psum.at(u, g))
                            act.activation(Qs[s][0:QK, g, :], bank[RING[g % 3]][0:QK, :], ACT.Identity, bias=bcol[0:QK, l, 0, g:g + 1],
                                           accum_out=qsum[0:QK, g:g + 1] if l == 1 else None).then_inc(*q_high.up(u, g))
                        if l == 1 and S0 + 2 <= i < S1 + 2:
                            n = i - S0 - 2
                            t, g = n // G, n % G
                            act.wait_ge(*block_less_max.at(u, n))
                            if n >= 3:
                                act.wait_ge(*temp_vector.at(u, "sums", n - 3))
                            if by_dve(n):
                                op = act.activation(Eb[:, n % 3, :], Eb[:, n % 3, :], ACT.Exp, scale=ROOT)
                            for j in range(0 if by_dve(n) else J):
                                op = act.activation(Eb[:, n % 3, j * S2:(j + 1) * S2],
                                                    bank[RING[(G + n) % 3]][:, j * S2:(j + 1) * S2], ACT.Exp, scale=ROOT,
                                                    bias=nms[:, t, g * J + j:g * J + j + 1],
                                                    accum_out=Z[:, 0, t, g * J + j:g * J + j + 1])
                            op.then_inc(*block_exp.up(u, n))
                        if i == S1 + 2:
                            act.wait_ge(*maxima_turned.at(u))
                            for g in range(G):
                                act.activation(Qs[s][QK:QK + H, g, :], bank[4][QK:QK + H, :], ACT.Copy).then_inc(*maxima_ready.up(u, g))
                        if i == S1 + 6:
                            act.wait_ge(*temp_psum.at(u, 0))
                            act.activation(hid[:, 0, :], bank[0][0:64, 0:H], ACT.Gelu, bias=t_b1[:, 0:1]).then_inc(*temp_scalar.up(u, 0))
                        if i == S1 + 8:
                            act.wait_ge(*temp_psum.at(u, 1))
                            act.activation(hid[:, 1, :], bank[1][0:64, 0:H], ACT.Gelu, bias=t_b2[:, 0:1]).then_inc(*temp_scalar.up(u, 1))
                        if i == S1 + 11:
                            act.wait_ge(*temp_vector.at(u, "clip"))
                            act.activation(invt[:, 1, :], invt[:, 0, :], ACT.Exp, scale=-1.0).then_inc(*temp_scalar.up(u, 2))
                    elif i == 4:
                        normalized()
                        if k == "A3":
                            act.wait_ge(*q_psum.at(u, 1))
                            act.activation(x2r[s][:], bank[1][:, 0:S2], ACT.Relu).then_inc(*x2_relu.up(u))
                    elif k == "A3":
                        if i == 6:
                            act.wait_ge(*q_psum.at(u, 0))
                            act.activation(x1r[s][0], bank[0][:], ACT.Relu).then_inc(*q_high.up(u, 0))
                        if i == 11:
                            act.wait_ge(*maxima_turned.at(u))
                            act.activation(nmT3[s], bank[4][0:1, :], ACT.Copy).then_inc(*maxima_ready.up(u))
                    elif k in router:
                        E = router[k][2]
                        if i == 5 and k in chunks:
                            act.wait_ge(*xf_ready.at(u))
                            act.activation(xf_hi[s], xf[s][:], ACT.Copy).then_inc(*xf_high.up(u))
                        if i == 7:
                            act.wait_ge(*logits_less_max.at(u))
                            act.activation(gw[s][:, :, 0:E], gw[s][:, :, 0:E], ACT.Exp).then_inc(*gates_exp.up(u))
                        if i == 10:
                            act.wait_ge(*gates_turned.at(u))
                            act.activation(gT[s][0:2 * E, :], bank[4][0:2 * E, :], ACT.Copy).then_inc(*gates_ready.up(u))
                    yield

            def body(u):
                s, k = u % STREAMS, kind(u)
                l = int(k[1])
                if k in MHA:
                    for h in range(H):
                        act.wait_ge(*scores_psum.at(u, h))
                        if h >= NPT:
                            act.wait_ge(*out_psum.at(u, (h - NPT) // J))
                        if l == 1:
                            act.wait_ge(*temp_vector.at(u, "invt"))
                        act.activation(PT[h % NPT][0:S2, :], bank[(2, 3, 5)[h % 3]][0:S2, :], ACT.Exp,
                                       scale=invt[:, 2, h:h + 1] if l == 1 else ROOT,
                                       bias=mk[s][:, 2:3] if l == 2 else 0.0).then_inc(*probs_ready.up(u, h))
                        if h % J == 0 and h:
                            copy_out(u, h // J - 1)
                        yield
                    yield
                    return
                if k == "A3":
                    act.wait_ge(*scores_psum.at(u, 0))
                    act.activation(PT[0][0:S2, :], bank[2][0:S2, :], ACT.Exp, bias=mk[s][:, 3:4]).then_inc(*probs_ready.up(u, 0))
                    yield
                    yield
                    yield
                    return
                if k == "F0":
                    for c in range(C0):
                        act.wait_ge(*chunk_psum.at(u, c))
                        if c >= 3:
                            act.wait_ge(*ffn_psum.at(u, c - 3))
                        act.activation(hb[c % 3], bank[(2, 3, 6)[c % 3]][:], ACT.Relu, scale=f0_cols[:, 0, c:c + 1],
                                       bias=f0_cols[:, 1, c:c + 1]).then_inc(*chunk_act.up(u, c))
                        yield
                    yield
                if k in chunks:
                    def share(e):
                        act.wait_ge(*share_psum.at(u, e))
                        if e >= 2:
                            act.wait_ge(*share_used.at(u, e - 2))
                        act.activation(shares[e % 2], bank[7][:], ACT.Copy).then_inc(*share_ready.up(u, e))

                    share(0)
                    for n, (e, i, o, m) in enumerate(chunks[k]):
                        if i == 1 and e + 1 < router[k][2]:
                            share(e + 1)
                        act.wait_ge(*chunk_psum.at(u, n, "up"))
                        if n >= 3:
                            act.wait_ge(*ffn_psum.at(u, n - 3))
                        act.activation(hb[n % 3][0:m, :], bank[(2, 3, 6)[2 * n % 3]][0:m, :], ACT.Silu).then_inc(*chunk_act.up(u, n))
                        yield
                    yield
                if k == "F3":
                    for _ in range(MOE3 + 1):
                        yield

            def tail(u):
                k = kind(u)
                for i in range(steps_tail(k)):
                    if k in MHA and i == 0:
                        copy_out(u, G - 1)
                    if k in MHA and i == 4:
                        act.wait_ge(*att_turned.at(u))
                        act.activation(attT, bank[6][:], ACT.Copy).then_inc(*attT_ready.up(u))
                    if k[0] == "F" and i == 0:
                        act.wait_ge(*ffn_psum.at(u, "end"))
                        act.activation(oT, bank[5][:], ACT.Identity, bias=f0_bias[:, 0:1] if k == "F0" else 0.0) \
                            .then_inc(*oT_ready.up(u))
                    yield

            run(pre, body, tail)

        @block.vector
        def _(dve):
            def divide(u, g):
                dve.wait_ge(*out_turned.at(u, g))
                if g == 0 and u >= 1 and kind(u - 1) in MHA:
                    dve.wait_ge(*att_turned.at(u - 1))
                turned = bank[6 + g % 2][:].rearrange("p (t j c) -> p t j c", t=T, j=J)
                dve.reciprocal(rden[:, g], turned[:, :, :, HD]).then_inc(*out_divided.up(u, g, "inv"))
                dve.wait_ge(*out_divided.at(u, g, "inv"))
                dve.tensor_tensor(att[:, :, 32 * g:32 * g + 32].rearrange("p t (j d) -> p t j d", d=HD),
                                  turned[:, :, :, 0:HD], rden[:, g].unsqueeze(3).to_broadcast([P, T, J, HD]),
                                  ALU.mult).then_inc(*out_divided.up(u, g))

            def pre(u):
                s, k = u % STREAMS, kind(u)
                l = int(k[1])

                def statistics():
                    if u < STREAMS:
                        dve.wait_ge(*in_x[s].at("all"))
                    else:
                        dve.wait_ge(*x_done.at(u - STREAMS))
                    for t in range(T):
                        dve.bn_stats(stats[s][:, t, :], x[s][:, t, :]).then_inc(*row_stats.up(u, t))
                    for t in range(T):
                        dve.wait_ge(*row_stats.at(u, t))
                        op = dve.bn_aggr(mv[s][:, t, :], stats[s][:, t, :])
                    op.then_inc(*mean_var.up(u))

                def masks():
                    dve.wait_ge(*in_mask[s].at(1, 1))
                    dve.tensor_copy(mk[s][:, 0:1], mk_i[s][:, 0:1])
                    dve.tensor_copy(mk[s][:, 3:4], mk_i[s][:, 1:2])
                    dve.tensor_copy(mr_f[s][:], mr_i[s][:]).then_inc(*masks_ready.up("raw", s))
                    dve.wait_ge(*masks_ready.at("raw", s))
                    dve.tensor_scalar(mk[s][:, 1:2], mk[s][:, 0:1], 0.0, None, ALU.not_equal)
                    dve.tensor_scalar(mk[s][:, 3:4], mk[s][:, 3:4], -1.0, 1.0e4, ALU.add, ALU.mult)
                    dve.tensor_scalar(mr_f[s][:, 0, :], mr_f[s][:, 0, :], 0.0, None, ALU.not_equal).then_inc(*masks_ready.up("kept", s))
                    dve.wait_ge(*masks_ready.at("kept", s))
                    dve.tensor_scalar(mk[s][:, 2:3], mk[s][:, 1:2], -1.0, OFF, ALU.add, ALU.mult)
                    dve.tensor_scalar(mr[s][:, 0, 0:S2], mr_f[s][:, 0, :], -1.0, OFF, ALU.add, ALU.mult)
                    dve.memset(mr[s][:, :, S2:S2E], 0.0)
                    dve.memset(x2p[s][:, :, S2:S2E].bitcast(F32), 0.0)
                    dve.tensor_scalar(mr[s][:, 1, 0:S2], mr_f[s][:, 1, :], -1.0, 1.0e4, ALU.add, ALU.mult) \
                        .then_inc(*masks_ready.up("all", s))

                def normalize():
                    dve.wait_ge(*rstd_ready.at(u))
                    if u >= 1:
                        dve.wait_ge(*x_turned.at(u - 1, T - 1))
                    for t in range(T):
                        dve.tensor_scalar(xn[:, t, :], x[s][:, t, :], mv[s][:, t, 0:1], rstd[s][:, 1, t:t + 1],
                                          ALU.subtract, ALU.mult).then_inc(*x_normal.up(u, t))
                    if k == "F2":
                        for t in range(T):
                            dve.wait_ge(*x_normal.at(u, t))
                            dve.scalar_tensor_tensor(out=x[s][:, t, :], in0=xn[:, t, :], scalar=gates_col[:, 1, 2:3],
                                                     in1=x[s][:, t, :], op0=ALU.mult, op1=ALU.add).then_inc(*x_normal.up(u, t, "x"))
                        dve.wait_ge(*rstd_ready.at(u, "rms"))
                        for t in range(T):
                            dve.wait_ge(*x_normal.at(u, t, "x"))
                            dve.tensor_scalar(xn[:, t, :], xn[:, t, :], rstd[s][:, 3, t:t + 1], None, ALU.mult) \
                                .then_inc(*x_normal.up(u, t, "y"))

                def two_largest(E):
                    dve.wait_ge(*logits_psum.at(u))
                    if E < EMAX:
                        dve.memset(lg[s][:, :, E:EMAX], PAD)
                    dve.tensor_copy(lg[s][:, :, 0:E], bank[0][:, 0:T * E].rearrange("p (t e) -> p t e", e=E)) \
                        .then_inc(*logits_vector.up(u, "logits"))
                    dve.wait_ge(*logits_vector.at(u, "logits"))
                    for t in range(T):
                        dve.max(top[s][:, t, :], lg[s][:, t, :]).then_inc(*logits_vector.up(u, "top", t))
                    dve.wait_ge(*logits_vector.at(u, "top", T - 1))
                    dve.tensor_tensor(gw[s][:, :, 0:E], lg[s][:, :, 0:E], top[s][:, :, 0:1].to_broadcast([P, T, E]),
                                      ALU.subtract).then_inc(*logits_less_max.up(u))
                    dve.memset(top[s][:, :, 2:8], PAD).then_inc(*logits_vector.up(u, "two"))
                    dve.wait_ge(*logits_vector.at(u, "two"))
                    for t in range(T):
                        dve.match_replace(rep[s][:, t, :], in_to_replace=top[s][:, t, :], in_values=lg[s][:, t, :],
                                          imm_value=-PAD).then_inc(*logits_vector.up(u, "rep", t))
                    dve.wait_ge(*logits_vector.at(u, "rep", T - 1))
                    dve.tensor_tensor(rep[s][:, :, 0:E], rep[s][:, :, 0:E], lg[s][:, :, 0:E], ALU.not_equal) \
                        .then_inc(*logits_vector.up(u, "sel"))

                def weigh_experts(E):
                    dve.wait_ge(*gates_exp.at(u))
                    dve.wait_ge(*logits_vector.at(u, "sel"))
                    if k == "F3":
                        dve.tensor_reduce(gs[s][:, 0, :], gw[s][:, :, 0:E], AX.X, ALU.add).then_inc(*logits_vector.up(u, "sum"))
                        dve.wait_ge(*logits_vector.at(u, "sum"))
                    dve.tensor_tensor(gw[s][:, :, 0:E], gw[s][:, :, 0:E], rep[s][:, :, 0:E], ALU.mult) \
                        .then_inc(*logits_vector.up(u, "kept"))
                    dve.wait_ge(*logits_vector.at(u, "kept"))
                    if k != "F3":
                        dve.tensor_reduce(gs[s][:, 0, :], gw[s][:, :, 0:E], AX.X, ALU.add).then_inc(*logits_vector.up(u, "sum"))
                        dve.wait_ge(*logits_vector.at(u, "sum"))
                    dve.reciprocal(gs[s][:, 1, :], gs[s][:, 0, :]).then_inc(*logits_vector.up(u, "inv"))
                    dve.wait_ge(*logits_vector.at(u, "inv"))
                    dve.tensor_tensor(gw[s][:, :, 0:E], gw[s][:, :, 0:E],
                                      gs[s][:, 1, :].unsqueeze(2).to_broadcast([P, T, E]), ALU.mult) \
                        .then_inc(*logits_vector.up(u, "whole"))
                    dve.wait_ge(*logits_vector.at(u, "whole"))
                    dve.tensor_copy(gp[s][:, :, 0:E].bitcast(F32R), gw[s][:, :, 0:E]).then_inc(*logits_vector.up(u, "high"))
                    dve.wait_ge(*logits_vector.at(u, "high"))
                    dve.tensor_tensor(gp[s][:, :, E:2 * E], gw[s][:, :, 0:E], gp[s][:, :, 0:E], ALU.subtract) \
                        .then_inc(*logits_vector.up(u, "gates"))

                for i in range(steps_pre(k)):
                    if i == 0:
                        statistics()
                        if k == "A0":
                            masks()
                    if i == 2:
                        normalize()
                    if k in MHA:
                        if i == 4:
                            dve.wait_ge(*k_high.at(u, G - 1))
                            for g in range(G):
                                dve.scalar_tensor_tensor(out=Ksp[32:64, g, :], in0=bank[0][32:64, g * S2:(g + 1) * S2],
                                                         scalar=bcol[32:64, l, 1, g:g + 1], in1=Ksp[32:64, g, :],
                                                         op0=ALU.add, op1=ALU.subtract).then_inc(*k_low.up(u, g))
                        if i == 5 and l != 1:
                            dve.wait_ge(*v_psum.at(u))
                            dve.wait_ge(*masks_ready.at("all", s))
                            dve.tensor_copy(VP[s][:, :, HD:HD + 1],
                                            (mk[s][:, 1:2] if l == 2 else ones[0:S2, 0:1]).unsqueeze(2).to_broadcast([S2, H, 1]))
                        if i == 5:
                            dve.wait_ge(*k_low.at(u, G - 1))
                            ktv = KT[s][0:QK].rearrange("p (g j) k -> p g j k", j=J)
                            for j in range(J):
                                dve.tensor_scalar(ktv[:, :, j, :], Ksp[:], hmask[0:QK, j:j + 1], None, ALU.mult) \
                                    .then_inc(*keys_ready.up(u, j))
                        if Q0 + 2 <= i < Q0 + 2 + G:
                            g = i - Q0 - 2
                            dve.wait_ge(*q_high.at(u, g))
                            dve.scalar_tensor_tensor(out=Qs[s][64:QK, g, :], in0=bank[RING[g % 3]][64:QK, :],
                                                     scalar=bcol[64:QK, l, 0, g:g + 1], in1=Qs[s][64:QK, g, :].bitcast(F32),
                                                     op0=ALU.add, op1=ALU.subtract).then_inc(*q_low.up(u, g))
                        if S0 < i <= S1:
                            n = i - S0 - 1
                            t, g = n // G, n % G
                            dve.wait_ge(*block_psum.at(u, n))
                            dve.tensor_reduce(nm[s][:, t, J * g:J * g + J],
                                              bank[RING[(G + n) % 3]][:, 0:J * S2].rearrange("p (h k) -> p h k", k=S2),
                                              AX.X, ALU.max, negate=True).then_inc(*maxima.up(u, n))
                        if l == 1 and S0 + 4 <= i < S1 + 4:
                            n = i - S0 - 4
                            t, g = n // G, n % G
                            if by_dve(n):
                                dve.wait_ge(*block_exp.at(u, n))
                                dve.tensor_reduce(Z[:, 0, t, J * g:J * g + J], Eb[:, n % 3, :].rearrange("p (h k) -> p h k", k=S2),
                                                  AX.X, ALU.add)
                            dve.wait_ge(*block_squared.at(u, n))
                            dve.tensor_reduce(Z[:, 1, t, J * g:J * g + J], Eq[:, n % 3, :].rearrange("p (h k) -> p h k", k=S2),
                                              AX.X, ALU.add).then_inc(*temp_vector.up(u, "sums", n))
                        if l == 1 and S0 < i <= S1:
                            n = i - S0 - 1
                            t, g = n // G, n % G
                            dve.wait_ge(*maxima.at(u, n))
                            if not by_dve(n):
                                dve.tensor_scalar(nms[:, t, J * g:J * g + J], nm[s][:, t, J * g:J * g + J], ROOT, None, ALU.mult) \
                                    .then_inc(*block_less_max.up(u, n))
                            else:
                                if n >= 3:
                                    dve.wait_ge(*temp_vector.at(u, "sums", n - 3))
                                dve.tensor_tensor(Eb[:, n % 3, :].rearrange("p (h k) -> p h k", k=S2),
                                                  bank[RING[(G + n) % 3]][:, 0:J * S2].rearrange("p (h k) -> p h k", k=S2),
                                                  nm[s][:, t, J * g:J * g + J].unsqueeze(2).to_broadcast([P, J, S2]), ALU.add) \
                                    .then_inc(*block_less_max.up(u, n))
                        if i == S1 + 4:
                            dve.wait_ge(*temp_vector.at(u, "sums", NS - 1))
                            dve.reciprocal(nms[:], Z[:, 0]).then_inc(*temp_vector.up(u, "inv"))
                            dve.tensor_reduce(feat[:, 1, :], nm[s][:].rearrange("p t h -> p h t"), AX.X, ALU.add)
                            dve.tensor_tensor(pk[0:QK], qsum[0:QK], ksum[s][0:QK], ALU.mult).then_inc(*temp_vector.up(u, "pk"))
                            dve.wait_ge(*temp_vector.at(u, "inv"))
                            dve.tensor_tensor(zt[:], Z[:, 1], nms[:], ALU.mult).then_inc(*temp_vector.up(u, "z1"))
                            dve.wait_ge(*temp_vector.at(u, "z1"))
                            dve.tensor_tensor(zt[:], zt[:], nms[:], ALU.mult).then_inc(*temp_vector.up(u, "z2"))
                            dve.wait_ge(*temp_vector.at(u, "z2"))
                            dve.tensor_scalar(zt[:], zt[:], 1.0 / S2, None, ALU.subtract).then_inc(*temp_vector.up(u, "z3"))
                            dve.tensor_tensor(feat[:, 0, :].rearrange("p (g j) -> p g j", j=J),
                                              pk[:].unsqueeze(2).to_broadcast([P, G, J]),
                                              quad[:, 0:1, :].to_broadcast([P, G, J]), ALU.mult)
                            dve.wait_ge(*temp_vector.at(u, "z3"))
                            dve.tensor_reduce(feat[:, 2, :], zt[:].rearrange("p t h -> p h t"), AX.X, ALU.add) \
                                .then_inc(*temp_vector.up(u, "feat"))
                        if i == S1 + 10:
                            dve.wait_ge(*temp_psum.at(u, 2))
                            dve.tensor_scalar(invt[:, 0, :], bank[0][0:S2, 0:H], t_b3[:, 0:1], LOG_T_MIN, ALU.add, ALU.max) \
                                .then_inc(*temp_vector.up(u, "low"))
                            dve.wait_ge(*temp_vector.at(u, "low"))
                            dve.tensor_scalar(invt[:, 0, :], invt[:, 0, :], LOG_T_MAX, None, ALU.min).then_inc(*temp_vector.up(u, "clip"))
                        if i == S1 + 12:
                            dve.wait_ge(*temp_scalar.at(u, 2))
                            if u >= 1 and kind(u - 1) == k:
                                dve.wait_ge(*probs_ready.at(u - 1, H - 1))
                            dve.tensor_scalar(invt[:, 2, :], invt[:, 1, :], 0.5, None, ALU.mult).then_inc(*temp_vector.up(u, "invt"))
                    elif k == "A3":
                        if i == 5:
                            dve.wait_ge(*x2_relu.at(u))
                            dve.tensor_scalar(x2r[s][:], x2r[s][:], diag[:, 0:1], None, ALU.mult).then_inc(*x1_parts.up(u, "raw"))
                            dve.wait_ge(*x1_parts.at(u, "raw"))
                            dve.tensor_copy(x2p[s][:, 0, 0:S2], x2r[s][:]).then_inc(*x1_parts.up(u, "high"))
                            dve.wait_ge(*x1_parts.at(u, "high"))
                            dve.tensor_tensor(x2p[s][:, 1, 0:S2], x2r[s][:], x2p[s][:, 0, 0:S2].bitcast(F32), ALU.subtract) \
                                .then_inc(*q_low.up(u, 1))
                        if i == 7:
                            dve.wait_ge(*q_high.at(u, 0))
                            dve.scalar_tensor_tensor(out=x1r[s][1], in0=bank[0][:], scalar=0.0, in1=x1r[s][0].bitcast(F32),
                                                     op0=ALU.max, op1=ALU.subtract).then_inc(*x1_parts.up(u, "low"))
                        if i == 9:
                            dve.wait_ge(*block_psum.at(u, 0))
                            dve.tensor_reduce(nm3[s][:], bank[1][:, 0:T * S2E].rearrange("p (t k) -> p t k", k=S2E)[:, :, 0:S2], AX.X, ALU.max,
                                              negate=True).then_inc(*maxima.up(u, 0))
                    elif k in router:
                        E = router[k][2]
                        if i == 6:
                            two_largest(E)
                            if k in chunks:
                                dve.wait_ge(*xf_high.at(u))
                                dve.tensor_tensor(xf_lo[s], xf[s][:], xf_hi[s].bitcast(F32), ALU.subtract).then_inc(*xf_low.up(u))
                        if i == 8:
                            weigh_experts(E)
                    yield

            def body(u):
                s, k = u % STREAMS, kind(u)
                l = int(k[1])
                gate = gates_col[:, 0 if k[0] == "A" else 1, l:l + 1]
                if k in MHA:
                    for h in range(H):
                        if h % J == 3 and h > J:
                            divide(u, h // J - 1)
                        yield
                    yield
                    return
                if k == "A3":
                    yield
                    dve.wait_ge(*out_psum.at(u, 0))
                    for b in (6, 7):
                        op = dve.reciprocal(gs[s][:, 0, 2 * (b - 6):2 * (b - 6) + 2],
                                            bank[b][:].rearrange("p (t c) -> p t c", t=2)[:, :, P])
                    op.then_inc(*x3_inverse.up(u, "inv"))
                    dve.wait_ge(*x3_inverse.at(u, "inv"))
                    dve.tensor_scalar(gs[s][:, 1, :], gs[s][:, 0, :], gate, None, ALU.mult).then_inc(*x3_inverse.up(u, "gate"))
                    yield
                    dve.wait_ge(*x3_inverse.at(u, "gate"))
                    for t in range(T):
                        op = dve.scalar_tensor_tensor(out=x[s][:, t, :], in0=bank[6 + t // 2][:, t % 2 * 256:t % 2 * 256 + P],
                                                      scalar=gs[s][:, 1, t:t + 1], in1=x[s][:, t, :],
                                                      op0=ALU.mult, op1=ALU.add)
                    op.then_inc(*x_done.up(u))
                    yield
                    return
                if k == "F0":
                    for c in range(C0 + 1):
                        yield
                if k in chunks:
                    todo = chunks[k]
                    for n, (e, i, o, m) in enumerate(todo):
                        dve.wait_ge(*chunk_act.at(u, n))
                        dve.wait_ge(*share_ready.at(u, e))
                        h = hb[n % 3][0:m, :]
                        op = dve.tensor_tensor(h, h, shares[e % 2][0:m, :], ALU.mult)
                        op.then_inc(*(share_used.up(u, e) if n + 1 == len(todo) or todo[n + 1][0] > e else share_used.up(u, n, "part")))
                        dve.wait_ge(*(share_used.at(u, e) if n + 1 == len(todo) or todo[n + 1][0] > e else share_used.at(u, n, "part")))
                        dve.wait_ge(*chunk_psum.at(u, n))
                        dve.tensor_tensor(h, h, bank[(2, 3, 6)[(2 * n + 1) % 3]][0:m, :], ALU.mult).then_inc(*chunk_ready.up(u, n))
                        yield
                if k == "F3":
                    for e in range(MOE3):
                        dve.wait_ge(*share_psum.at(u, e))
                        if e >= 2:
                            dve.wait_ge(*ffn_psum.at(u, e - 2))
                        dve.tensor_tensor(xw[e % 2], xf[s][:], bank[(2, 7)[e % 2]][:], ALU.mult).then_inc(*share_used.up(u, e))
                        yield
                if k == "F3" or k in chunks:
                    yield

            def tail(u):
                s, k = u % STREAMS, kind(u)
                for i in range(steps_tail(k)):
                    if k in MHA and i == 2:
                        divide(u, G - 1)
                    if i == steps_tail(k) - 1:
                        l = int(k[1])
                        dve.wait_ge(*result_psum.at(u))
                        dve.scalar_tensor_tensor(out=x[s][:].rearrange("p t d -> p (t d)"), in0=bank[7][:],
                                                 scalar=gates_col[:, 0 if k[0] == "A" else 1, l:l + 1],
                                                 in1=x[s][:].rearrange("p t d -> p (t d)"), op0=ALU.mult, op1=ALU.add) \
                            .then_inc(*x_done.up(u))
                    yield

            run(pre, body, tail)

        @block.tensor
        def _(pe):
            reader = {}

            def free(b):
                if b in reader:
                    signal, *key = reader[b]
                    pe.wait_ge(*signal.at(*key))

            def turn(u, g):
                free(6 + g % 2)
                pe.wait_ge(*out_kept.at(u, g))
                for t in range(T):
                    op = pe.transpose(bank[6 + g % 2][:, t * P:(t + 1) * P], Os[:, g % 2, t * P:(t + 1) * P], ident[:])
                op.then_inc(*out_turned.up(u, g))
                reader[6 + g % 2] = (out_divided, u, g)

            def pre(u):
                s, k = u % STREAMS, kind(u)
                l = int(k[1])

                def transpose_x():
                    free(4)
                    for t in range(T):
                        pe.wait_ge(*(x_normal.at(u, t, "y") if k == "F2" else x_normal.at(u, t)))
                        pe.transpose(bank[4][:, t * P:(t + 1) * P], xn[:, t, :], ident[:]).then_inc(*x_turned.up(u, t))
                    reader[4] = (xf_ready, u)

                for i in range(steps_pre(k)):
                    if k in MHA:
                        if i == 0 and k == "A0":
                            pe.wait_ge(*in_ctx[s].at("all"))
                            free(1)
                            pe.transpose(bank[1][:, 0:S2], ctxn[s][:, 0:P], ident[0:S2, 0:S2]).then_inc(*ctx_turned.up(s))
                            reader[1] = (ctx_ready, s)
                        if i == 2:
                            free(0)
                            pe.wait_ge(*ctx_ready.at(s))
                            for g in range(G):
                                op = pe.matmul(bank[0][0:QK, g * S2:(g + 1) * S2], WkR[l][:, g, :], ctxT[s][:], start=True, stop=True)
                            op.then_inc(*k_psum.up(u))
                            reader[0] = (k_low, u, G - 1)
                            free(1)
                            pe.matmul(bank[1][0:S2, 0:P], ctxT[s][:], Wv[l][:], start=True, stop=False)
                            pe.matmul(bank[1][0:S2, 0:P], ones[0:1, 0:S2], bv[0:1, l, :], start=False, stop=True) \
                                .then_inc(*v_psum.up(u))
                            reader[1] = (values_ready, u)
                        if i == 3:
                            transpose_x()
                        if Q0 <= i < S0:
                            g = i - Q0
                            b = RING[g % 3]
                            pe.wait_ge(*xf_ready.at(u))
                            free(b)
                            pe.matmul(bank[b][0:QK, :], WqR[l][:, g, :], xf[s][:], start=True, stop=True).then_inc(*q_psum.up(u, g))
                            reader[b] = (q_low, u, g)
                        if S0 <= i < S1:
                            n = i - S0
                            t, g = n // G, n % G
                            b = RING[(G + n) % 3]
                            free(b)
                            if n == 0:
                                pe.wait_ge(*keys_ready.at(u, J - 1))
                            if n < G:
                                pe.wait_ge(*q_low.at(u, g))
                            dst = bank[b][:, 0:J * S2]
                            op = pe.matmul(dst, Qs[s][0:QK, g, t * P:(t + 1) * P],
                                           KT[s][0:QK, J * g:J * g + J, :].rearrange("p h k -> p (h k)"),
                                           start=True, stop=l == 1)
                            if l == 0:
                                op = pe.matmul(dst, identb[:], mask_q[:, t:t + 1, :].to_broadcast([P, J, S2]),
                                               start=False, stop=True)
                            if l == 2:
                                pe.wait_ge(*masks_ready.at("all", s))
                                op = pe.matmul(dst, onesb[:], mr[s][0:1, 0:1, 0:S2].to_broadcast([1, J, S2]),
                                               start=False, stop=True)
                            op.then_inc(*block_psum.up(u, n))
                            reader[b] = (maxima, u, n) if l != 1 else (block_less_max, u, n) if by_dve(n) else (block_exp, u, n)
                        if i == S1 + 1:
                            pe.wait_ge(*maxima.at(u, NS - 1))
                            free(4)
                            for t in range(T):
                                op = pe.matmul(bank[4][QK:QK + H, t * P:(t + 1) * P], nm[s][:, t, :], ident[:],
                                               start=True, stop=True, tile_position=(0, QK))
                            op.then_inc(*maxima_turned.up(u))
                            reader[4] = (maxima_ready, u, G - 1)
                        if i == S1 + 5:
                            free(0)
                            pe.wait_ge(*temp_vector.at(u, "feat"))
                            for f in range(3):
                                op = pe.matmul(bank[0][0:64, 0:H], t_w1b[:, f, :], feat[:, f, :], start=f == 0, stop=f == 2)
                            op.then_inc(*temp_psum.up(u, 0))
                        if i == S1 + 7:
                            free(1)
                            pe.wait_ge(*temp_scalar.at(u, 0))
                            pe.matmul(bank[1][0:64, 0:H], t_w2T[:], hid[:, 0, :], start=True, stop=True).then_inc(*temp_psum.up(u, 1))
                        if i == S1 + 9:
                            pe.wait_ge(*temp_scalar.at(u, 1))
                            pe.matmul(bank[0][0:S2, 0:H], t_w3[:, 0:1].to_broadcast([64, S2]), hid[:, 1, :],
                                      start=True, stop=True).then_inc(*temp_psum.up(u, 2))
                            reader[0] = (temp_vector, u, "low")
                            reader[1] = (temp_scalar, u, 1)
                    elif i == 3:
                        transpose_x()
                        if k == "A3":
                            free(1)
                            pe.matmul(bank[1][:, 0:S2], W3x[:], ctxT[s][:], start=True, stop=True).then_inc(*q_psum.up(u, 1))
                            reader[1] = (x2_relu, u)
                    elif k == "A3":
                        if i == 5:
                            free(0)
                            pe.wait_ge(*xf_ready.at(u))
                            pe.matmul(bank[0][:], W3x[:], xf[s][:], start=True, stop=True).then_inc(*q_psum.up(u, 0))
                            reader[0] = (x1_parts, u, "low")
                        if i == 8:
                            free(1)
                            pe.wait_ge(*q_low.at(u, 1))
                            pe.wait_ge(*x1_parts.at(u, "low"))
                            pe.matmul(bank[1][:, 0:T * S2E], onesb[:], mr[s][0:1, 1:2, :].to_broadcast([1, T, S2E]),
                                      start=True, stop=False)
                            for t in range(T):
                                for p1, p2 in ((1, 0), (0, 1), (0, 0)):
                                    op = pe.matmul(bank[1][:, t * S2E:(t + 1) * S2E], x1r[s][p1][:, t * P:(t + 1) * P], x2p[s][:, p2, :],
                                                   start=False, stop=t == T - 1 and p1 + p2 == 0)
                            op.then_inc(*block_psum.up(u, 0))
                            reader[1] = (maxima, u, 0)
                        if i == 10:
                            free(4)
                            pe.wait_ge(*maxima.at(u, 0))
                            for t in range(T):
                                op = pe.transpose(bank[4][0:1, t * P:(t + 1) * P], nm3[s][:, t:t + 1], ident[:])
                            op.then_inc(*maxima_turned.up(u))
                            reader[4] = (maxima_ready, u)
                    elif k in router:
                        w, b, E = router[k]
                        if i == 5:
                            free(0)
                            pe.wait_ge(*xf_ready.at(u))
                            if b is not None:
                                pe.matmul(bank[0][:, 0:T * E], ones[0:1, 0:P], b[0:1, None, :].to_broadcast([1, T, E]),
                                          start=True, stop=False)
                            for t in range(T):
                                op = pe.matmul(bank[0][:, t * E:(t + 1) * E], xf[s][:, t * P:(t + 1) * P], w[:],
                                               start=b is None, stop=b is None or t == T - 1)
                            op.then_inc(*logits_psum.up(u))
                            reader[0] = (logits_vector, u, "logits")
                        if i == 9:
                            free(4)
                            pe.wait_ge(*logits_vector.at(u, "gates"))
                            for t in range(T):
                                op = pe.transpose(bank[4][0:2 * E, t * P:(t + 1) * P], gp[s][:, t, 0:2 * E], ident[:])
                            op.then_inc(*gates_turned.up(u))
                            reader[4] = (gates_ready, u)
                    yield

            def body(u):
                s, k = u % STREAMS, kind(u)
                l = int(k[1])
                if k in MHA:

                    def weigh(g):
                        free(6 + g % 2)
                        for j in range(J):
                            h = g * J + j
                            pe.wait_ge(*probs_ready.at(u, h))
                            op = pe.matmul(bank[6 + g % 2][32 * j:32 * j + 32, :], VP[s][:, h, :], PT[h % NPT][0:S2, :],
                                           start=True, stop=True, tile_position=(0, 32 * j))
                        op.then_inc(*out_psum.up(u, g))
                        reader[6 + g % 2] = (out_kept, u, g)

                    def scores(h):
                        b = (2, 3, 5)[h % 3]
                        free(b)
                        dst = bank[b][0:S2, :]
                        if l == 0:
                            pe.matmul(dst, identb[0:S2, 0:S2], mask_k[:], start=True, stop=False)
                        pe.wait_ge(*maxima_ready.at(u, h // J))
                        pe.matmul(dst, KT[s][:, h, :], Qs[s][0:QK + H, h // J, :], start=l != 0, stop=True).then_inc(*scores_psum.up(u, h))
                        reader[b] = (probs_ready, u, h)

                    scores(0)
                    for h in range(H):
                        if h + 1 < H:
                            scores(h + 1)
                        if h % J == 0 and h:
                            weigh(h // J - 1)
                        if h % J == 2 and h > J:
                            turn(u, h // J - 1)
                        yield
                    weigh(G - 1)
                    yield
                    return
                if k == "A3":
                    free(2)
                    pe.wait_ge(*maxima_ready.at(u))
                    for p2, p1 in ((1, 0), (0, 1), (0, 0)):
                        pe.matmul(bank[2][0:S2, :], x2p[s][:, p2, 0:S2], x1r[s][p1], start=(p2, p1) == (1, 0), stop=False)
                    pe.matmul(bank[2][0:S2, :], ones_r[0:1, 0:S2], nmT3[s], start=False, stop=True).then_inc(*scores_psum.up(u, 0))
                    reader[2] = (probs_ready, u, 0)
                    yield
                    free(6)
                    free(7)
                    pe.wait_ge(*probs_ready.at(u, 0))
                    for t in range(T):
                        op = pe.matmul(bank[6 + t // 2][:, t % 2 * 256:t % 2 * 256 + P + 1], PT[0][0:S2, t * P:(t + 1) * P],
                                       ctxn[s][:], start=True, stop=True)
                    op.then_inc(*out_psum.up(u, 0))
                    reader[6] = reader[7] = (x_done, u)
                    yield
                    yield
                    return
                if k == "F0":
                    def down(c):
                        if c == 0:
                            free(5)
                        pe.wait_ge(*chunk_act.at(u, c))
                        pe.matmul(bank[5][:], f0_out[:, c, :], hb[c % 3], start=c == 0, stop=c == C0 - 1) \
                            .then_inc(*ffn_psum.up(u, c))
                    pe.wait_ge(*xf_ready.at(u))
                    for c in range(C0):
                        free((2, 3, 6)[c % 3])
                        pe.matmul(bank[(2, 3, 6)[c % 3]][:], f0_in[:, c * P:(c + 1) * P], xf[s][:], start=True, stop=True) \
                            .then_inc(*chunk_psum.up(u, c))
                        reader[(2, 3, 6)[c % 3]] = (chunk_act, u, c)
                        if c >= 1:
                            down(c - 1)
                        yield
                    down(C0 - 1)
                    ffn_psum.counts[(u, "end")] = ffn_psum.counts[(u, C0 - 1)]
                    reader[5] = (oT_ready, u)
                    yield
                if k in chunks:
                    todo = chunks[k]
                    E = router[k][2]
                    pe.wait_ge(*gates_ready.at(u))

                    def exact(dst, w_hi, w_lo, x_hi, x_lo):
                        pe.matmul(dst, w_lo, x_hi, start=True, stop=False)
                        pe.matmul(dst, w_hi, x_hi, start=False, stop=False)
                        return pe.matmul(dst, w_hi, x_lo, start=False, stop=True)

                    def broadcast(e):
                        free(7)
                        pe.matmul(bank[7][:], pick[k][:, e:e + 1].to_broadcast([2 * E, P]), gT[s][0:2 * E, :], start=True, stop=True) \
                            .then_inc(*share_psum.up(u, e))
                        reader[7] = (share_ready, u, e)

                    def down(n):
                        e, i, o, m = todo[n]
                        if n == 0:
                            free(5)
                        pe.wait_ge(*chunk_ready.at(u, n))
                        wd = m1_w2[0:m, e, i, :] if k == "F1" else m2_w3[0:m, e, i, :]
                        pe.matmul(bank[5][:], wd, hb[n % 3][0:m, :], start=n == 0, stop=n == len(todo) - 1) \
                            .then_inc(*ffn_psum.up(u, n))

                    broadcast(0)
                    for n, (e, i, o, m) in enumerate(todo):
                        if k == "F1":
                            (wu, wul), (wg, wgl) = ([w[:, e, o:o + m] for w in pair] for pair in (m1_w1, m1_w3))
                        else:
                            (wu, wul), (wg, wgl) = ([w[:, e * F2 + o:e * F2 + o + m] for w in pair] for pair in (m2_w1, m2_w2))
                        bu, bg = (2, 3, 6)[2 * n % 3], (2, 3, 6)[(2 * n + 1) % 3]
                        free(bu)
                        if n == 0:
                            pe.wait_ge(*xf_low.at(u))
                        exact(bank[bu][0:m, :], wu, wul, xf_hi[s], xf_lo[s]).then_inc(*chunk_psum.up(u, n, "up"))
                        reader[bu] = (chunk_act, u, n)
                        free(bg)
                        exact(bank[bg][0:m, :], wg, wgl, xf_hi[s], xf_lo[s]).then_inc(*chunk_psum.up(u, n))
                        reader[bg] = (chunk_ready, u, n)
                        if i == 0 and e + 1 < E:
                            broadcast(e + 1)
                        if n >= 1:
                            down(n - 1)
                        yield
                    down(len(todo) - 1)
                    ffn_psum.counts[(u, "end")] = ffn_psum.counts[(u, len(todo) - 1)]
                    reader[5] = (oT_ready, u)
                    yield
                if k == "F3":
                    pe.wait_ge(*gates_ready.at(u))
                    free(5)
                    pe.matmul(bank[5][:], m3_b[:], gT[s].bitcast(F32), start=True, stop=False)
                    for e in range(MOE3):
                        b = (2, 7)[e % 2]
                        free(b)
                        pe.matmul(bank[b][:], pick[k][:, e:e + 1].to_broadcast([2 * MOE3, P]), gT[s], start=True, stop=True) \
                            .then_inc(*share_psum.up(u, e))
                        reader[b] = (share_used, u, e)
                        if e:
                            pe.wait_ge(*share_used.at(u, e - 1))
                            pe.matmul(bank[5][:], m3_w[:, e - 1, :], xw[(e - 1) % 2], start=False, stop=False) \
                                .then_inc(*ffn_psum.up(u, e - 1))
                        yield
                    pe.wait_ge(*share_used.at(u, MOE3 - 1))
                    pe.matmul(bank[5][:], m3_w[:, MOE3 - 1, :], xw[(MOE3 - 1) % 2], start=False, stop=True) \
                        .then_inc(*ffn_psum.up(u, MOE3 - 1))
                    ffn_psum.counts[(u, "end")] = ffn_psum.counts[(u, MOE3 - 1)]
                    reader[5] = (oT_ready, u)
                    yield

            def tail(u):
                k = kind(u)
                l = int(k[1])
                for i in range(steps_tail(k)):
                    if k[0] == "F" and i == 1:
                        free(7)
                        pe.wait_ge(*oT_ready.at(u))
                        for t in range(T):
                            op = pe.transpose(bank[7][:, t * P:(t + 1) * P], oT[:, t * P:(t + 1) * P], ident[:])
                        op.then_inc(*result_psum.up(u))
                        reader[7] = (x_done, u)
                    if k in MHA and i == 1:
                        turn(u, G - 1)
                    if k in MHA and i == 3:
                        free(6)
                        pe.wait_ge(*out_divided.at(u, G - 1))
                        for t in range(T):
                            op = pe.transpose(bank[6][:, t * P:(t + 1) * P], att[:, t, :], ident[:])
                        op.then_inc(*att_turned.up(u))
                        reader[6] = (attT_ready, u)
                    if k in MHA and i == 5:
                        free(7)
                        pe.wait_ge(*attT_ready.at(u))
                        pe.matmul(bank[7][:], ones_r[:], bo[:, l:l + 1, :].to_broadcast([2, T, P]), start=True, stop=False)
                        for t in range(T):
                            op = pe.matmul(bank[7][:, t * P:(t + 1) * P], attT[:, t * P:(t + 1) * P], Wo[l][:],
                                           start=False, stop=t == T - 1)
                        op.then_inc(*result_psum.up(u))
                        reader[7] = (x_done, u)
                    yield

            run(pre, body, tail)

    nc.all_engine_barrier(sems_to_clear=to_clear)


_INS = """x ctx_1024 mask_SxS2_bk0 mask_BxS2_ik0 mask_BxS2_if1 g_xattn g_ffn
L0_xattn_Wq L0_xattn_bq L0_xattn_Wk L0_xattn_bk L0_xattn_Wv L0_xattn_bv L0_xattn_Wo L0_xattn_bo
L0_ffn_Win L0_ffn_bin_ L0_ffn_W1 L0_ffn_b1 L0_ffn_W2 L0_ffn_b2 L0_ffn_Wout L0_ffn_bout
L1_xattn_Wq L1_xattn_bq L1_xattn_Wk L1_xattn_bk L1_xattn_Wv L1_xattn_bv L1_xattn_Wo L1_xattn_bo
L1_xattn_w1 L1_xattn_b1 L1_xattn_w2 L1_xattn_b2 L1_xattn_w3 L1_xattn_b3
L1_ffn_router_w L1_ffn_router_b L1_ffn_w1 L1_ffn_w3 L1_ffn_w2
L2_xattn_Wq L2_xattn_bq L2_xattn_Wk L2_xattn_bk L2_xattn_Wv L2_xattn_bv L2_xattn_Wo L2_xattn_bo
L2_ffn_gate_w L2_ffn_rms_w L2_ffn_W1 L2_ffn_W2 L2_ffn_W3
L3_xattn_W L3_xattn_diagonal L3_ffn_W_experts L3_ffn_b_experts L3_ffn_W_router L3_ffn_b_router""".split()


def kernel(**inputs):
    import numpy as _np
    import concourse.bacc as _bacc
    from concourse import mybir as _mybir
    from concourse.bass_utils import run_bass_kernel_spmd as _run

    def program(seen, counts):
        nc = _bacc.Bacc("TRN2", target_bir_lowering=False, num_devices=1)
        arrays, args = {}, {}
        for name in _INS:
            arr = _np.ascontiguousarray(inputs[name])
            arrays[f"in_{name}_dram"] = arr
            args[name] = nc.dram_tensor(f"in_{name}_dram", arr.shape, _mybir.dt.from_np(arr.dtype),
                                        kind="ExternalInput").ap()
        out = nc.dram_tensor("out_0_dram", (B, N, P), _mybir.dt.float32, kind="ExternalOutput").ap()
        build(nc, args, out, seen, counts)
        return nc, arrays

    counts = {}
    program({}, counts)
    nc, arrays = program(counts, {})
    r = _run(nc, [arrays], core_ids=[0])
    return r.results[0]["out_0_dram"]
```
